# Optimizing a Trainium2 kernel written in Bass

```python
import numpy as np
import jax
import jax.numpy as jnp

def _softmax(x, axis=-1):
    return jax.nn.softmax(x, axis=axis)

def _gelu(x):
    return jax.nn.gelu(x, approximate=True)

def _silu(x):
    return jax.nn.silu(x)

def _sigmoid(x):
    return jax.nn.sigmoid(x)

def _layernorm(x, axis=-1, eps=1e-05):
    m = jnp.mean(x, axis=axis, keepdims=True)
    v = jnp.var(x, axis=axis, keepdims=True)
    return (x - m) / jnp.sqrt(v + eps)

def _scatter_add(tgt, idx, src, axis=0):
    return tgt.at[idx].add(src)

def _segment_sum(src, seg, n):
    return jax.ops.segment_sum(src, seg, n)
kernel_name = 'mk_gnn_preln_d4_gnn_r16_d080dc'

def setup_inputs(seed: int=0):
    np.random.seed(seed)
    _w = jnp.asarray

    def _rec_inputs():
        import jax
        import jax.numpy as jnp
        _gk = jax.random.key(seed)
        x = -0.000202 + 1 * jax.random.normal(jax.random.fold_in(_gk, 1), (3125, 128), jnp.float32)
        src = jax.random.randint(jax.random.fold_in(_gk, 2), (100000,), 0, 3125, jnp.int32)
        dst = jax.random.randint(jax.random.fold_in(_gk, 3), (100000,), 0, 3125, jnp.int32)
        _o = jnp.argsort(dst, stable=True)
        src = src[_o]
        dst = dst[_o]
        edge_attr_64 = 0.000149146 + 1.0001 * jax.random.normal(jax.random.fold_in(_gk, 12), (100000, 64), jnp.float32)
        edge_weight = jax.random.uniform(jax.random.fold_in(_gk, 14), (100000,), jnp.float32, 0.0, 999.998)
        node_vec = jax.random.uniform(jax.random.fold_in(_gk, 15), (3125,), jnp.float32, 0.0, 999.994)
        return (x, src, dst, edge_attr_64, edge_weight, node_vec)
    x, src, dst, edge_attr_64, edge_weight, node_vec = _rec_inputs()

    def _L0_gnn_setup():
        import jax, jax.numpy as jnp
        import numpy as np
        N, E, D, H = (3125, 50000, 128, 8)
        DH = D // H
        DFF = 512

        def _gat(x, W_fc, a_l, a_r, edge_src, edge_dst):
            z = jnp.einsum('nd,hdk->nhk', x, W_fc)
            el = jnp.einsum('nhk,hk->nh', z, a_l)
            er = jnp.einsum('nhk,hk->nh', z, a_r)
            e = jax.nn.leaky_relu(el[edge_src] + er[edge_dst], 0.01)
            m = jax.ops.segment_max(e, edge_dst, num_segments=N)
            m = jnp.where(jnp.isfinite(m), m, 0.0)
            ee = jnp.exp(e - m[edge_dst])
            s = jax.ops.segment_sum(ee, edge_dst, num_segments=N)
            alpha = ee / jnp.maximum(s[edge_dst], 1e-09)
            msg = alpha[:, :, None] * z[edge_src]
            h = jax.ops.segment_sum(msg, edge_dst, num_segments=N)
            return h.reshape(N, H * DH)
        key = jax.random.key(seed)
        ks = jax.random.split(key, 8)
        return {'x': jax.random.normal(ks[0], (N, D), jnp.float32), 'W_fc': jax.random.normal(ks[1], (H, D, DH), jnp.float32) * 0.05, 'a_l': jax.random.normal(ks[2], (H, DH), jnp.float32) * 0.1, 'a_r': jax.random.normal(ks[3], (H, DH), jnp.float32) * 0.1, 'ln_gamma': jnp.ones((D,), jnp.float32), 'ln_beta': jnp.zeros((D,), jnp.float32), 'W1': jax.random.normal(ks[4], (D, DFF), jnp.float32) * 0.05, 'b1': jnp.zeros((DFF,), jnp.float32), 'W2': jax.random.normal(ks[5], (DFF, D), jnp.float32) * 0.05, 'b2': jnp.zeros((D,), jnp.float32), 'edge_src': jax.random.randint(ks[6], (E,), 0, N, jnp.int32), 'edge_dst': jax.random.randint(ks[7], (E,), 0, N, jnp.int32)}
    _L0_gnn_all = _L0_gnn_setup()
    _L0_gnn_in = {k: v for k, v in _L0_gnn_all.items() if k in ('W_fc', 'a_l', 'a_r', 'ln_gamma', 'ln_beta', 'W1', 'b1', 'W2', 'b2')}
    del _L0_gnn_all

    def _L1_gnn_setup():
        import jax, jax.numpy as jnp
        import numpy as np
        N = 6250
        E = 40000
        IN_CH = 128
        OUT_CH = 128
        MSG_DIM = 64
        TIME_DIM = 64
        EDGE_DIM = MSG_DIM + TIME_DIM
        HEADS = 4

        def _linear_params(key, fan_in, fan_out, bias=True, scale=0.02):
            k1, k2 = jax.random.split(key)
            W = jax.random.normal(k1, (fan_in, fan_out), jnp.float32) * scale
            if bias:
                b = jax.random.normal(k2, (fan_out,), jnp.float32) * scale
                return (W, b)
            return W

        def transformer_conv(x, src, dst, edge_attr, Wq, bq, Wk, bk, Wv, bv, We, Wskip, bskip):
            n = x.shape[0]
            HC = Wq.shape[1]
            C = HC // HEADS
            q = (x @ Wq + bq).reshape(n, HEADS, C)
            k = (x @ Wk + bk).reshape(n, HEADS, C)
            v = (x @ Wv + bv).reshape(n, HEADS, C)
            e = (edge_attr @ We).reshape(-1, HEADS, C)
            k_j = k[src] + e
            v_j = v[src] + e
            alpha = jnp.einsum('ehc,ehc->eh', q[dst], k_j) / jnp.sqrt(jnp.float32(C))
            amax = jax.ops.segment_max(alpha, dst, num_segments=n)
            expa = jnp.exp(alpha - amax[dst])
            denom = jax.ops.segment_sum(expa, dst, num_segments=n)
            attn = expa / (denom[dst] + 1e-16)
            out = jax.ops.segment_sum(attn[:, :, None] * v_j, dst, num_segments=n)
            out = out.reshape(n, HC)
            return out + x @ Wskip + bskip
        key = jax.random.key(seed)
        ks = jax.random.split(key, 16)
        inp = {'x': jax.random.normal(ks[0], (N, IN_CH), jnp.float32), 'last_update': jax.random.uniform(ks[1], (N,), jnp.float32) * 1000.0, 't': jax.random.uniform(ks[2], (E,), jnp.float32) * 1000.0, 'msg': jax.random.normal(ks[3], (E, MSG_DIM), jnp.float32), 'edge_index': jax.random.randint(ks[4], (2, E), 0, N, jnp.int64)}
        inp['Wt'], inp['bt'] = _linear_params(ks[5], 1, TIME_DIM)
        HC1 = HEADS * (IN_CH // 4)
        inp['Wq1'], inp['bq1'] = _linear_params(ks[6], IN_CH, HC1)
        inp['Wk1'], inp['bk1'] = _linear_params(ks[7], IN_CH, HC1)
        inp['Wv1'], inp['bv1'] = _linear_params(ks[8], IN_CH, HC1)
        inp['We1'] = _linear_params(ks[9], EDGE_DIM, HC1, bias=False)
        inp['Wskip1'], inp['bskip1'] = _linear_params(ks[10], IN_CH, HC1)
        HC2 = HEADS * (OUT_CH // 4)
        inp['Wq2'], inp['bq2'] = _linear_params(ks[11], IN_CH, HC2)
        inp['Wk2'], inp['bk2'] = _linear_params(ks[12], IN_CH, HC2)
        inp['Wv2'], inp['bv2'] = _linear_params(ks[13], IN_CH, HC2)
        inp['We2'] = _linear_params(ks[14], EDGE_DIM, HC2, bias=False)
        inp['Wskip2'], inp['bskip2'] = _linear_params(ks[15], IN_CH, HC2)
        return inp
    _L1_gnn_all = _L1_gnn_setup()
    _L1_gnn_in = {k: v for k, v in _L1_gnn_all.items() if k in ('Wt', 'bt', 'Wq1', 'bq1', 'Wk1', 'bk1', 'Wv1', 'bv1', 'We1', 'Wskip1', 'bskip1', 'Wq2', 'bq2', 'Wk2', 'bk2', 'Wv2', 'bv2', 'We2', 'Wskip2', 'bskip2')}
    del _L1_gnn_all

    def _L2_gnn_setup():
        import jax, jax.numpy as jnp
        import numpy as np
        N, E, IN_C, H, C = (3125, 50000, 128, 4, 32)
        key = jax.random.key(seed)
        ks = jax.random.split(key, 10)
        s = 1.0 / np.sqrt(IN_C)
        x = jax.random.normal(ks[0], (N, IN_C), dtype=jnp.float32)
        edge_index = jax.random.randint(ks[1], (2, E), 0, N, dtype=jnp.int64)
        Wq = jax.random.uniform(ks[2], (IN_C, H * C), jnp.float32, -s, s)
        bq = jax.random.uniform(ks[3], (H * C,), jnp.float32, -s, s)
        Wk = jax.random.uniform(ks[4], (IN_C, H * C), jnp.float32, -s, s)
        bk = jax.random.uniform(ks[5], (H * C,), jnp.float32, -s, s)
        Wv = jax.random.uniform(ks[6], (IN_C, H * C), jnp.float32, -s, s)
        bv = jax.random.uniform(ks[7], (H * C,), jnp.float32, -s, s)
        Wr = jax.random.uniform(ks[8], (IN_C, H * C), jnp.float32, -s, s)
        br = jax.random.uniform(ks[9], (H * C,), jnp.float32, -s, s)
        return {'x': x, 'edge_index': edge_index, 'Wq': Wq, 'bq': bq, 'Wk': Wk, 'bk': bk, 'Wv': Wv, 'bv': bv, 'Wr': Wr, 'br': br}
    _L2_gnn_all = _L2_gnn_setup()
    _L2_gnn_in = {k: v for k, v in _L2_gnn_all.items() if k in ('Wq', 'bq', 'Wk', 'bk', 'Wv', 'bv', 'Wr', 'br')}
    del _L2_gnn_all

    def _L3_gnn_setup():
        import jax, jax.numpy as jnp
        import numpy as np
        N = 2500
        E = 40000
        IN_DIM = 128
        HID_DIM = 128
        OUT_DIM = 128
        HEADS = 8
        DH1 = HID_DIM // HEADS
        DH2 = OUT_DIM // HEADS
        NEG_SLOPE = 0.2
        LN_EPS = 1e-05

        def gatv2_layer(x, Wl, Wr, att, bias, src, dst, heads, dh):
            n = x.shape[0]
            xl = (x @ Wl).reshape(n, heads, dh)
            xr = (x @ Wr).reshape(n, heads, dh)
            m = xl[src] + xr[dst]
            e = jnp.einsum('ehd,hd->eh', jax.nn.leaky_relu(m, NEG_SLOPE), att)
            emax = jax.ops.segment_max(e, dst, num_segments=n)
            ex = jnp.exp(e - emax[dst])
            denom = jax.ops.segment_sum(ex, dst, num_segments=n)
            alpha = ex / denom[dst]
            out = jax.ops.segment_sum(alpha[..., None] * xl[src], dst, num_segments=n)
            return out.reshape(n, heads * dh) + bias

        def layer_norm(x, g, b):
            mu = jnp.mean(x, axis=-1, keepdims=True)
            var = jnp.mean((x - mu) ** 2, axis=-1, keepdims=True)
            return (x - mu) * jax.lax.rsqrt(var + LN_EPS) * g + b
        key = jax.random.key(seed)
        ks = jax.random.split(key, 12)
        s1 = 1.0 / np.sqrt(IN_DIM)
        s2 = 1.0 / np.sqrt(HID_DIM)
        return {'x': jax.random.normal(ks[0], (N, IN_DIM), jnp.float32), 'edge_idx': jax.random.randint(ks[1], (2, E), 0, N), 'Wl1': jax.random.normal(ks[2], (IN_DIM, HEADS * DH1), jnp.float32) * s1, 'Wr1': jax.random.normal(ks[3], (IN_DIM, HEADS * DH1), jnp.float32) * s1, 'att1': jax.random.normal(ks[4], (HEADS, DH1), jnp.float32) * s2, 'b1': jnp.zeros((HEADS * DH1,), jnp.float32), 'g1': jnp.ones((HID_DIM,), jnp.float32), 'be1': jnp.zeros((HID_DIM,), jnp.float32), 'Wl2': jax.random.normal(ks[5], (HID_DIM, HEADS * DH2), jnp.float32) * s2, 'Wr2': jax.random.normal(ks[6], (HID_DIM, HEADS * DH2), jnp.float32) * s2, 'att2': jax.random.normal(ks[7], (HEADS, DH2), jnp.float32) * s2, 'b2': jnp.zeros((HEADS * DH2,), jnp.float32), 'g2': jnp.ones((OUT_DIM,), jnp.float32), 'be2': jnp.zeros((OUT_DIM,), jnp.float32)}
    _L3_gnn_all = _L3_gnn_setup()
    _L3_gnn_in = {k: v for k, v in _L3_gnn_all.items() if k in ('Wl1', 'Wr1', 'att1', 'b1', 'g1', 'be1', 'Wl2', 'Wr2', 'att2', 'b2', 'g2', 'be2')}
    del _L3_gnn_all
    return {'x': x, 'src': src, 'dst': dst, 'edge_attr_64': edge_attr_64, 'edge_weight': edge_weight, 'node_vec': node_vec, 'L0_gnn_W_fc': _L0_gnn_in['W_fc'], 'L0_gnn_a_l': _L0_gnn_in['a_l'], 'L0_gnn_a_r': _L0_gnn_in['a_r'], 'L0_gnn_ln_gamma': _L0_gnn_in['ln_gamma'], 'L0_gnn_ln_beta': _L0_gnn_in['ln_beta'], 'L0_gnn_W1': _L0_gnn_in['W1'], 'L0_gnn_b1': _L0_gnn_in['b1'], 'L0_gnn_W2': _L0_gnn_in['W2'], 'L0_gnn_b2': _L0_gnn_in['b2'], 'L1_gnn_Wt': _L1_gnn_in['Wt'], 'L1_gnn_bt': _L1_gnn_in['bt'], 'L1_gnn_Wq1': _L1_gnn_in['Wq1'], 'L1_gnn_bq1': _L1_gnn_in['bq1'], 'L1_gnn_Wk1': _L1_gnn_in['Wk1'], 'L1_gnn_bk1': _L1_gnn_in['bk1'], 'L1_gnn_Wv1': _L1_gnn_in['Wv1'], 'L1_gnn_bv1': _L1_gnn_in['bv1'], 'L1_gnn_We1': _L1_gnn_in['We1'], 'L1_gnn_Wskip1': _L1_gnn_in['Wskip1'], 'L1_gnn_bskip1': _L1_gnn_in['bskip1'], 'L1_gnn_Wq2': _L1_gnn_in['Wq2'], 'L1_gnn_bq2': _L1_gnn_in['bq2'], 'L1_gnn_Wk2': _L1_gnn_in['Wk2'], 'L1_gnn_bk2': _L1_gnn_in['bk2'], 'L1_gnn_Wv2': _L1_gnn_in['Wv2'], 'L1_gnn_bv2': _L1_gnn_in['bv2'], 'L1_gnn_We2': _L1_gnn_in['We2'], 'L1_gnn_Wskip2': _L1_gnn_in['Wskip2'], 'L1_gnn_bskip2': _L1_gnn_in['bskip2'], 'L2_gnn_Wq': _L2_gnn_in['Wq'], 'L2_gnn_bq': _L2_gnn_in['bq'], 'L2_gnn_Wk': _L2_gnn_in['Wk'], 'L2_gnn_bk': _L2_gnn_in['bk'], 'L2_gnn_Wv': _L2_gnn_in['Wv'], 'L2_gnn_bv': _L2_gnn_in['bv'], 'L2_gnn_Wr': _L2_gnn_in['Wr'], 'L2_gnn_br': _L2_gnn_in['br'], 'L3_gnn_Wl1': _L3_gnn_in['Wl1'], 'L3_gnn_Wr1': _L3_gnn_in['Wr1'], 'L3_gnn_att1': _L3_gnn_in['att1'], 'L3_gnn_b1': _L3_gnn_in['b1'], 'L3_gnn_g1': _L3_gnn_in['g1'], 'L3_gnn_be1': _L3_gnn_in['be1'], 'L3_gnn_Wl2': _L3_gnn_in['Wl2'], 'L3_gnn_Wr2': _L3_gnn_in['Wr2'], 'L3_gnn_att2': _L3_gnn_in['att2'], 'L3_gnn_b2': _L3_gnn_in['b2'], 'L3_gnn_g2': _L3_gnn_in['g2'], 'L3_gnn_be2': _L3_gnn_in['be2']}

def reference(x, src, dst, edge_attr_64, edge_weight, node_vec, L0_gnn_W_fc, L0_gnn_a_l, L0_gnn_a_r, L0_gnn_ln_gamma, L0_gnn_ln_beta, L0_gnn_W1, L0_gnn_b1, L0_gnn_W2, L0_gnn_b2, L1_gnn_Wt, L1_gnn_bt, L1_gnn_Wq1, L1_gnn_bq1, L1_gnn_Wk1, L1_gnn_bk1, L1_gnn_Wv1, L1_gnn_bv1, L1_gnn_We1, L1_gnn_Wskip1, L1_gnn_bskip1, L1_gnn_Wq2, L1_gnn_bq2, L1_gnn_Wk2, L1_gnn_bk2, L1_gnn_Wv2, L1_gnn_bv2, L1_gnn_We2, L1_gnn_Wskip2, L1_gnn_bskip2, L2_gnn_Wq, L2_gnn_bq, L2_gnn_Wk, L2_gnn_bk, L2_gnn_Wv, L2_gnn_bv, L2_gnn_Wr, L2_gnn_br, L3_gnn_Wl1, L3_gnn_Wr1, L3_gnn_att1, L3_gnn_b1, L3_gnn_g1, L3_gnn_be1, L3_gnn_Wl2, L3_gnn_Wr2, L3_gnn_att2, L3_gnn_b2, L3_gnn_g2, L3_gnn_be2):
    import jax
    import jax.numpy as jnp

    def _L0_gnn_ref(x, W_fc, a_l, a_r, ln_gamma, ln_beta, W1, b1, W2, b2, edge_src, edge_dst):
        import jax, jax.numpy as jnp
        import numpy as np
        N, E, D, H = (3125, 50000, 128, 8)
        DH = D // H
        DFF = 512

        def _gat(x, W_fc, a_l, a_r, edge_src, edge_dst):
            z = jnp.einsum('nd,hdk->nhk', x, W_fc)
            el = jnp.einsum('nhk,hk->nh', z, a_l)
            er = jnp.einsum('nhk,hk->nh', z, a_r)
            e = jax.nn.leaky_relu(el[edge_src] + er[edge_dst], 0.01)
            m = jax.ops.segment_max(e, edge_dst, num_segments=N)
            m = jnp.where(jnp.isfinite(m), m, 0.0)
            ee = jnp.exp(e - m[edge_dst])
            s = jax.ops.segment_sum(ee, edge_dst, num_segments=N)
            alpha = ee / jnp.maximum(s[edge_dst], 1e-09)
            msg = alpha[:, :, None] * z[edge_src]
            h = jax.ops.segment_sum(msg, edge_dst, num_segments=N)
            return h.reshape(N, H * DH)
        h = jax.nn.elu(_gat(x, W_fc, a_l, a_r, edge_src, edge_dst))
        h = x + h
        mu = jnp.mean(h, axis=-1, keepdims=True)
        var = jnp.var(h, axis=-1, keepdims=True)
        ln = (h - mu) * jax.lax.rsqrt(var + 1e-05) * ln_gamma + ln_beta
        inter = jax.nn.relu(ln @ W1 + b1)
        return inter @ W2 + b2 + h

    def _L1_gnn_ref(x, last_update, t, msg, edge_index, Wt, bt, Wq1, bq1, Wk1, bk1, Wv1, bv1, We1, Wskip1, bskip1, Wq2, bq2, Wk2, bk2, Wv2, bv2, We2, Wskip2, bskip2):
        import jax, jax.numpy as jnp
        import numpy as np
        N = 6250
        E = 40000
        IN_CH = 128
        OUT_CH = 128
        MSG_DIM = 64
        TIME_DIM = 64
        EDGE_DIM = MSG_DIM + TIME_DIM
        HEADS = 4

        def _linear_params(key, fan_in, fan_out, bias=True, scale=0.02):
            k1, k2 = jax.random.split(key)
            W = jax.random.normal(k1, (fan_in, fan_out), jnp.float32) * scale
            if bias:
                b = jax.random.normal(k2, (fan_out,), jnp.float32) * scale
                return (W, b)
            return W

        def transformer_conv(x, src, dst, edge_attr, Wq, bq, Wk, bk, Wv, bv, We, Wskip, bskip):
            n = x.shape[0]
            HC = Wq.shape[1]
            C = HC // HEADS
            q = (x @ Wq + bq).reshape(n, HEADS, C)
            k = (x @ Wk + bk).reshape(n, HEADS, C)
            v = (x @ Wv + bv).reshape(n, HEADS, C)
            e = (edge_attr @ We).reshape(-1, HEADS, C)
            k_j = k[src] + e
            v_j = v[src] + e
            alpha = jnp.einsum('ehc,ehc->eh', q[dst], k_j) / jnp.sqrt(jnp.float32(C))
            amax = jax.ops.segment_max(alpha, dst, num_segments=n)
            expa = jnp.exp(alpha - amax[dst])
            denom = jax.ops.segment_sum(expa, dst, num_segments=n)
            attn = expa / (denom[dst] + 1e-16)
            out = jax.ops.segment_sum(attn[:, :, None] * v_j, dst, num_segments=n)
            out = out.reshape(n, HC)
            return out + x @ Wskip + bskip
        src, dst = (edge_index[0], edge_index[1])
        rel_t = last_update[src] - t
        rel_t_enc = jnp.cos(rel_t[:, None] * Wt[0][None, :] + bt)
        edge_attr = jnp.concatenate([rel_t_enc, msg], axis=-1)
        h = transformer_conv(x, src, dst, edge_attr, Wq1, bq1, Wk1, bk1, Wv1, bv1, We1, Wskip1, bskip1)
        return transformer_conv(h, src, dst, edge_attr, Wq2, bq2, Wk2, bk2, Wv2, bv2, We2, Wskip2, bskip2)

    def _L2_gnn_ref(x, edge_index, Wq, bq, Wk, bk, Wv, bv, Wr, br):
        import jax, jax.numpy as jnp
        import numpy as np
        N, E, IN_C, H, C = (3125, 50000, 128, 4, 32)
        n = x.shape[0]
        row, col = (edge_index[0], edge_index[1])
        q = (x @ Wq + bq).reshape(n, H, C)
        k = (x @ Wk + bk).reshape(n, H, C)
        v = (x @ Wv + bv).reshape(n, H, C)
        scores = jnp.einsum('ehc,ehc->eh', q[col], k[row]) / np.sqrt(C)
        m = jax.ops.segment_max(scores, col, num_segments=n)
        ex = jnp.exp(scores - m[col])
        denom = jax.ops.segment_sum(ex, col, num_segments=n)
        w = ex / denom[col]
        out = jax.ops.segment_sum(v[row] * w[:, :, None], col, num_segments=n)
        out = out.reshape(n, H * C)
        root = x @ Wr + br
        return out + root

    def _L3_gnn_ref(x, edge_idx, Wl1, Wr1, att1, b1, g1, be1, Wl2, Wr2, att2, b2, g2, be2):
        import jax, jax.numpy as jnp
        import numpy as np
        N = 2500
        E = 40000
        IN_DIM = 128
        HID_DIM = 128
        OUT_DIM = 128
        HEADS = 8
        DH1 = HID_DIM // HEADS
        DH2 = OUT_DIM // HEADS
        NEG_SLOPE = 0.2
        LN_EPS = 1e-05

        def gatv2_layer(x, Wl, Wr, att, bias, src, dst, heads, dh):
            n = x.shape[0]
            xl = (x @ Wl).reshape(n, heads, dh)
            xr = (x @ Wr).reshape(n, heads, dh)
            m = xl[src] + xr[dst]
            e = jnp.einsum('ehd,hd->eh', jax.nn.leaky_relu(m, NEG_SLOPE), att)
            emax = jax.ops.segment_max(e, dst, num_segments=n)
            ex = jnp.exp(e - emax[dst])
            denom = jax.ops.segment_sum(ex, dst, num_segments=n)
            alpha = ex / denom[dst]
            out = jax.ops.segment_sum(alpha[..., None] * xl[src], dst, num_segments=n)
            return out.reshape(n, heads * dh) + bias

        def layer_norm(x, g, b):
            mu = jnp.mean(x, axis=-1, keepdims=True)
            var = jnp.mean((x - mu) ** 2, axis=-1, keepdims=True)
            return (x - mu) * jax.lax.rsqrt(var + LN_EPS) * g + b
        src, dst = (edge_idx[0], edge_idx[1])
        h = gatv2_layer(x, Wl1, Wr1, att1, b1, src, dst, HEADS, DH1)
        h = layer_norm(jax.nn.relu(h), g1, be1)
        h = gatv2_layer(h, Wl2, Wr2, att2, b2, src, dst, HEADS, DH2)
        h = layer_norm(jax.nn.relu(h), g2, be2)
        return h
    edge_index = jnp.stack([src, dst])
    h = jnp.maximum(_layernorm(x, axis=-1), 0.0)
    x = x + _L0_gnn_ref(h, L0_gnn_W_fc, L0_gnn_a_l, L0_gnn_a_r, L0_gnn_ln_gamma, L0_gnn_ln_beta, L0_gnn_W1, L0_gnn_b1, L0_gnn_W2, L0_gnn_b2, src, dst)
    h = jnp.maximum(_layernorm(x, axis=-1), 0.0)
    x = x + _L1_gnn_ref(h, node_vec, edge_weight, edge_attr_64, edge_index, L1_gnn_Wt, L1_gnn_bt, L1_gnn_Wq1, L1_gnn_bq1, L1_gnn_Wk1, L1_gnn_bk1, L1_gnn_Wv1, L1_gnn_bv1, L1_gnn_We1, L1_gnn_Wskip1, L1_gnn_bskip1, L1_gnn_Wq2, L1_gnn_bq2, L1_gnn_Wk2, L1_gnn_bk2, L1_gnn_Wv2, L1_gnn_bv2, L1_gnn_We2, L1_gnn_Wskip2, L1_gnn_bskip2)
    h = jnp.maximum(_layernorm(x, axis=-1), 0.0)
    x = x + _L2_gnn_ref(h, edge_index, L2_gnn_Wq, L2_gnn_bq, L2_gnn_Wk, L2_gnn_bk, L2_gnn_Wv, L2_gnn_bv, L2_gnn_Wr, L2_gnn_br)
    h = jnp.maximum(_layernorm(x, axis=-1), 0.0)
    x = x + _L3_gnn_ref(h, edge_index, L3_gnn_Wl1, L3_gnn_Wr1, L3_gnn_att1, L3_gnn_b1, L3_gnn_g1, L3_gnn_be1, L3_gnn_Wl2, L3_gnn_Wr2, L3_gnn_att2, L3_gnn_b2, L3_gnn_g2, L3_gnn_be2)
    return x

_drawn_inputs = setup_inputs


def setup_inputs(seed=0):
    import zlib

    import numpy as np

    out = dict(_drawn_inputs(seed))
    spreads = {'L0_gnn_ln_gamma': (1.0, 0.2),
     'L0_gnn_ln_beta': (0.0, 0.3),
     'L0_gnn_b1': (0.0, 0.1),
     'L0_gnn_b2': (0.0, 0.1),
     'L3_gnn_b1': (0.0, 0.1),
     'L3_gnn_g1': (1.0, 0.2),
     'L3_gnn_be1': (0.0, 0.1),
     'L3_gnn_b2': (0.0, 0.1),
     'L3_gnn_g2': (1.0, 0.2),
     'L3_gnn_be2': (0.0, 0.1)}
    factors = {'edge_attr_64': 3.843,
     'edge_weight': 5.981,
     'node_vec': 6.008,
     'L0_gnn_a_l': 8.0,
     'L0_gnn_a_r': 8.0,
     'L1_gnn_bt': 8.0,
     'L1_gnn_Wq1': 8.0,
     'L1_gnn_bq1': 8.0,
     'L1_gnn_Wk1': 8.0,
     'L1_gnn_bk1': 8.0,
     'L1_gnn_Wv1': 3.056,
     'L1_gnn_bv1': 8.0,
     'L1_gnn_We1': 5.289,
     'L1_gnn_bskip1': 8.0,
     'L1_gnn_Wq2': 8.0,
     'L1_gnn_bq2': 8.0,
     'L1_gnn_Wk2': 8.0,
     'L1_gnn_bk2': 8.0,
     'L1_gnn_bv2': 4.222,
     'L1_gnn_bskip2': 4.85,
     'L2_gnn_Wq': 8.0,
     'L2_gnn_bq': 8.0,
     'L2_gnn_Wk': 8.0,
     'L2_gnn_bk': 8.0,
     'L3_gnn_Wr1': 7.956,
     'L3_gnn_Wr2': 8.0,
     'L3_gnn_att2': 8.0}
    for name, (base, spread) in spreads.items():
        noise = np.random.default_rng([zlib.crc32(name.encode()), seed]).standard_normal(out[name].shape)
        drawn = base * np.exp(spread * noise) if base else spread * noise
        out[name] = jnp.asarray(drawn.astype(out[name].dtype))
    for name, factor in factors.items():
        out[name] = (out[name] * factor).astype(out[name].dtype)
    return out
```

```python
from contextlib import ExitStack

import numpy as np

import concourse.bass as bass
from concourse import mybir

F32 = mybir.dt.float32
I32 = mybir.dt.int32
ALU = mybir.AluOpType
ACT = mybir.ActivationFunctionType
AX = mybir.AxisListType

P = 128
D = 128
G = 8
HALF = G // 2
SLOTS = 3
FAR = -1.0e38
TINY = 1.0e-9
EPS = 1.0e-5
MAGIC = 12582912.0
TWO_PI_HIGH = 6.28125
TWO_PI_LOW = float(2 * np.pi - 6.28125)


def bc(ap, shape):
    return ap.to_broadcast(shape)


class Plan:

    def __init__(self, nc, ctx, x, src, edge_attr):
        self.N, self.E = x.shape[0], src.shape[0]
        tiles = -(-self.E // P)
        self.NG = -(-tiles // G)
        self.TT = self.NG * G
        self.TB = -(-self.TT // P)
        self.NB = 2 * -(-self.N // (2 * P))
        self.NP = self.NB * P
        self.DL_W = 2 * P + 4
        self.edge_attr = edge_attr
        assert self.NG >= 9 and x.shape[1] == D

        def sb(name, shape, dt=F32):
            return ctx.enter_context(nc.sbuf_tensor(name, shape, dt))

        def dram(name, shape):
            return nc.dram_tensor(name, shape, F32, kind="Internal").ap()

        NB, TB, NP, TT = self.NB, self.TB, self.NP, self.TT
        self.banks = [ctx.enter_context(nc.psum_tensor(f"bank{b}", [P, 512], F32)) for b in range(8)]
        self.ident = sb("ident", [P, P])
        self.head8, self.head4 = sb("head8", [P, D]), sb("head4", [P, D])
        self.iota_free, self.iota_free_i = sb("iota_free", [P, P]), sb("iota_free_i", [P, P], I32)
        self.node_id_i = sb("node_id_i", [P, NB], I32)
        self.half_pi = sb("half_pi", [P, 1])
        self.eps = sb("eps", [P, 1])
        self.x_sb = sb("x_sb", [P, NB, D])
        self.hn = sb("hn", [P, NB, D])
        self.res = sb("res", [P, NB, D])
        self.node_vec_sb = sb("node_vec_sb", [P, NB])
        self.src_col = sb("src_col", [P, TB * P])
        self.rank_col = sb("rank_col", [P, TB * P])
        self.last_col = sb("last_col", [P, TB * P])
        self.weight_col = sb("weight_col", [P, TB * P])
        self.whole_row = sb("whole_row", [P, TB * P])
        self.whole_pen = sb("whole_pen", [P, TB * P])
        self.window_i = sb("window_i", [1, TB * P], I32)
        self.tile_last_i = sb("tile_last_i", [P, TB], I32)
        self.part_i = sb("part_i", [P, NB], I32)
        self.carry_i = sb("carry_i", [P, NB], I32)
        self.carry_pen = sb("carry_pen", [P, NB])
        self.has_edges = sb("has_edges", [P, NB])
        self.compact_i = sb("compact_i", [P, NB], I32)
        self.dl_tab = dram("dl_tab", [TB * P, self.DL_W])
        self.neg_tab = {H: dram(f"neg_tab{H}", [TB * P * H, 2 * P]) for H in (8, 4)}
        self.row_tab = dram("row_tab", [3 * TB * P])
        self.gat_tab = dram("gat_tab", [NP, D + 16])
        self.kv_tab = dram("kv_tab", [NP, 2 * D])
        self.xl_tab = dram("xl_tab", [NP, D])
        self.q_tab = dram("q_tab", [NP + P, D])
        self.er_tab = dram("er_tab", [NP + P, 8])
        self.attr_tab = dram("attr_tab", [self.NG * P, G * P])
        self.part_tab = {H: dram(f"part_tab{H}", [TT * P, D + 2 * H]) for H in (8, 4)}
        self.carry_tab = {H: dram(f"carry_tab{H}", [TB * P, D + 2 * H]) for H in (8, 4)}


def wait(eng, sem, value):
    if isinstance(value, int) and value <= 0:
        return
    eng.wait_ge(sem, value)


def pairs(eng, pair, count):
    pair(0)
    with eng.Fori(1, count) as j:
        pair(j)


def settle(eng, passed):
    eng.sem_inc(passed, 1)


class Stage:

    def __init__(self, nc, shared):
        self.nc, self.shared, self.used = nc, shared, {}
        shared["stages"] += 1
        self.number = shared["stages"]

    def __call__(self, name):
        if name not in self.used:
            free = self.shared["semaphores"]
            if len(self.used) == len(free):
                free.append(self.nc.alloc_semaphore(f"stage_semaphore_{len(free)}"))
            self.used[name] = free[len(self.used)]
        return self.used[name]

    def indirect(self, name):
        return self.nc.alloc_semaphore(f"s{self.number}_{name}")

    def tensor(self, ctx, name, shape, dt=F32):
        return ctx.enter_context(self.nc.sbuf_tensor(f"s{self.number}_{name}", shape, dt))

    def close(self):
        with self.nc.Block() as block:
            @block.gpsimd
            def _(pool):
                for s in self.used.values():
                    pool.sem_clear(s)


def chain(eng, sem):
    count = [0]

    def link(ins):
        count[0] += 1
        ins.then_inc(sem, 1)
        eng.wait_ge(sem, count[0])

    return link



def setup_graph(nc, pl, sems, x, src, dst, edge_weight, node_vec):
    sem = Stage(nc, sems)
    TB, NB = pl.TB, pl.NB
    E = pl.E
    whole_tiles = E // P
    whole_blocks = whole_tiles // P
    rest_tiles = whole_tiles - whole_blocks * P
    rest_edges = E - whole_tiles * P

    with ExitStack() as ctx:
        def sb(name, shape, dt=F32):
            return sem.tensor(ctx, name, shape, dt)

        src_i = sb("src_i", [P, TB, P], I32)
        dst_i = sb("dst_i", [P, TB, P], I32)
        weight = sb("weight", [P, TB, P])
        dst_f = sb("dst_f", [P, TB, P])
        src_f = sb("src_f", [P, TB, P])
        start = sb("start", [P, TB, P])
        local_start = sb("local_start", [P, TB, P])
        not_first = sb("not_first", [P, TB, P])
        rank1 = sb("rank1", [P, TB, P])
        last_in_tile = sb("last_in_tile", [P, TB, P])
        dl = sb("dl", [P, TB, pl.DL_W])
        neg = sb("neg", [P, TB, 2 * P])
        dst_last1 = sb("dst_last1", [P, TB])
        prev_dst = sb("prev_dst", [P, TB])
        lr_last = sb("lr_last", [P, TB])
        prev_lr = sb("prev_lr", [P, TB])
        n_starts = sb("n_starts", [P, TB])
        totals = sb("totals", [P, TB])
        running = sb("running", [P, TB])
        ones_row = sb("ones_row", [P, max(TB, NB)])
        window = sb("window", [P, TB])
        whole = sb("whole", [P, TB])
        tile_id = sb("tile_id", [P, TB])
        tile_last = sb("tile_last", [P, TB])
        rows3 = sb("rows3", [P, 3 * TB])
        rows3_t = sb("rows3_t", [3 * TB, P])
        last_row = sb("last_row", [P, TB * P])
        window_f = sb("window_f", [1, TB * P])
        shift_m = sb("shift_m", [P, P])
        corner_m = sb("corner_m", [P, P])
        below_m = sb("below_m", [P, P])
        ones_m = sb("ones_m", [P, P])
        zeros = sb("zeros", [P, P])
        le = sb("le", [P, TB * P])
        tb_f = sb("tb_f", [P, NB])
        tb_i = sb("tb_i", [P, NB], I32)
        found = sb("found", [P, NB, pl.DL_W])
        hit = sb("hit", [P, NB, P])
        cnt = sb("cnt", [P, NB])
        row_end = sb("row_end", [P, NB])
        row_start = sb("row_start", [P, NB])
        lr_end = sb("lr_end", [P, NB])
        lr_sel = sb("lr_sel", [P, NB])
        at_edge = sb("at_edge", [P, NB])
        pe_pos = sb("pe_pos", [P, NB])
        te = sb("te", [P, NB])
        tmp = sb("tmp", [P, NB])
        node_id = sb("node_id", [P, NB])
        before = sb("before", [P, NB])
        n_tot = sb("n_tot", [P, NB])
        n_run = sb("n_run", [P, NB])
        compact = sb("compact", [P, NB])

        padded, loaded = sem("padded"), sem("loaded")
        consts, made = sem("consts"), sem("pool_made")
        shifted, shift_used = sem("shifted"), sem("shift_used")
        tables, marks, rows = sem("tables_stored"), sem("marks_stored"), sem("rows_stored")
        turned, turned_used = sem("turned"), sem("turned_used")
        dve = sem("dve")
        dl_ready, last_ready = sem("dl_ready"), sem("last_ready")
        starts_ready, prefix_done = sem("starts_ready"), sem("prefix_done")
        rows3_ready, rows3_turned, rows3_copied = sem("rows3_ready"), sem("rows3_turned"), sem("rows3_copied")
        row_loaded = sem("row_loaded")
        tb_ready, searched = sem("tb_ready"), sem.indirect("searched")
        end_ready, end_shifted = sem("end_ready"), sem("end_shifted")
        has_ready, has_prefix = sem("has_ready"), sem("has_prefix")
        lists_ready = sem("lists_ready")
        small_loaded, zeroed = sem("small_loaded"), sem("zeroed")
        zero_done = sem("zero_done")
        ps = pl.banks

        with nc.Block() as block:
            @block.sync
            def _(sp):
                def load_tiles(tile, flat):
                    n = 0
                    if whole_blocks:
                        sp.dma_start(tile[:, 0:whole_blocks, :],
                                     flat[0:whole_blocks * P * P].rearrange("(g p e) -> p g e", p=P, e=P)
                                     ).then_inc(loaded, 16)
                        n += 1
                    if rest_tiles:
                        lo = whole_blocks * P * P
                        sp.dma_start(tile[0:rest_tiles, whole_blocks, :],
                                     flat[lo:lo + rest_tiles * P].rearrange("(p e) -> p e", e=P)
                                     ).then_inc(loaded, 16)
                        n += 1
                    if rest_edges:
                        sp.dma_start(tile[rest_tiles:rest_tiles + 1, whole_blocks, 0:rest_edges],
                                     flat[whole_tiles * P:E].rearrange("(p e) -> p e", p=1)
                                     ).then_inc(loaded, 16)
                        n += 1
                    return n

                sp.wait_ge(padded, 4)
                pl.list_loads = load_tiles(dst_i, dst) + load_tiles(src_i, src) + load_tiles(weight, edge_weight)
                full = pl.N // P
                sp.dma_start(pl.x_sb[:, 0:full, :], x[0:full * P, :].rearrange("(b p) c -> p b c", p=P)
                             ).then_inc(small_loaded, 16)
                sp.dma_start(pl.x_sb[0:pl.N - full * P, full, :], x[full * P:pl.N, :]).then_inc(small_loaded, 16)
                sp.dma_start(pl.node_vec_sb[:, 0:full], node_vec[0:full * P].rearrange("(b p) -> p b", p=P),
                             allow_slow_non_contiguous=True).then_inc(small_loaded, 16)
                sp.dma_start(pl.node_vec_sb[0:pl.N - full * P, full:full + 1],
                             node_vec[full * P:pl.N].rearrange("(p b) -> p b", b=1),
                             allow_slow_non_contiguous=True).then_inc(small_loaded, 16)
                sp.wait_ge(zero_done, 1)
                sp.dma_start(pl.q_tab[pl.NP:pl.NP + P, :], zeros[:, :]).then_inc(zeroed, 16)
                sp.dma_start(pl.er_tab[pl.NP:pl.NP + P, :], zeros[:, 0:8]).then_inc(zeroed, 16)
                sp.wait_ge(dl_ready, 1)
                sp.dma_start(pl.dl_tab.rearrange("(g p) w -> p g w", p=P), dl[:, :, :]).then_inc(tables, 16)
                for H, tab in pl.neg_tab.items():
                    for h in range(H):
                        sp.dma_start(tab.rearrange("(g p h) w -> p g h w", p=P, h=H)[:, :, h, :], neg[:, :, :]
                                     ).then_inc(marks, 16)
                sp.wait_ge(rows3_copied, 1)
                sp.dma_start(pl.row_tab.rearrange("(k p) -> k p", p=P), rows3_t[:, :]).then_inc(rows, 16)
                sp.wait_ge(rows, 16)
                n = TB * P
                sp.dma_start(last_row[:, :], pl.row_tab[0:n].partition_broadcast(P)).then_inc(row_loaded, 16)
                sp.dma_start(pl.whole_row[:, :], pl.row_tab[n:2 * n].partition_broadcast(P)).then_inc(row_loaded, 16)
                sp.dma_start(window_f[:, :], pl.row_tab[2 * n:3 * n].rearrange("(a n) -> a n", a=1)
                             ).then_inc(row_loaded, 16)
                sp.wait_ge(zeroed, 32)
                sp.wait_ge(marks, 16 * sum(pl.neg_tab))
                sp.wait_ge(small_loaded, 64)

            @block.gpsimd
            def _(pool):
                pool.memset(zeros[:, :], 0.0).then_inc(zero_done, 1)
                for m in (pl.ident, shift_m, corner_m, below_m, pl.head8, pl.head4):
                    pool.memset(m[:, :], 0.0).then_inc(made, 1)
                pool.memset(ones_m[:, :], 1.0).then_inc(made, 1)
                pool.wait_ge(made, 7)
                pool.affine_select(out=pl.ident[:, :], in_=pl.ident[:, :], compare_op=ALU.not_equal, fill=1.0, base=0,
                                   pattern=[[-1, P]], channel_multiplier=1).then_inc(made, 1)
                pool.affine_select(out=shift_m[:, :], in_=shift_m[:, :], compare_op=ALU.not_equal, fill=1.0, base=1,
                                   pattern=[[-1, P]], channel_multiplier=1).then_inc(made, 1)
                pool.affine_select(out=corner_m[:, :], in_=corner_m[:, :], compare_op=ALU.not_equal, fill=1.0,
                                   base=-(P - 1), pattern=[[-P, P]], channel_multiplier=1).then_inc(made, 1)
                pool.affine_select(out=below_m[:, :], in_=below_m[:, :], compare_op=ALU.is_ge, fill=1.0, base=0,
                                   pattern=[[-1, P]], channel_multiplier=1).then_inc(made, 1)
                for m, c in ((pl.head8, 16), (pl.head4, 32)):
                    v = m[:, :].rearrange("h (a c) -> h a c", c=c)
                    pool.affine_select(out=v, in_=v, compare_op=ALU.not_equal, fill=1.0, base=0,
                                       pattern=[[-1, D // c], [0, c]], channel_multiplier=1).then_inc(made, 1)
                pool.iota(pl.iota_free_i[:, :], pattern=[[1, P]], base=0, channel_multiplier=0).then_inc(made, 1)
                pool.iota(pl.node_id_i[:, :], pattern=[[P, NB]], base=0, channel_multiplier=1).then_inc(made, 1)
                pool.wait_ge(tables, 16)
                pool.wait_ge(tb_ready, 1)
                for b in range(NB):
                    pool.indirect_dma_start(out=found[:, b, :], out_offset=None, in_=pl.dl_tab,
                                            in_offset=bass.IndirectOffsetOnAxis(ap=tb_i[:, b:b + 1], axis=0)
                                            ).then_inc(searched, 16)

            @block.vector
            def _(v):
                link = chain(v, dve)
                v.memset(dst_i[:, :, :], pl.NP).then_inc(padded, 1)
                v.memset(src_i[:, :, :], 0).then_inc(padded, 1)
                v.memset(weight[:, :, :], 0.0).then_inc(padded, 1)
                v.memset(pl.x_sb[:, :, :], 0.0)
                v.memset(pl.node_vec_sb[:, :], 0.0).then_inc(padded, 1)
                v.memset(ones_row[:, :], 1.0)
                v.memset(pl.half_pi[:, :], float(np.pi / 2))
                v.memset(pl.eps[:, :], EPS)
                v.memset(not_first[:, :, :], 1.0)
                v.memset(dl[:, :, 2 * P:pl.DL_W], 0.0)
                link(v.memset(last_in_tile[:, :, P - 1:P], 1.0))
                link(v.memset(not_first[:, :, 0:1], 0.0))
                v.wait_ge(made, 15)
                v.tensor_copy(pl.iota_free[:, :], pl.iota_free_i[:, :])
                link(v.tensor_copy(node_id[:, :], pl.node_id_i[:, :]))
                v.wait_ge(loaded, 16 * pl.list_loads)
                link(v.tensor_copy(dst_f[:, :, :], dst_i[:, :, :]))
                v.tensor_copy(dl[:, :, 0:P], dst_f[:, :, :])
                link(v.tensor_copy(src_f[:, :, :], src_i[:, :, :]))
                v.tensor_scalar(dst_last1[:, :], dst_f[:, :, P - 1], 1.0, None, ALU.add).then_inc(last_ready, 1)
                v.wait_ge(shifted, 1)
                link(v.tensor_scalar(prev_dst[:, :], ps[0][:, 0:TB], -1.0, None, ALU.add))
                link(v.tensor_tensor(prev_dst[:, 1:TB], prev_dst[:, 1:TB], ps[0][:, 64:64 + TB - 1], ALU.add))
                v.tensor_tensor(start[:, :, 1:P], dst_f[:, :, 1:P], dst_f[:, :, 0:P - 1], ALU.not_equal)
                link(v.tensor_tensor(start[:, :, 0], dst_f[:, :, 0], prev_dst[:, :], ALU.not_equal))
                v.tensor_copy(local_start[:, :, 1:P], start[:, :, 1:P])
                v.memset(local_start[:, :, 0:1], 1.0)
                v.tensor_reduce(n_starts[:, :], start[:, :, :], AX.X, ALU.add).then_inc(starts_ready, 1)
                link(v.tensor_copy(last_in_tile[:, :, 0:P - 1], start[:, :, 1:P]))
                link(v.tensor_tensor_scan(rank1[:, :, :].rearrange("p g e -> p (g e)"),
                                          not_first[:, :, :].rearrange("p g e -> p (g e)"),
                                          local_start[:, :, :].rearrange("p g e -> p (g e)"), 0.0, ALU.mult, ALU.add))
                v.tensor_scalar(neg[:, :, 0:P], local_start[:, :, :], FAR, None, ALU.mult)
                v.tensor_scalar(neg[:, :, P:2 * P], last_in_tile[:, :, :], FAR, None, ALU.mult)
                v.tensor_scalar(lr_last[:, :], rank1[:, :, P - 1], -1.0, None, ALU.add).then_inc(last_ready, 1)
                link(v.tensor_scalar(dl[:, :, P:2 * P], rank1[:, :, :], -1.0, None, ALU.add))
                v.wait_ge(shifted, 2)
                link(v.tensor_copy(prev_lr[:, :], ps[1][:, 0:TB]))
                link(v.tensor_tensor(prev_lr[:, 1:TB], prev_lr[:, 1:TB], ps[1][:, 64:64 + TB - 1], ALU.add))
                v.tensor_copy(dl[:, :, 2 * P], prev_lr[:, :]).then_inc(dl_ready, 1)
                v.wait_ge(prefix_done, 1)
                link(v.tensor_copy(totals[:, :], ps[2][:, 64:64 + TB]))
                link(v.tensor_tensor_scan(running[:, :], ones_row[:, 0:TB], totals[:, :], 0.0, ALU.mult, ALU.add))
                link(v.tensor_tensor(running[:, :], running[:, :], totals[:, :], ALU.subtract))
                link(v.tensor_tensor(window[:, :], running[:, :], ps[2][:, 0:TB], ALU.add))
                link(v.tensor_tensor(window[:, :], window[:, :], start[:, :, 0], ALU.add))
                v.tensor_scalar(rows3[:, 2 * TB:3 * TB], window[:, :], -1.0, None, ALU.add)
                link(v.tensor_scalar(whole[:, :], lr_last[:, :], 0.0, None, ALU.is_equal))
                link(v.tensor_scalar(prev_dst[:, :], start[:, :, 0], -1.0, 1.0, ALU.mult, ALU.add))
                v.tensor_tensor(rows3[:, TB:2 * TB], whole[:, :], prev_dst[:, :], ALU.mult)
                v.tensor_copy(rows3[:, 0:TB], dst_f[:, :, P - 1]).then_inc(rows3_ready, 1)
                link(v.tensor_scalar(tile_id[:, :], node_id[:, 0:TB], float(P), None, ALU.mult))
                link(v.tensor_tensor(tile_last[:, :], tile_id[:, :], lr_last[:, :], ALU.add))
                link(v.tensor_scalar(tile_last[:, :], tile_last[:, :], float(pl.TT * P - 1), None, ALU.min))
                v.tensor_copy(pl.tile_last_i[:, :], tile_last[:, :])
                v.wait_ge(rows3_turned, 1)
                v.tensor_copy(rows3_t[:, :], ps[3][0:3 * TB, 0:P]).then_inc(rows3_copied, 1)
                for n, out in enumerate((pl.src_col, pl.rank_col, pl.last_col, pl.weight_col)):
                    for half in range(2):
                        v.wait_ge(turned, 2 * n + half + 1)
                        lo, hi = (0, 4) if half == 0 else (4, TB)
                        v.tensor_copy(out[:, lo * P:hi * P], ps[4 + half][:, 0:(hi - lo) * P]).then_inc(turned_used, 1)
                v.wait_ge(row_loaded, 48)
                v.tensor_copy(pl.window_i[:, :], window_f[:, :])
                v.tensor_scalar(pl.whole_pen[:, :], pl.whole_row[:, :], -FAR, FAR, ALU.mult, ALU.add)
                for b in range(NB):
                    link(v.tensor_tensor(le[:, :], last_row[:, :], bc(node_id[:, b:b + 1], [P, TB * P]), ALU.is_le))
                    link(v.tensor_reduce(tb_f[:, b:b + 1], le[:, :], AX.X, ALU.add))
                v.tensor_copy(tb_i[:, :], tb_f[:, :]).then_inc(tb_ready, 1)
                v.wait_ge(searched, 16 * NB)
                link(v.tensor_tensor(hit[:, :, :], found[:, :, 0:P],
                                     bc(node_id[:, :].unsqueeze(2), [P, NB, P]), ALU.is_le))
                link(v.tensor_reduce(cnt[:, :], hit[:, :, :], AX.X, ALU.add))
                v.scalar_tensor_tensor(row_end[:, :], tb_f[:, :], float(P), cnt[:, :], ALU.mult, ALU.add
                                       ).then_inc(end_ready, 1)
                v.wait_ge(end_shifted, 1)
                link(v.tensor_copy(row_start[:, :], ps[6][:, 0:NB]))
                link(v.tensor_tensor(row_start[:, 1:NB], row_start[:, 1:NB], ps[6][:, 64:64 + NB - 1], ALU.add))
                v.tensor_tensor(pl.has_edges[:, :], row_end[:, :], row_start[:, :], ALU.is_gt).then_inc(has_ready, 1)
                v.wait_ge(has_ready, 1)
                link(v.tensor_scalar(at_edge[:, :], cnt[:, :], 0.0, None, ALU.is_equal))
                link(v.tensor_tensor(te[:, :], tb_f[:, :], at_edge[:, :], ALU.subtract))
                link(v.tensor_scalar(te[:, :], te[:, :], 0.0, None, ALU.max))
                link(v.tensor_scalar(pe_pos[:, :], cnt[:, :], -1.0, None, ALU.add))
                link(v.tensor_tensor(hit[:, :, :], bc(pl.iota_free[:, :].unsqueeze(1), [P, NB, P]),
                                     bc(pe_pos[:, :].unsqueeze(2), [P, NB, P]), ALU.is_equal))
                link(v.tensor_tensor(hit[:, :, :], hit[:, :, :], found[:, :, P:2 * P], ALU.mult))
                link(v.tensor_reduce(lr_sel[:, :], hit[:, :, :], AX.X, ALU.add))
                link(v.tensor_tensor(lr_end[:, :], at_edge[:, :], found[:, :, 2 * P], ALU.mult))
                link(v.tensor_tensor(lr_end[:, :], lr_end[:, :], lr_sel[:, :], ALU.add))
                link(v.scalar_tensor_tensor(tmp[:, :], te[:, :], float(P), lr_end[:, :], ALU.mult, ALU.add))
                v.tensor_copy(pl.part_i[:, :], tmp[:, :])
                link(v.tensor_scalar(lr_sel[:, :], te[:, :], -1.0, 0.0, ALU.add, ALU.max))
                v.tensor_copy(pl.carry_i[:, :], lr_sel[:, :])
                link(v.tensor_scalar(tmp[:, :], te[:, :], float(P), None, ALU.mult))
                link(v.tensor_tensor(tmp[:, :], row_start[:, :], tmp[:, :], ALU.is_lt))
                link(v.tensor_tensor(tmp[:, :], tmp[:, :], pl.has_edges[:, :], ALU.mult))
                v.tensor_scalar(pl.carry_pen[:, :], tmp[:, :], -FAR, FAR, ALU.mult, ALU.add)
                v.wait_ge(has_prefix, 1)
                link(v.tensor_copy(n_tot[:, :], ps[7][:, 64:64 + NB]))
                link(v.tensor_tensor_scan(n_run[:, :], ones_row[:, 0:NB], n_tot[:, :], 0.0, ALU.mult, ALU.add))
                link(v.tensor_tensor(before[:, :], n_run[:, :], n_tot[:, :], ALU.subtract))
                link(v.tensor_tensor(before[:, :], before[:, :], ps[7][:, 0:NB], ALU.add))
                link(v.tensor_tensor(compact[:, :], node_id[:, :], before[:, :], ALU.subtract))
                link(v.tensor_tensor(compact[:, :], compact[:, :], bc(n_run[:, NB - 1:NB], [P, NB]), ALU.add))
                link(v.tensor_tensor(tmp[:, :], before[:, :], compact[:, :], ALU.subtract))
                link(v.tensor_tensor(tmp[:, :], tmp[:, :], pl.has_edges[:, :], ALU.mult))
                link(v.tensor_tensor(compact[:, :], compact[:, :], tmp[:, :], ALU.add))
                link(v.tensor_copy(pl.compact_i[:, :], compact[:, :]))

            @block.tensor
            def _(pe):
                def shift(bank, vals, n, done):
                    pe.matmul(ps[bank][:, 0:n], shift_m[:, :], vals[:, 0:n], start=True, stop=True)
                    pe.matmul(ps[bank][:, 64:64 + n - 1], corner_m[:, :], vals[:, 0:n - 1], start=True, stop=True
                              ).then_inc(done, 1)

                def prefix(bank, vals, n, done):
                    pe.matmul(ps[bank][:, 0:n], below_m[:, :], vals[:, 0:n], start=True, stop=True)
                    pe.matmul(ps[bank][:, 64:64 + n], ones_m[:, :], vals[:, 0:n], start=True, stop=True
                              ).then_inc(done, 1)

                pe.wait_ge(made, 13)
                pe.wait_ge(last_ready, 1)
                shift(0, dst_last1, TB, shifted)
                pe.wait_ge(last_ready, 2)
                shift(1, lr_last, TB, shifted)
                pe.wait_ge(starts_ready, 1)
                prefix(2, n_starts, TB, prefix_done)
                pe.wait_ge(rows3_ready, 1)
                pe.transpose(ps[3][0:3 * TB, 0:P], rows3[:, :], pl.ident[:, :]).then_inc(rows3_turned, 1)
                pe.wait_ge(dl_ready, 1)
                for n, tiles in enumerate((src_f, dl[:, :, P:2 * P], last_in_tile, weight)):
                    for half in range(2):
                        wait(pe, turned_used, 2 * n + half - 1)
                        lo, hi = (0, 4) if half == 0 else (4, TB)
                        for g in range(lo, hi):
                            ins = pe.transpose(ps[4 + half][:, (g - lo) * P:(g - lo + 1) * P], tiles[:, g, :],
                                               pl.ident[:, :])
                        ins.then_inc(turned, 1)
                pe.wait_ge(end_ready, 1)
                shift(6, row_end, NB, end_shifted)
                pe.wait_ge(has_ready, 1)
                prefix(7, pl.has_edges, NB, has_prefix)
        sem.close()



def edge_sweep(nc, pl, sems, kind, H, tab, q_tab, part_tab, scale, w):
    sem = Stage(nc, sems)
    TW = tab.shape[1]
    QW = q_tab.shape[1]
    C = D // H
    R = G * H
    W = D + 2 * H
    NG = pl.NG
    QB = 1 if kind == "gat" else 2
    PAIR = 2
    NP_ = G // PAIR

    with ExitStack() as ctx:
        def sb(name, shape, dt=F32):
            return sem.tensor(ctx, name, shape, dt)

        rows = [sb(f"rows{u}", [P, G, TW]) for u in range(SLOTS)]
        qwin = [sb(f"qwin{u}", [P, G, QW]) for u in range(SLOTS)]
        neg = [sb(f"neg{u}", [R, 2 * P]) for u in range(SLOTS)]
        idx = [sb(f"idx{u}", [P, G], I32) for u in range(SLOTS)]
        hot = [sb(f"hot{u}", [P, G, P]) for u in range(SLOTS)]
        hot_t = sb("hot_t", [P, G, P])
        alpha = sb("alpha", [P, G, H])
        fwd = sb("fwd", [R, P])
        seg_max = sb("seg_max", [R, P])
        diff = sb("diff", [R, P])
        prob = sb("prob", [R, P])
        pm = sb("pm", [P, 2 * R])
        msg = sb("msg", [P, G, W])
        part = [sb(f"part{u}", [P, G, W]) for u in range(SLOTS)]
        prod = [sb(f"prod{h}", [P, HALF, D]) for h in range(2)]
        if kind == "gat":
            rel = sb("rel", [P, G])
            attr = [sb(f"attr{u}", [P, G, D]) for u in range(SLOTS)]
            ang = sb("ang", [P, G, 64])
            turns = sb("turns", [P, G, 64])
            ang2 = sb("ang2", [P, G, 64])
            attr_t = [sb(f"attr_t{u}", [P, G * P]) for u in range(SLOTS)]
        if kind == "tconv":
            attr_t = [sb(f"attr_t{u}", [P, G * P]) for u in range(SLOTS)]

        hot_ps = pl.banks[0]
        q_ps = [pl.banks[1], pl.banks[2]]
        e_ps = [pl.banks[3], pl.banks[4]]
        small = pl.banks[5]
        alpha_t = small[0:R, 0:P]
        prob_ps, max_ps = small[:, P:P + R], small[:, P + R:P + 2 * R]
        part_ps = [pl.banks[6], pl.banks[7]]

        gathered = [sem.indirect(f"gathered{u}") for u in range(SLOTS)]
        q_loaded = [sem(f"q_loaded{u}") for u in range(SLOTS)]
        neg_loaded = [sem(f"neg_loaded{u}") for u in range(SLOTS)]
        part_stored = [sem(f"part_stored{u}") for u in range(SLOTS)]
        idx_ready = sem("idx_ready")
        hot_built = sem("hot_built")
        hot_turned = sem("hot_turned")
        hot_copied = sem("hot_copied")
        q_done = sem("q_done")
        q_used = sem("q_used")
        alpha_done = sem("alpha_done")
        alpha_turned = sem("alpha_turned")
        fwd_done, max_done, diff_done = sem("fwd_done"), sem("max_done"), sem("diff_done")
        exp_done = sem("exp_done")
        prob_turned = sem("prob_turned")
        msg_done = sem("msg_done")
        prob_copied = sem("prob_copied")
        part_done = sem("part_done")
        part_copied = sem("part_copied")
        pool_passed, pe_passed = sem("pool_passed"), sem("pe_passed")
        step = sem("score_step")
        STEPS = {"gat": 7, "gatv2": 4}.get(kind, 0)
        if kind == "gat":
            attr_loaded = [sem(f"attr_loaded{u}") for u in range(SLOTS)]
            attr_stored = [sem(f"attr_stored{u}") for u in range(SLOTS)]
            angle_done = sem("angle_done")
            cos_done = sem("cos_done")
            attr_turned = sem("attr_turned")
            attr_copied = sem("attr_copied")
            tail_zeroed = sem("tail_zeroed")
        if kind == "tconv":
            attr_loaded = [sem(f"attr_loaded{u}") for u in range(SLOTS)]
            e_used = sem("e_used")
        ring = [(3 * j + u, j, u) for j in range((NG + 2) // 3) for u in range(3)][:NG]
        FIRST, LAST = 3, (NG - 3) // 3 * 3

        def groups(eng, body, tail=None):
            for i, k, u in ring[:FIRST]:
                body(i, k, u, i)
            with eng.Fori(1, LAST // 3) as j:
                for u in range(3):
                    body(j * 3 + u, j, u, FIRST + u)
            for i, k, u in ring[LAST:]:
                body(i, k, u, i)
            if tail is not None:
                tail()

        def ahead(i, k, u, d):
            return i + d, k + (u + d) // 3, (u + d) % 3

        def has(n, d):
            return 0 <= n + d < NG

        with nc.Block() as block:
            @block.sync
            def _(sp):
                def load(i, k, u, n):
                    wait(sp, q_done, (i - 2) * QB if n >= 3 else 0)
                    for t in range(G):
                        first = sp.value_load(pl.window_i[0:1, bass.ds(i * G + t, 1)], min_val=0, max_val=pl.NP)
                        sp.dma_start(qwin[u][:, t, :], q_tab[bass.ds(first, P), :]).then_inc(q_loaded[u], 16)
                    if n >= 3:
                        wait(sp, max_done, i - 2)
                    sp.dma_start(neg[u][:, :], pl.neg_tab[H][bass.ds(i * R, R), :]).then_inc(neg_loaded[u], 16)
                    if kind == "tconv":
                        sp.dma_start(attr_t[u][:, :], pl.attr_tab[bass.ds(i * P, P), :]).then_inc(attr_loaded[u], 16)
                    if kind == "gat":
                        load_attr(i, k, u, n)

                def load_attr(i, k, u, n):
                    if n >= 3:
                        wait(sp, attr_turned, 2 * (i - 2))
                    edges = pl.E - (NG - 1) * G * P
                    if n < NG - 1:
                        src_ap = pl.edge_attr[bass.ds(i * (G * P), G * P), :].rearrange("(t p) c -> p t c", p=P)
                        sp.dma_start(attr[u][:, :, 64:D], src_ap).then_inc(attr_loaded[u], 16)
                    else:
                        sp.wait_ge(tail_zeroed, 1)
                        base, full = (NG - 1) * G * P, edges // P
                        if full:
                            sp.dma_start(attr[u][:, 0:full, 64:D],
                                         pl.edge_attr[base:base + full * P, :].rearrange("(t p) c -> p t c", p=P)
                                         ).then_inc(attr_loaded[u], 16)
                        if edges > full * P:
                            sp.dma_start(attr[u][0:edges - full * P, full, 64:D],
                                         pl.edge_attr[base + full * P:pl.E, :]).then_inc(attr_loaded[u], 16)

                def store(i, k, u, n):
                    wait(sp, part_copied, (i + 1) * NP_)
                    out = part_tab[bass.ds(i * (G * P), G * P), :].rearrange("(t p) w -> p t w", p=P)
                    sp.dma_start(out, part[u][:, :, :]).then_inc(part_stored[u], 16)

                def body(i, k, u, n):
                    if has(n, 2):
                        load(*ahead(i, k, u, 2), n + 2)
                    if kind == "gat":
                        wait(sp, attr_copied, 2 * (i + 1))
                        sp.dma_start(pl.attr_tab[bass.ds(i * P, P), :], attr_t[u][:, :]).then_inc(attr_stored[u], 16)
                    if has(n, -1):
                        store(*ahead(i, k, u, -1), n - 1)

                load(0, 0, 0, 0)
                load(1, 0, 1, 1)
                groups(sp, body, lambda: store(*ring[NG - 1], NG - 1))
                for u in range(SLOTS):
                    turns_of = len([r for r in ring if r[2] == u])
                    sp.wait_ge(part_stored[u], 16 * turns_of)
                    if kind == "gat":
                        sp.wait_ge(attr_stored[u], 16 * turns_of)

            @block.gpsimd
            def _(pool):
                def gather(i, k, u, n):
                    if n >= 3:
                        wait(pool, msg_done, 3 * (i - 2))
                    wait(pool, idx_ready, i + 1)
                    settle(pool, pool_passed)
                    for t in range(G):
                        pool.indirect_dma_start(out=rows[u][:, t, :], out_offset=None, in_=tab,
                                                in_offset=bass.IndirectOffsetOnAxis(ap=idx[u][:, t:t + 1], axis=0)
                                                ).then_inc(gathered[u], 16)

                def body(i, k, u, n):
                    if has(n, 2):
                        gather(*ahead(i, k, u, 2), n + 2)

                gather(0, 0, 0, 0)
                gather(1, 0, 1, 1)
                groups(pool, body)

            @block.scalar
            def _(act):
                def indices(i, k, u, n):
                    if n >= 3:
                        wait(act, gathered[u], 16 * G * k)
                    act.activation(idx[u][:, :], pl.src_col[:, bass.ds(i * G, G)], ACT.Copy).then_inc(idx_ready, 1)

                def copy_hot(i, k, u, n):
                    for h in range(2):
                        wait(act, hot_turned, 2 * i + h + 1)
                        act.activation(hot_t[:, h * HALF:(h + 1) * HALF, :],
                                       hot_ps[:, :].rearrange("p (t e) -> p t e", t=HALF), ACT.Copy
                                       ).then_inc(hot_copied, 1)

                def exps(i, k, u, n):
                    wait(act, diff_done, i + 1)
                    if n >= 1:
                        wait(act, prob_turned, i)
                    act.activation(prob[:, :], diff[:, :], ACT.Exp, scale=scale).then_inc(exp_done, 1)

                def sums(i, k, u, n):
                    wait(act, prob_turned, i + 1)
                    if n >= 1:
                        wait(act, msg_done, 3 * i)
                    act.activation(pm[:, :], small[:, P:P + 2 * R], ACT.Copy).then_inc(prob_copied, 1)
                    if n >= 3:
                        wait(act, part_stored[u], 16 * k)
                    for c in range(NP_):
                        wait(act, part_done, NP_ * i + c + 1)
                        act.activation(part[u][:, PAIR * c:PAIR * (c + 1), :],
                                       part_ps[c % 2][:, 0:PAIR * W].rearrange("p (t w) -> p t w", t=PAIR), ACT.Copy
                                       ).then_inc(part_copied, 1)

                def features(i, k, u, n):
                    wait(act, angle_done, i + 1)
                    if n >= 3:
                        wait(act, attr_turned, 2 * (i - 2))
                    act.activation(attr[u][:, :, 0:64], ang2[:, :, :], ACT.Sin, bias=pl.half_pi[:, 0:1]
                                   ).then_inc(cos_done, 1)
                    if n >= 3:
                        wait(act, attr_stored[u], 16 * k)
                    for h in range(2):
                        wait(act, attr_turned, 2 * i + h + 1)
                        act.activation(attr_t[u][:, h * HALF * P:(h + 1) * HALF * P], e_ps[h][:, :], ACT.Copy
                                       ).then_inc(attr_copied, 1)

                def body(i, k, u, n):
                    if has(n, 2):
                        indices(*ahead(i, k, u, 2), n + 2)
                    if has(n, -1):
                        exps(*ahead(i, k, u, -1), n - 1)
                    if has(n, 1):
                        copy_hot(*ahead(i, k, u, 1), n + 1)
                    if has(n, -1):
                        sums(*ahead(i, k, u, -1), n - 1)
                    if kind == "gat":
                        features(i, k, u, n)

                def tail():
                    exps(*ring[NG - 1], NG - 1)
                    sums(*ring[NG - 1], NG - 1)

                indices(0, 0, 0, 0)
                indices(1, 0, 1, 1)
                copy_hot(0, 0, 0, 0)
                groups(act, body, tail)

            @block.tensor
            def _(pe):
                def turn_hot(i, k, u, n):
                    for h in range(2):
                        wait(pe, hot_built, 2 * i + h + 1)
                        wait(pe, hot_copied, 2 * i + h)
                        for t in range(HALF):
                            ins = pe.transpose(hot_ps[:, t * P:(t + 1) * P], hot[u][:, h * HALF + t, :], pl.ident[:, :])
                        ins.then_inc(hot_turned, 1)

                def queries(i, k, u, n):
                    wait(pe, hot_copied, 2 * i + 2)
                    wait(pe, q_loaded[u], 16 * G * (k + 1))
                    if kind == "tconv":
                        wait(pe, attr_loaded[u], 16 * (k + 1))
                    per = G // QB
                    for h in range(QB):
                        if n >= 1:
                            wait(pe, q_used, QB * (i - 1) + h + 1)
                        if kind == "tconv":
                            if n >= 1:
                                wait(pe, e_used, 2 * (i - 1) + h + 1)
                            for t in range(h * per, (h + 1) * per):
                                pe.matmul(e_ps[h][:, (t - h * per) * D:(t - h * per + 1) * D],
                                          attr_t[u][:, t * P:(t + 1) * P], w["We"][:, :], start=True, stop=True)
                        for t in range(h * per, (h + 1) * per):
                            ins = pe.matmul(q_ps[h][:, (t - h * per) * QW:(t - h * per + 1) * QW], hot_t[:, t, :],
                                            qwin[u][:, t, :], start=True, stop=True)
                        ins.then_inc(q_done, 1)

                def turn_probs(i, k, u, n):
                    wait(pe, exp_done, i + 1)
                    settle(pe, pe_passed)
                    pe.transpose(max_ps, seg_max[:, :], pl.ident[0:R, 0:R])
                    pe.transpose(prob_ps, prob[:, :], pl.ident[0:R, 0:R]).then_inc(prob_turned, 1)

                def turn_alpha(i, k, u, n):
                    wait(pe, alpha_done, QB * (i + 1))
                    if n >= 1:
                        wait(pe, prob_copied, i)
                    settle(pe, pe_passed)
                    pe.transpose(alpha_t, alpha[:, :, :].rearrange("p t h -> p (t h)"), pl.ident[:, :]
                                 ).then_inc(alpha_turned, 1)

                def sum_parts(i, k, u, n):
                    wait(pe, msg_done, 3 * (i + 1))
                    for c in range(NP_):
                        if n >= 1 or c >= 2:
                            wait(pe, part_copied, NP_ * i + c - 1)
                        for t in range(PAIR):
                            ins = pe.matmul(part_ps[c % 2][:, t * W:(t + 1) * W], hot[u][:, PAIR * c + t, :],
                                            msg[:, PAIR * c + t, :], start=True, stop=True)
                        ins.then_inc(part_done, 1)

                def turn_attr(i, k, u, n):
                    wait(pe, cos_done, i + 1)
                    if n < NG - 1:
                        wait(pe, attr_loaded[u], 16 * (k + 1))
                    else:
                        wait(pe, attr_loaded[u], 16 * (k + 2))
                    for h in range(2):
                        if n >= 1:
                            wait(pe, attr_copied, 2 * (i - 1) + h + 1)
                        for t in range(HALF):
                            ins = pe.transpose(e_ps[h][:, t * P:(t + 1) * P], attr[u][:, h * HALF + t, :],
                                               pl.ident[:, :])
                        ins.then_inc(attr_turned, 1)

                def body(i, k, u, n):
                    queries(i, k, u, n)
                    if has(n, 1):
                        turn_hot(*ahead(i, k, u, 1), n + 1)
                    if has(n, -1):
                        turn_probs(*ahead(i, k, u, -1), n - 1)
                    turn_alpha(i, k, u, n)
                    if has(n, -1):
                        sum_parts(*ahead(i, k, u, -1), n - 1)
                    if kind == "gat":
                        turn_attr(i, k, u, n)

                def tail():
                    turn_probs(*ring[NG - 1], NG - 1)
                    sum_parts(*ring[NG - 1], NG - 1)

                turn_hot(0, 0, 0, 0)
                groups(pe, body, tail)

            @block.vector
            def _(v):
                def build_hot(i, k, u, n):
                    if n >= 3:
                        wait(v, part_done, NP_ * (i - 2))
                    for h in range(2):
                        v.tensor_tensor(hot[u][:, h * HALF:(h + 1) * HALF, :],
                                        bc(pl.iota_free[:, :].unsqueeze(1), [P, HALF, P]),
                                        bc(pl.rank_col[:, bass.ds(i * G + h * HALF, HALF)].unsqueeze(2), [P, HALF, P]),
                                        ALU.is_equal).then_inc(hot_built, 1)

                def maxima(i, k, u, n):
                    wait(v, alpha_turned, i + 1)
                    wait(v, neg_loaded[u], 16 * (k + 1))
                    v.tensor_tensor_scan(fwd[:, :], neg[u][:, 0:P], alpha_t, 0.0, ALU.add, ALU.max).then_inc(fwd_done, 1)
                    wait(v, fwd_done, i + 1)
                    if n >= 1:
                        wait(v, prob_turned, i)
                    v.tensor_tensor_scan(seg_max[:, ::-1], neg[u][:, 2 * P - 1:P - 1:-1], fwd[:, ::-1], 0.0,
                                         ALU.add, ALU.max).then_inc(max_done, 1)
                    wait(v, max_done, i + 1)
                    if n >= 1:
                        wait(v, exp_done, i)
                    v.tensor_tensor(diff[:, :], alpha_t, seg_max[:, :], ALU.subtract).then_inc(diff_done, 1)

                def scores(i, k, u, n):
                    at = [0]

                    def then(ins):
                        at[0] += 1
                        ins.then_inc(step, 1)
                        wait(v, step, i * STEPS + at[0])

                    wait(v, gathered[u], 16 * G * (k + 1))
                    if n >= 1:
                        wait(v, alpha_turned, i)
                    if kind == "gat":
                        wait(v, q_done, i + 1)
                        s = prod[0][:, 0, 0:G * H].rearrange("p (t h) -> p t h", h=H)
                        v.tensor_tensor(s, q_ps[0][:, 0:G * H].rearrange("p (t h) -> p t h", h=H),
                                        rows[u][:, :, D:D + H], ALU.add).then_inc(q_used, 1)
                        v.wait_ge(q_used, i + 1)
                        v.scalar_tensor_tensor(alpha[:, :, :], s, 0.01, s, ALU.mult, ALU.max).then_inc(alpha_done, 1)
                        return
                    for h in range(2):
                        wait(v, q_done, 2 * i + h + 1)
                        t0, t1 = h * HALF, (h + 1) * HALF
                        q = q_ps[h][:, :].rearrange("p (t d) -> p t d", t=HALF)
                        if kind == "tconv":
                            e = e_ps[h][:, :].rearrange("p (t d) -> p t d", t=HALF)
                            kv = rows[u][:, t0:t1, :].rearrange("p t (a d) -> p t a d", a=2)
                            v.tensor_tensor(kv, kv, bc(e.unsqueeze(2), [P, HALF, 2, D]), ALU.add).then_inc(e_used, 1)
                            v.wait_ge(e_used, 2 * i + h + 1)
                            v.tensor_tensor(prod[h][:, :, :], q, rows[u][:, t0:t1, 0:D], ALU.mult).then_inc(q_used, 1)
                            v.wait_ge(q_used, 2 * i + h + 1)
                        elif kind == "mha":
                            v.tensor_tensor(prod[h][:, :, :], q, rows[u][:, t0:t1, 0:D], ALU.mult).then_inc(q_used, 1)
                            v.wait_ge(q_used, 2 * i + h + 1)
                        else:
                            v.tensor_tensor(prod[h][:, :, :], q, rows[u][:, t0:t1, :], ALU.add).then_inc(q_used, 1)
                            v.wait_ge(q_used, 2 * i + h + 1)
                            flat = prod[h][:, :, :].rearrange("p t d -> p (t d)")
                            then(v.scalar_tensor_tensor(flat, flat, 0.2, flat, ALU.mult, ALU.max))
                            then(v.tensor_tensor(prod[h][:, :, :], prod[h][:, :, :],
                                                 bc(w["att"][:, :].unsqueeze(1), [P, HALF, D]), ALU.mult))
                        v.tensor_reduce(alpha[:, t0:t1, :], prod[h][:, :, :].rearrange("p t (h c) -> p t h c", c=C),
                                        AX.X, ALU.add).then_inc(alpha_done, 1)

                def angles(i, k, u, n):
                    at = [0]

                    def then(ins):
                        at[0] += 1
                        ins.then_inc(step, 1)
                        wait(v, step, i * STEPS + at[0])

                    then(v.tensor_tensor(rel[:, :], rows[u][:, :, D + H], pl.weight_col[:, bass.ds(i * G, G)], ALU.subtract))
                    then(v.tensor_tensor(ang[:, :, :], bc(rel[:, :].unsqueeze(2), [P, G, 64]),
                                         bc(w["Wt"][:, :].unsqueeze(1), [P, G, 64]), ALU.mult))
                    then(v.tensor_tensor(ang[:, :, :], ang[:, :, :], bc(w["bt"][:, :].unsqueeze(1), [P, G, 64]), ALU.add))
                    then(v.tensor_scalar(turns[:, :, :], ang[:, :, :], float(1 / (2 * np.pi)), MAGIC, ALU.mult, ALU.add))
                    then(v.tensor_scalar(turns[:, :, :], turns[:, :, :], MAGIC, None, ALU.subtract))
                    fl = "p t c -> p (t c)"
                    a, tn = ang[:, :, :].rearrange(fl), turns[:, :, :].rearrange(fl)
                    then(v.scalar_tensor_tensor(a, tn, -TWO_PI_HIGH, a, ALU.mult, ALU.add))
                    then(v.scalar_tensor_tensor(a, tn, -TWO_PI_LOW, a, ALU.mult, ALU.add))
                    if n >= 1:
                        wait(v, cos_done, i)
                    v.scalar_tensor_tensor(ang2[:, :, :].rearrange(fl), a, -1.0, a, ALU.mult, ALU.min
                                           ).then_inc(angle_done, 1)

                def messages(i, k, u, n):
                    wait(v, prob_copied, i + 1)
                    if n >= 1:
                        wait(v, part_done, NP_ * i)
                    vals = rows[u][:, :, TW - D:TW] if kind in ("tconv", "mha") else rows[u][:, :, 0:D]
                    p = pm[:, 0:R].rearrange("p (t h) -> p t h", h=H)
                    v.tensor_copy(msg[:, :, D:D + H], p).then_inc(msg_done, 1)
                    v.tensor_tensor(msg[:, :, 0:D].rearrange("p t (h c) -> p t h c", c=C),
                                    vals.rearrange("p t (h c) -> p t h c", c=C),
                                    bc(p.unsqueeze(3), [P, G, H, C]), ALU.mult).then_inc(msg_done, 1)
                    v.tensor_tensor(msg[:, :, D + H:W], pm[:, R:2 * R].rearrange("p (t h) -> p t h", h=H),
                                    bc(pl.last_col[:, bass.ds(i * G, G)].unsqueeze(2), [P, G, H]), ALU.mult
                                    ).then_inc(msg_done, 1)

                def body(i, k, u, n):
                    if has(n, 1):
                        build_hot(*ahead(i, k, u, 1), n + 1)
                    if has(n, -1):
                        maxima(*ahead(i, k, u, -1), n - 1)
                    scores(i, k, u, n)
                    if kind == "gat":
                        angles(i, k, u, n)
                        if n == NG - 3:
                            v.wait_ge(attr_turned, 2 * (NG - 3))
                            v.memset(attr[(NG - 1) % 3][:, :, 64:D], 0.0).then_inc(tail_zeroed, 1)
                    if has(n, -1):
                        messages(*ahead(i, k, u, -1), n - 1)

                def tail():
                    maxima(*ring[NG - 1], NG - 1)
                    messages(*ring[NG - 1], NG - 1)

                build_hot(0, 0, 0, 0)
                groups(v, body, tail)
        sem.close()



def merge_parts(nc, pl, sems, H, scale, att):
    sem = Stage(nc, sems)
    TB, NB = pl.TB, pl.NB
    W = D + 2 * H
    C = D // H
    NT = TB * P
    HALVES = ((0, 4), (4, TB))
    head = pl.head8 if H == 8 else pl.head4
    part_tab, carry_tab = pl.part_tab[H], pl.carry_tab[H]
    with ExitStack() as ctx:
        def sb(name, shape, dt=F32):
            return sem.tensor(ctx, name, shape, dt)

        last_rows = sb("last_rows", [P, TB, W])
        num, num_run = sb("num", [P, NT]), sb("num_run", [P, NT])
        den, den_run = sb("den", [H, NT]), sb("den_run", [H, NT])
        top = sb("top", [H, NT])
        top_run = sb("top_run", [H, 1 + NT])
        keep, take = sb("keep", [H, NT]), sb("take", [H, NT])
        keep_e, take_e = sb("keep_e", [H, NT]), sb("take_e", [H, NT])
        carry = sb("carry", [P, TB, W])
        own = sb("own", [P, NB, W])
        run = sb("run", [P, NB, W])
        m_run, m_all = sb("m_run", [P, NB, H]), sb("m_all", [P, NB, H])
        d_own, d_run = sb("d_own", [P, NB, H]), sb("d_run", [P, NB, H])
        f_own, f_run = sb("f_own", [P, NB, H]), sb("f_run", [P, NB, H])
        s_own, s_run = sb("s_own", [P, NB, H]), sb("s_run", [P, NB, H])
        last_got, own_got, run_got = sem.indirect("last_gathered"), sem.indirect("own_gathered"), sem.indirect("run_gathered")
        turned, copied = sem("turned"), sem("copied")
        args_ready, exps_ready, spread = sem("args_ready"), sem("exps_ready"), sem("spread")
        carried, back, back_copied, stored = sem("carried"), sem("back"), sem("back_copied"), sem("carry_stored")
        node_args, node_exps = sem("node_args"), sem("node_exps")
        dve = sem("dve")
        ps = pl.banks

        with nc.Block() as block:
            @block.gpsimd
            def _(pool):
                for g in range(TB):
                    pool.indirect_dma_start(out=last_rows[:, g, :], out_offset=None, in_=part_tab,
                                            in_offset=bass.IndirectOffsetOnAxis(ap=pl.tile_last_i[:, g:g + 1], axis=0)
                                            ).then_inc(last_got, 16)
                for b in range(NB):
                    pool.indirect_dma_start(out=own[:, b, :], out_offset=None, in_=part_tab,
                                            in_offset=bass.IndirectOffsetOnAxis(ap=pl.part_i[:, b:b + 1], axis=0)
                                            ).then_inc(own_got, 16)
                pool.wait_ge(stored, 16)
                for b in range(NB):
                    pool.indirect_dma_start(out=run[:, b, :], out_offset=None, in_=carry_tab,
                                            in_offset=bass.IndirectOffsetOnAxis(ap=pl.carry_i[:, b:b + 1], axis=0)
                                            ).then_inc(run_got, 16)

            @block.sync
            def _(sp):
                sp.wait_ge(back_copied, 2 + 2 * TB)
                sp.dma_start(carry_tab.rearrange("(g p) w -> p g w", p=P), carry[:, :, :]).then_inc(stored, 16)
                sp.wait_ge(stored, 16)

            @block.tensor
            def _(pe):
                pe.wait_ge(last_got, 16 * TB)
                for lo, hi, rows, bank in ((0, D, P, 0), (D, D + H, H, 2), (D + H, W, H, 4)):
                    for half, (a, b) in enumerate(HALVES):
                        for g in range(a, b):
                            ins = pe.transpose(ps[bank + half][0:rows, (g - a) * P:(g - a + 1) * P],
                                               last_rows[:, g, lo:hi], pl.ident[:, :])
                        ins.then_inc(turned, 1)
                pe.wait_ge(exps_ready, 2)
                pe.wait_ge(copied, 6)
                for f, bank in ((keep_e, 0), (take_e, 2)):
                    for half, (a, b) in enumerate(HALVES):
                        pe.matmul(ps[bank + half][:, 0:(b - a) * P], head[0:H, :], f[:, a * P:b * P], start=True, stop=True
                                  ).then_inc(spread, 1)
                pe.wait_ge(carried, 2)
                for half, (a, b) in enumerate(HALVES):
                    for g in range(a, b):
                        ins = pe.transpose(ps[4 + half][:, (g - a) * P:(g - a + 1) * P], num_run[:, g * P:(g + 1) * P],
                                           pl.ident[:, :])
                    ins.then_inc(back, 1)
                for g in range(TB):
                    pe.transpose(ps[6][:, 2 * g * H:(2 * g + 1) * H], den_run[:, g * P:(g + 1) * P], pl.ident[0:H, 0:H])
                    ins = pe.transpose(ps[6][:, (2 * g + 1) * H:(2 * g + 2) * H], top_run[:, 1 + g * P:1 + (g + 1) * P],
                                       pl.ident[0:H, 0:H])
                ins.then_inc(back, 1)

            @block.scalar
            def _(act):
                n = 0
                for out, rows, bank in ((num, P, 0), (den, H, 2), (top, H, 4)):
                    for half, (a, b) in enumerate(HALVES):
                        n += 1
                        act.wait_ge(turned, n)
                        act.activation(out[:, a * P:b * P], ps[bank + half][0:rows, 0:(b - a) * P], ACT.Copy
                                       ).then_inc(copied, 1)
                act.wait_ge(args_ready, 1)
                act.activation(keep_e[:, :], keep[:, :], ACT.Exp, scale=scale).then_inc(exps_ready, 1)
                act.activation(take_e[:, :], take[:, :], ACT.Exp, scale=scale).then_inc(exps_ready, 1)
                for half, (a, b) in enumerate(HALVES):
                    act.wait_ge(back, half + 1)
                    act.activation(carry[:, a:b, 0:D], ps[4 + half][:, 0:(b - a) * P].rearrange("p (g d) -> p g d", d=D),
                                   ACT.Copy).then_inc(back_copied, 1)
                act.wait_ge(back, 3)
                for g in range(TB):
                    for k in range(2):
                        act.activation(carry[:, g, D + k * H:D + (k + 1) * H], ps[6][:, (2 * g + k) * H:(2 * g + k + 1) * H],
                                       ACT.Copy).then_inc(back_copied, 1)
                act.wait_ge(node_args, 1)
                act.activation(f_own[:, :, :], d_own[:, :, :], ACT.Exp, scale=scale).then_inc(node_exps, 1)
                act.activation(f_run[:, :, :], d_run[:, :, :], ACT.Exp, scale=scale).then_inc(node_exps, 1)

            @block.vector
            def _(v):
                link = chain(v, dve)
                link(v.memset(top_run[:, 0:1], 0.0))
                v.wait_ge(copied, 6)
                link(v.tensor_tensor_scan(top_run[:, 1:1 + NT], pl.whole_pen[0:H, :], top[:, :], 0.0, ALU.add, ALU.max))
                link(v.tensor_tensor(keep[:, :], top_run[:, 0:NT], pl.whole_pen[0:H, :], ALU.add))
                link(v.tensor_tensor(keep[:, :], keep[:, :], top_run[:, 1:1 + NT], ALU.subtract))
                v.tensor_tensor(take[:, :], top[:, :], top_run[:, 1:1 + NT], ALU.subtract).then_inc(args_ready, 1)
                v.wait_ge(exps_ready, 2)
                link(v.tensor_tensor(den[:, :], den[:, :], take_e[:, :], ALU.mult))
                v.tensor_tensor_scan(den_run[:, :], keep_e[:, :], den[:, :], 0.0, ALU.mult, ALU.add).then_inc(carried, 1)
                v.wait_ge(spread, 4)
                for half, (a, b) in enumerate(HALVES):
                    link(v.tensor_tensor(num[:, a * P:b * P], num[:, a * P:b * P], ps[2 + half][:, 0:(b - a) * P], ALU.mult))
                a = HALVES[0][1] * P
                link(v.tensor_tensor_scan(num_run[:, 0:a], ps[0][:, 0:a], num[:, 0:a], 0.0, ALU.mult, ALU.add))
                v.tensor_tensor_scan(num_run[:, a:NT], ps[1][:, 0:NT - a], num[:, a:NT], num_run[:, a - 1:a],
                                     ALU.mult, ALU.add).then_inc(carried, 1)
                v.wait_ge(own_got, 16 * NB)
                v.wait_ge(run_got, 16 * NB)
                link(v.tensor_tensor(m_run[:, :, :], run[:, :, D + H:W],
                                     bc(pl.carry_pen[:, :].unsqueeze(2), [P, NB, H]), ALU.add))
                link(v.tensor_tensor(m_all[:, :, :], own[:, :, D + H:W], m_run[:, :, :], ALU.max))
                v.tensor_tensor(d_own[:, :, :], own[:, :, D + H:W], m_all[:, :, :], ALU.subtract)
                v.tensor_tensor(d_run[:, :, :], m_run[:, :, :], m_all[:, :, :], ALU.subtract).then_inc(node_args, 1)
                v.wait_ge(node_exps, 2)
                v.tensor_tensor(s_own[:, :, :], own[:, :, D:D + H], f_own[:, :, :], ALU.mult)
                link(v.tensor_tensor(s_run[:, :, :], run[:, :, D:D + H], f_run[:, :, :], ALU.mult))
                link(v.tensor_tensor(s_own[:, :, :], s_own[:, :, :], s_run[:, :, :], ALU.add))
                link(v.tensor_scalar(s_own[:, :, :], s_own[:, :, :], TINY, None, ALU.max))
                link(v.reciprocal(s_run[:, :, :], s_own[:, :, :]))
                link(v.tensor_tensor(s_run[:, :, :], s_run[:, :, :],
                                     bc(pl.has_edges[:, :].unsqueeze(2), [P, NB, H]), ALU.mult))
                v.tensor_tensor(f_own[:, :, :], f_own[:, :, :], s_run[:, :, :], ALU.mult)
                link(v.tensor_tensor(f_run[:, :, :], f_run[:, :, :], s_run[:, :, :], ALU.mult))
                for b in range(NB):
                    o = att[:, b, :].rearrange("p (h c) -> p h c", c=C)
                    r = run[:, b, 0:D].rearrange("p (h c) -> p h c", c=C)
                    v.tensor_tensor(o, own[:, b, 0:D].rearrange("p (h c) -> p h c", c=C),
                                    bc(f_own[:, b, :].unsqueeze(2), [P, H, C]), ALU.mult)
                    ins = v.tensor_tensor(r, r, bc(f_run[:, b, :].unsqueeze(2), [P, H, C]), ALU.mult)
                link(ins)
                link(v.tensor_tensor(att[:, :, :], att[:, :, :], run[:, :, 0:D], ALU.add))
        sem.close()



class Norm:

    def __init__(self, nc, ctx, pl, sem):
        def sb(name, shape):
            return sem.tensor(ctx, "ln_" + name, shape, F32)

        self.pl = pl
        self.square = sb("square", [P, pl.NB, D])
        self.mean, self.var, self.std = sb("mean", [P, pl.NB]), sb("var", [P, pl.NB]), sb("std", [P, pl.NB])
        self.var_ready, self.std_ready = sem("var_ready"), sem("std_ready")
        self.count = 0

    def roots(self, act, n):
        for k in range(n):
            act.wait_ge(self.var_ready, k + 1)
            act.activation(self.std[:, :], self.var[:, :], ACT.Sqrt, bias=self.pl.eps[:, 0:1], scale=1.0 / D
                           ).then_inc(self.std_ready, 1)

    def apply(self, v, link, out, x):
        shape = [P, self.pl.NB, D]
        link(v.tensor_reduce(self.mean[:, :], x, AX.X, ALU.add))
        link(v.tensor_scalar(self.mean[:, :], self.mean[:, :], 1.0 / D, None, ALU.mult))
        link(v.tensor_tensor(out, x, bc(self.mean[:, :].unsqueeze(2), shape), ALU.subtract))
        link(v.tensor_tensor(self.square[:, :, :], out, out, ALU.mult))
        v.tensor_reduce(self.var[:, :], self.square[:, :, :], AX.X, ALU.add).then_inc(self.var_ready, 1)
        self.count += 1
        v.wait_ge(self.std_ready, self.count)
        link(v.reciprocal(self.std[:, :], self.std[:, :]))
        link(v.tensor_tensor(out, out, bc(self.std[:, :].unsqueeze(2), shape), ALU.mult))


def norm_input(nc, pl, sems):
    sem = Stage(nc, sems)
    with ExitStack() as ctx:
        norm = Norm(nc, ctx, pl, sem)
        dve = sem("dve")
        with nc.Block() as block:
            @block.scalar
            def _(act):
                norm.roots(act, 1)

            @block.vector
            def _(v):
                link = chain(v, dve)
                norm.apply(v, link, pl.hn[:, :, :], pl.x_sb[:, :, :])
                link(v.tensor_scalar(pl.hn[:, :, :], pl.hn[:, :, :], 0.0, None, ALU.max))
        sem.close()


def project(nc, pl, sems, weights, biases, dest, gat=None):
    sem = Stage(nc, sems)
    NB = pl.NB
    n_out = len(weights)
    cols = [d for d in dest if d in ("k", "v", "xl", "z")]
    TW = D + 16 if gat else D * len(cols)
    table = pl.gat_tab if gat else (pl.kv_tab if len(cols) == 2 else pl.xl_tab)
    with ExitStack() as ctx:
        def sb(name, shape, dt=F32):
            return sem.tensor(ctx, name, shape, dt)

        wcat = sb("wcat", [P, n_out * D])
        flag = sb("flag", [P, 1])
        bias = sb("bias", [P, n_out * D])
        hb = [sb(f"hb{u}", [P, P]) for u in range(2)]
        ht = [sb(f"ht{u}", [P, P]) for u in range(2)]
        q_rows = sb("q_rows", [P, NB, 8 if gat else D])
        t_rows = sb("t_rows", [P, NB, TW])
        if gat:
            a_l, a_r, prod = sb("a_l", [P, D]), sb("a_r", [P, D]), sb("prod", [P, NB, D])
        loaded, stored, scattered = sem("loaded"), sem("stored"), sem.indirect("scattered")
        block_ready = [sem(f"block_ready{u}") for u in range(2)]
        turned = [sem(f"turned{u}") for u in range(2)]
        turned_copied = [sem(f"turned_copied{u}") for u in range(2)]
        multiplied = [sem(f"multiplied{u}") for u in range(2)]
        written = [sem(f"written{u}") for u in range(2)]
        dve, tables_ready = sem("dve"), sem("tables_ready")
        n_loads = n_out + sum(b is not None for b in biases) + (2 if gat else 0)
        place = {"q": (q_rows, 0), "res": (pl.res, 0), "k": (t_rows, 0), "xl": (t_rows, 0), "z": (t_rows, 0), "v": (t_rows, D)}

        def target(d, b):
            t, lo = place[d]
            return t[:, bass.ds(b, 1), lo:lo + D].rearrange("p a d -> p (a d)")

        with nc.Block() as block:
            @block.sync
            def _(sp):
                for n, wt in enumerate(weights):
                    out = wcat[:, n * D:(n + 1) * D]
                    if len(wt.shape) == 3:
                        out = out.rearrange("d (h k) -> d h k", h=wt.shape[0])
                        wt = wt.rearrange("h d k -> d h k")
                    sp.dma_start(out, wt).then_inc(loaded, 16)
                for n, b in enumerate(biases):
                    if b is not None:
                        sp.dma_start(bias[:, n * D:(n + 1) * D], b.partition_broadcast(P)).then_inc(loaded, 16)
                if gat:
                    for t, a in ((a_l, gat[0]), (a_r, gat[1])):
                        sp.dma_start(t[:, :], a.rearrange("h k -> (h k)").partition_broadcast(P)).then_inc(loaded, 16)
                sp.wait_ge(tables_ready, 1)
                sp.dma_start(table.rearrange("(b p) w -> p b w", p=P), t_rows[:, :, :]).then_inc(stored, 16)
                sp.wait_ge(stored, 16)

            @block.gpsimd
            def _(pool):
                pool.wait_ge(tables_ready, 1)
                q_tab = pl.er_tab if gat else pl.q_tab
                for b in range(NB):
                    pool.indirect_dma_start(out=q_tab, out_offset=bass.IndirectOffsetOnAxis(
                        ap=pl.compact_i[:, b:b + 1], axis=0), in_=q_rows[:, b, :], in_offset=None).then_inc(scattered, 16)
                pool.wait_ge(scattered, 16 * NB)

            @block.scalar
            def _(act):
                def pair(j):
                    for u in range(2):
                        wait(act, turned[u], j)
                        act.activation(hb[u][:, :], pl.hn[:, bass.ds(j * 2 + u, 1), :].rearrange("p a d -> p (a d)"),
                                       ACT.Copy).then_inc(block_ready[u], 1)
                    for u in range(2):
                        wait(act, turned[u], j + 1)
                        wait(act, multiplied[u], j)
                        act.activation(ht[u][:, :], pl.banks[u][:, 0:P], ACT.Copy).then_inc(turned_copied[u], 1)

                pairs(act, pair, NB // 2)

            @block.tensor
            def _(pe):
                pe.wait_ge(loaded, 16 * n_loads)
                def pair(j):
                    for u in range(2):
                        wait(pe, block_ready[u], j + 1)
                        wait(pe, turned_copied[u], j)
                        pe.transpose(pl.banks[u][:, 0:P], hb[u][:, :], pl.ident[:, :]).then_inc(turned[u], 1)
                    for u in range(2):
                        wait(pe, turned_copied[u], j + 1)
                        wait(pe, written[u], j * n_out)
                        pe.matmul(pl.banks[2 + u][:, 0:n_out * D], ht[u][:, :], wcat[:, :], start=True, stop=True
                                  ).then_inc(multiplied[u], 1)

                pairs(pe, pair, NB // 2)

            @block.vector
            def _(v):
                link = chain(v, dve)
                if gat:
                    v.memset(t_rows[:, :, D + 9:TW], 0.0)
                v.wait_ge(loaded, 16 * n_loads)
                def pair(j):
                    for u in range(2):
                        wait(v, multiplied[u], j + 1)
                        for n, (d, b) in enumerate(zip(dest, biases)):
                            got = pl.banks[2 + u][:, n * D:(n + 1) * D]
                            if b is None:
                                ins = v.tensor_copy(target(d, j * 2 + u), got)
                            else:
                                ins = v.tensor_tensor(target(d, j * 2 + u), got, bias[:, n * D:(n + 1) * D], ALU.add)
                            ins.then_inc(written[u], 1)

                pairs(v, pair, NB // 2)
                for u in range(2):
                    v.wait_ge(written[u], NB // 2 * n_out)
                if gat:
                    H, K = gat[0].shape
                    for t, a, out in ((t_rows, a_l, t_rows[:, :, D:D + H]), (t_rows, a_r, q_rows[:, :, :])):
                        link(v.tensor_tensor(prod[:, :, :], t[:, :, 0:D], bc(a[:, :].unsqueeze(1), [P, NB, D]), ALU.mult))
                        link(v.tensor_reduce(out, prod[:, :, :].rearrange("p b (h k) -> p b h k", k=K), AX.X, ALU.add))
                    link(v.tensor_copy(t_rows[:, :, D + H], pl.node_vec_sb[:, :]))
                    link(v.tensor_copy(pl.res[:, :, :], pl.hn[:, :, :]))
                v.memset(flag[:, :], 1.0).then_inc(tables_ready, 1)
        sem.close()


def feed_forward(nc, pl, sems, att, gamma, beta, W1, b1, W2, b2):
    sem = Stage(nc, sems)
    NB = pl.NB
    CH = W1.shape[1] // P
    with ExitStack() as ctx:
        def sb(name, shape, dt=F32):
            return sem.tensor(ctx, name, shape, dt)

        norm = Norm(nc, ctx, pl, sem)
        g_row, be_row, b2_row = sb("g_row", [P, D]), sb("be_row", [P, D]), sb("b2_row", [P, D])
        w1 = sb("w1", [P, CH * P])
        w2 = sb("w2", [P, CH, D])
        b1_col = sb("b1_col", [P, CH])
        below = sb("below", [P, NB, D])
        e = sb("e", [P, NB, D])
        hb = [sb(f"hb{u}", [P, P]) for u in range(2)]
        ht = [sb(f"ht{u}", [P, P]) for u in range(2)]
        inter = [sb(f"inter{u}", [P, CH, P]) for u in range(2)]
        loaded, min_ready, exp_ready, normed, dve = sem("loaded"), sem("min_ready"), sem("exp_ready"), sem("normed"), sem("dve")
        block_ready = [sem(f"block_ready{u}") for u in range(2)]
        turned = [sem(f"turned{u}") for u in range(2)]
        turned_copied = [sem(f"turned_copied{u}") for u in range(2)]
        hidden = [sem(f"hidden{u}") for u in range(2)]
        hidden_used = [sem(f"hidden_used{u}") for u in range(2)]
        multiplied = [sem(f"multiplied{u}") for u in range(2)]
        written = [sem(f"written{u}") for u in range(2)]
        shape = [P, NB, D]
        with nc.Block() as block:
            @block.sync
            def _(sp):
                for t, a in ((g_row, gamma), (be_row, beta), (b2_row, b2)):
                    sp.dma_start(t[:, :], a.partition_broadcast(P)).then_inc(loaded, 16)
                sp.dma_start(w1[:, :], W1).then_inc(loaded, 16)
                sp.dma_start(w2[:, :, :], W2.rearrange("(c p) n -> p c n", p=P)).then_inc(loaded, 16)
                sp.dma_start(b1_col[:, :], b1.rearrange("(c p) -> p c", p=P), allow_slow_non_contiguous=True).then_inc(loaded, 16)
                sp.wait_ge(loaded, 96)

            @block.scalar
            def _(act):
                act.wait_ge(min_ready, 1)
                act.activation(e[:, :, :], below[:, :, :], ACT.Exp).then_inc(exp_ready, 1)
                norm.roots(act, 1)
                act.wait_ge(loaded, 96)
                act.wait_ge(normed, 1)
                def pair(j):
                    for u in range(2):
                        wait(act, turned[u], j)
                        act.activation(hb[u][:, :], pl.hn[:, bass.ds(j * 2 + u, 1), :].rearrange("p a d -> p (a d)"),
                                       ACT.Copy).then_inc(block_ready[u], 1)
                    for u in range(2):
                        wait(act, turned[u], j + 1)
                        wait(act, hidden[u], j)
                        act.activation(ht[u][:, :], pl.banks[u][:, 0:P], ACT.Copy).then_inc(turned_copied[u], 1)
                    for u in range(2):
                        wait(act, hidden[u], j + 1)
                        wait(act, multiplied[u], j)
                        for c in range(CH):
                            act.activation(inter[u][:, c, :], pl.banks[2 + u][:, c * P:(c + 1) * P], ACT.Relu,
                                           bias=b1_col[:, c:c + 1]).then_inc(hidden_used[u], 1)

                pairs(act, pair, NB // 2)

            @block.tensor
            def _(pe):
                pe.wait_ge(loaded, 96)
                def pair(j):
                    for u in range(2):
                        wait(pe, block_ready[u], j + 1)
                        wait(pe, turned_copied[u], j)
                        pe.transpose(pl.banks[u][:, 0:P], hb[u][:, :], pl.ident[:, :]).then_inc(turned[u], 1)
                    for u in range(2):
                        wait(pe, turned_copied[u], j + 1)
                        wait(pe, hidden_used[u], j * CH)
                        for c in range(CH):
                            ins = pe.matmul(pl.banks[2 + u][:, c * P:(c + 1) * P], w1[:, c * P:(c + 1) * P], ht[u][:, :],
                                            start=True, stop=True)
                        ins.then_inc(hidden[u], 1)
                    for u in range(2):
                        wait(pe, hidden_used[u], j * CH + CH)
                        wait(pe, written[u], j)
                        for c in range(CH):
                            ins = pe.matmul(pl.banks[4 + u][:, 0:D], inter[u][:, c, :], w2[:, c, :],
                                            start=(c == 0), stop=(c == CH - 1))
                        ins.then_inc(multiplied[u], 1)

                pairs(pe, pair, NB // 2)

            @block.vector
            def _(v):
                link = chain(v, dve)
                v.tensor_scalar(below[:, :, :], att[:, :, :], 0.0, None, ALU.min).then_inc(min_ready, 1)
                link(v.tensor_scalar(att[:, :, :], att[:, :, :], 0.0, None, ALU.max))
                link(v.tensor_tensor(att[:, :, :], att[:, :, :], pl.res[:, :, :], ALU.add))
                v.wait_ge(exp_ready, 1)
                f = "p b d -> p (b d)"
                link(v.scalar_tensor_tensor(att[:, :, :].rearrange(f), e[:, :, :].rearrange(f), -1.0,
                                            att[:, :, :].rearrange(f), ALU.add, ALU.add))
                norm.apply(v, link, pl.hn[:, :, :], att[:, :, :])
                v.wait_ge(loaded, 96)
                link(v.tensor_tensor(pl.hn[:, :, :], pl.hn[:, :, :], bc(g_row[:, :].unsqueeze(1), shape), ALU.mult))
                v.tensor_tensor(pl.hn[:, :, :], pl.hn[:, :, :], bc(be_row[:, :].unsqueeze(1), shape), ALU.add
                                ).then_inc(normed, 1)
                link(v.tensor_tensor(att[:, :, :], att[:, :, :], bc(b2_row[:, :].unsqueeze(1), shape), ALU.add))
                link(v.tensor_tensor(pl.x_sb[:, :, :], pl.x_sb[:, :, :], att[:, :, :], ALU.add))
                def pair(j):
                    for u in range(2):
                        wait(v, multiplied[u], j + 1)
                        o = pl.x_sb[:, bass.ds(j * 2 + u, 1), :].rearrange("p a d -> p (a d)")
                        v.tensor_tensor(o, o, pl.banks[4 + u][:, 0:D], ALU.add).then_inc(written[u], 1)

                pairs(v, pair, NB // 2)
                for u in range(2):
                    v.wait_ge(written[u], NB // 2)
        sem.close()


def add_residual(nc, pl, sems, att, to_stream, bias=None, norm_by=None):
    sem = Stage(nc, sems)
    NB = pl.NB
    shape = [P, NB, D]
    with ExitStack() as ctx:
        def sb(name, shape):
            return sem.tensor(ctx, name, shape, F32)

        dve, loaded = sem("dve"), sem("loaded")
        norm = Norm(nc, ctx, pl, sem) if norm_by else None
        rows = [sb(f"row{n}", [P, D]) for n in range(3)] if norm_by else []
        with nc.Block() as block:
            if norm_by:
                @block.sync
                def _(sp):
                    for t, a in zip(rows, (bias,) + norm_by):
                        sp.dma_start(t[:, :], a.partition_broadcast(P)).then_inc(loaded, 16)
                    sp.wait_ge(loaded, 48)

                @block.scalar
                def _(act):
                    norm.roots(act, 1)

            @block.vector
            def _(v):
                link = chain(v, dve)
                if norm_by:
                    v.wait_ge(loaded, 48)
                    r = [bc(t[:, :].unsqueeze(1), shape) for t in rows]
                    link(v.tensor_tensor(att[:, :, :], att[:, :, :], r[0], ALU.add))
                    link(v.tensor_scalar(att[:, :, :], att[:, :, :], 0.0, None, ALU.max))
                    norm.apply(v, link, pl.hn[:, :, :], att[:, :, :])
                    link(v.tensor_tensor(pl.hn[:, :, :], pl.hn[:, :, :], r[1], ALU.mult))
                    link(v.tensor_tensor(pl.hn[:, :, :], pl.hn[:, :, :], r[2], ALU.add))
                    if to_stream:
                        link(v.tensor_tensor(pl.x_sb[:, :, :], pl.x_sb[:, :, :], pl.hn[:, :, :], ALU.add))
                elif to_stream:
                    link(v.tensor_tensor(att[:, :, :], att[:, :, :], pl.res[:, :, :], ALU.add))
                    link(v.tensor_tensor(pl.x_sb[:, :, :], pl.x_sb[:, :, :], att[:, :, :], ALU.add))
                else:
                    link(v.tensor_tensor(pl.hn[:, :, :], att[:, :, :], pl.res[:, :, :], ALU.add))
        sem.close()


def load_sweep_weights(nc, sems, ctx, pieces):
    sem = Stage(nc, sems)
    loaded = sem("loaded")
    out = {}
    for name, ap in pieces.items():
        shape = list(ap.shape) if len(ap.shape) == 2 else [P, ap.shape[0]]
        out[name] = ctx.enter_context(nc.sbuf_tensor(f"s{sem.number}_{name}", shape, F32))
    with nc.Block() as block:
        @block.sync
        def _(sp):
            for name, ap in pieces.items():
                sp.dma_start(out[name][:, :], ap if len(ap.shape) == 2 else ap.partition_broadcast(P)
                             ).then_inc(loaded, 16)
            sp.wait_ge(loaded, 16 * len(pieces))
    sem.close()
    return out


def store_output(nc, pl, sems, out):
    sem = Stage(nc, sems)
    stored = sem("stored")
    full = pl.N // P
    with nc.Block() as block:
        @block.sync
        def _(sp):
            sp.dma_start(out[0:full * P, :].rearrange("(b p) c -> p b c", p=P), pl.x_sb[:, 0:full, :]).then_inc(stored, 16)
            sp.dma_start(out[full * P:pl.N, :], pl.x_sb[0:pl.N - full * P, full, :]).then_inc(stored, 16)
            sp.wait_ge(stored, 32)


def gnn_kernel(nc, a, out):
    sems = {"semaphores": [], "stages": 0}
    with ExitStack() as ctx:
        pl = Plan(nc, ctx, a["x"], a["src"], a["edge_attr_64"])
        att_shape = [P, pl.NB, D]

        def attend(name, kind, H, tab, q_tab, scale, pieces, after):
            with ExitStack() as c:
                w = load_sweep_weights(nc, sems, c, pieces) if pieces else {}
                edge_sweep(nc, pl, sems, kind, H, tab, q_tab, pl.part_tab[H], scale, w)
            with ExitStack() as c:
                att = c.enter_context(nc.sbuf_tensor("att_" + name, att_shape, F32))
                merge_parts(nc, pl, sems, H, scale, att)
                after(att)

        setup_graph(nc, pl, sems, a["x"], a["src"], a["dst"], a["edge_weight"], a["node_vec"])

        norm_input(nc, pl, sems)
        project(nc, pl, sems, [a["L0_gnn_W_fc"]], [None], ["z"], gat=(a["L0_gnn_a_l"], a["L0_gnn_a_r"]))
        attend("gat", "gat", 8, pl.gat_tab, pl.er_tab, 1.0,
               {"Wt": a["L1_gnn_Wt"].rearrange("a c -> (a c)"), "bt": a["L1_gnn_bt"]},
               lambda att: feed_forward(nc, pl, sems, att, a["L0_gnn_ln_gamma"], a["L0_gnn_ln_beta"], a["L0_gnn_W1"],
                                        a["L0_gnn_b1"], a["L0_gnn_W2"], a["L0_gnn_b2"]))

        norm_input(nc, pl, sems)
        for n in "12":
            w = {k: a[f"L1_gnn_{k}{n}"] for k in ("Wq", "bq", "Wk", "bk", "Wv", "bv", "We", "Wskip", "bskip")}
            project(nc, pl, sems, [w["Wq"], w["Wk"], w["Wv"], w["Wskip"]], [w["bq"], w["bk"], w["bv"], w["bskip"]],
                    ["q", "k", "v", "res"])
            attend("conv" + n, "tconv", 4, pl.kv_tab, pl.q_tab, 32 ** -0.5, {"We": w["We"]},
                   lambda att: add_residual(nc, pl, sems, att, n == "2"))

        norm_input(nc, pl, sems)
        w = {k: a[f"L2_gnn_{k}"] for k in ("Wq", "bq", "Wk", "bk", "Wv", "bv", "Wr", "br")}
        project(nc, pl, sems, [w["Wq"], w["Wk"], w["Wv"], w["Wr"]], [w["bq"], w["bk"], w["bv"], w["br"]],
                ["q", "k", "v", "res"])
        attend("mha", "mha", 4, pl.kv_tab, pl.q_tab, 32 ** -0.5, {},
               lambda att: add_residual(nc, pl, sems, att, True))

        norm_input(nc, pl, sems)
        for n in "12":
            project(nc, pl, sems, [a["L3_gnn_Wl" + n], a["L3_gnn_Wr" + n]], [None, None], ["xl", "q"])
            attend("gatv2" + n, "gatv2", 8, pl.xl_tab, pl.q_tab, 1.0,
                   {"att": a["L3_gnn_att" + n].rearrange("h k -> (h k)")},
                   lambda att: add_residual(nc, pl, sems, att, n == "2", a["L3_gnn_b" + n],
                                            (a["L3_gnn_g" + n], a["L3_gnn_be" + n])))
        store_output(nc, pl, sems, out)


def kernel(**inputs):
    import numpy as _np
    import concourse.bacc as _bacc
    from concourse import mybir as _mybir
    from concourse.bass_utils import run_bass_kernel_spmd as _run

    nc = _bacc.Bacc("TRN2", target_bir_lowering=False, num_devices=1)
    arrays, args = {}, {}
    for name, value in inputs.items():
        a = _np.ascontiguousarray(value)
        arrays["in_" + name] = a
        args[name] = nc.dram_tensor("in_" + name, a.shape, _mybir.dt.from_np(a.dtype), kind="ExternalInput").ap()
    out = nc.dram_tensor("out", arrays["in_x"].shape, F32, kind="ExternalOutput").ap()
    gnn_kernel(nc, args, out)
    return _run(nc, [arrays], core_ids=[0]).results[0]["out"]
```

```python
from contextlib import ExitStack

import numpy as np

import concourse.bass as bass
from concourse import mybir

F32 = mybir.dt.float32
I32 = mybir.dt.int32
BF16 = mybir.dt.bfloat16
ALU = mybir.AluOpType
ACT = mybir.ActivationFunctionType
AX = mybir.AxisListType

P = 128
D = 128
G = 8
HALF = G // 2
SLOTS = 4
FAR = -1.0e38
TINY = 1.0e-9
EPS = 1.0e-5
MAGIC = 12582912.0
TWO_PI_HIGH = 6.28125
TWO_PI_LOW = float(2 * np.pi - 6.28125)


def bc(ap, shape):
    return ap.to_broadcast(shape)


class Plan:

    def __init__(self, nc, ctx, x, src, edge_attr):
        self.N, self.E = x.shape[0], src.shape[0]
        tiles = -(-self.E // P)
        self.NG = -(-tiles // G)
        self.TT = self.NG * G
        self.TB = -(-self.TT // P)
        self.NB = 2 * -(-self.N // (2 * P))
        self.NP = self.NB * P
        self.DL_W = 2 * P + 4
        self.edge_attr = edge_attr
        assert self.NG >= 16 and x.shape[1] == D

        def sb(name, shape, dt=F32):
            return ctx.enter_context(nc.sbuf_tensor(name, shape, dt))

        def dram(name, shape):
            return nc.dram_tensor(name, shape, F32, kind="Internal").ap()

        NB, TB, NP, TT = self.NB, self.TB, self.NP, self.TT
        self.banks = [ctx.enter_context(nc.psum_tensor(f"bank{b}", [P, 512], F32)) for b in range(8)]
        self.ident = sb("ident", [P, P])
        self.ident_b = sb("ident_b", [P, P], BF16)
        self.head8, self.head4 = sb("head8", [P, D]), sb("head4", [P, D])
        self.iota_free, self.iota_free_i = sb("iota_free", [P, P]), sb("iota_free_i", [P, P], I32)
        self.node_id_i = sb("node_id_i", [P, NB], I32)
        self.half_pi = sb("half_pi", [P, 1])
        self.eps = sb("eps", [P, 1])
        self.one = sb("one", [P, 1])
        self.x_sb = sb("x_sb", [P, NB, D])
        self.hn = sb("hn", [P, NB, D])
        self.res = sb("res", [P, NB, D])
        self.node_vec_sb = sb("node_vec_sb", [P, NB])
        self.src_col = sb("src_col", [P, TB * P])
        self.rank_col = sb("rank_col", [P, TB * P])
        self.last_col = sb("last_col", [P, TB * P])
        self.weight_col = sb("weight_col", [P, TB * P])
        self.whole_row = sb("whole_row", [P, TB * P])
        self.whole_pen = sb("whole_pen", [P, TB * P])
        self.window_i = sb("window_i", [1, TB * P], I32)
        self.tile_last_i = sb("tile_last_i", [P, TB], I32)
        self.part_i = sb("part_i", [P, NB], I32)
        self.carry_i = sb("carry_i", [P, NB], I32)
        self.carry_pen = sb("carry_pen", [P, NB])
        self.has_edges = sb("has_edges", [P, NB])
        self.compact_i = sb("compact_i", [P, NB], I32)
        self.dl_tab = dram("dl_tab", [TB * P, self.DL_W])
        self.neg_tab = {H: dram(f"neg_tab{H}", [TB * P * H, 2 * P]) for H in (8, 4)}
        self.row_tab = dram("row_tab", [3 * TB * P])
        self.gat_tab = dram("gat_tab", [NP, D + 16])
        self.kv_tab = dram("kv_tab", [NP, 2 * D])
        self.xl_tab = dram("xl_tab", [NP, D])
        self.q_tab = dram("q_tab", [NP + P, D])
        self.er_tab = dram("er_tab", [NP + P, 8])
        self.attr_tab = dram("attr_tab", [self.NG * P, G * P])
        self.part_tab = {H: dram(f"part_tab{H}", [TT * P, D + 2 * H]) for H in (8, 4)}
        self.carry_tab = {H: dram(f"carry_tab{H}", [TB * P, D + 2 * H]) for H in (8, 4)}


def wait(eng, sem, value):
    if isinstance(value, int) and value <= 0:
        return
    eng.wait_ge(sem, value)


def pairs(eng, pair, count):
    pair(0)
    with eng.Fori(1, count) as j:
        pair(j)


def settle(eng, passed):
    eng.sem_inc(passed, 1)


class Stage:

    def __init__(self, nc, shared):
        self.nc, self.shared, self.used = nc, shared, {}
        shared["stages"] += 1
        self.number = shared["stages"]

    def __call__(self, name):
        if name not in self.used:
            free = self.shared["semaphores"]
            if len(self.used) == len(free):
                free.append(self.nc.alloc_semaphore(f"stage_semaphore_{len(free)}"))
            self.used[name] = free[len(self.used)]
        return self.used[name]

    def indirect(self, name):
        return self.nc.alloc_semaphore(self.name(name))

    def name(self, name):
        return f"s{self.number}_{name}"

    def tensor(self, ctx, name, shape, dt=F32):
        return ctx.enter_context(self.nc.sbuf_tensor(self.name(name), shape, dt))

    def close(self):
        with self.nc.Block() as block:
            @block.gpsimd
            def _(pool):
                for s in self.used.values():
                    pool.sem_clear(s)


def chain(eng, sem):
    count = [0]

    def link(ins):
        count[0] += 1
        ins.then_inc(sem, 1)
        eng.wait_ge(sem, count[0])

    return link



def setup_graph(nc, pl, sems, x, src, dst, edge_weight, node_vec):
    sem = Stage(nc, sems)
    TB, NB = pl.TB, pl.NB
    E = pl.E
    whole_tiles = E // P
    whole_blocks = whole_tiles // P
    rest_tiles = whole_tiles - whole_blocks * P
    rest_edges = E - whole_tiles * P

    with ExitStack() as ctx:
        def sb(name, shape, dt=F32):
            return sem.tensor(ctx, name, shape, dt)

        src_i = sb("src_i", [P, TB, P], I32)
        dst_i = sb("dst_i", [P, TB, P], I32)
        weight = sb("weight", [P, TB, P])
        dst_f = sb("dst_f", [P, TB, P])
        src_f = sb("src_f", [P, TB, P])
        start = sb("start", [P, TB, P])
        local_start = sb("local_start", [P, TB, P])
        not_first = sb("not_first", [P, TB, P])
        rank1 = sb("rank1", [P, TB, P])
        last_in_tile = sb("last_in_tile", [P, TB, P])
        dl = sb("dl", [P, TB, pl.DL_W])
        neg = sb("neg", [P, TB, 2 * P])
        dst_last1 = sb("dst_last1", [P, TB])
        prev_dst = sb("prev_dst", [P, TB])
        lr_last = sb("lr_last", [P, TB])
        prev_lr = sb("prev_lr", [P, TB])
        n_starts = sb("n_starts", [P, TB])
        totals = sb("totals", [P, TB])
        running = sb("running", [P, TB])
        ones_row = sb("ones_row", [P, max(TB, NB)])
        window = sb("window", [P, TB])
        whole = sb("whole", [P, TB])
        tile_id = sb("tile_id", [P, TB])
        tile_last = sb("tile_last", [P, TB])
        rows3 = sb("rows3", [P, 3 * TB])
        rows3_t = sb("rows3_t", [3 * TB, P])
        last_row = sb("last_row", [P, TB * P])
        window_f = sb("window_f", [1, TB * P])
        shift_m = sb("shift_m", [P, P])
        corner_m = sb("corner_m", [P, P])
        below_m = sb("below_m", [P, P])
        ones_m = sb("ones_m", [P, P])
        zeros = sb("zeros", [P, P])
        le = sb("le", [P, TB * P])
        tb_f = sb("tb_f", [P, NB])
        tb_i = sb("tb_i", [P, NB], I32)
        found = sb("found", [P, NB, pl.DL_W])
        hit = sb("hit", [P, NB, P])
        cnt = sb("cnt", [P, NB])
        row_end = sb("row_end", [P, NB])
        row_start = sb("row_start", [P, NB])
        lr_end = sb("lr_end", [P, NB])
        lr_sel = sb("lr_sel", [P, NB])
        at_edge = sb("at_edge", [P, NB])
        pe_pos = sb("pe_pos", [P, NB])
        te = sb("te", [P, NB])
        tmp = sb("tmp", [P, NB])
        node_id = sb("node_id", [P, NB])
        before = sb("before", [P, NB])
        n_tot = sb("n_tot", [P, NB])
        n_run = sb("n_run", [P, NB])
        compact = sb("compact", [P, NB])

        padded, loaded = sem("padded"), sem("loaded")
        consts, made = sem("consts"), sem("pool_made")
        shifted, shift_used = sem("shifted"), sem("shift_used")
        tables, marks, rows = sem("tables_stored"), sem("marks_stored"), sem("rows_stored")
        turned, turned_used = sem("turned"), sem("turned_used")
        dve = sem("dve")
        dl_ready, last_ready = sem("dl_ready"), sem("last_ready")
        starts_ready, prefix_done = sem("starts_ready"), sem("prefix_done")
        rows3_ready, rows3_turned, rows3_copied = sem("rows3_ready"), sem("rows3_turned"), sem("rows3_copied")
        row_loaded = sem("row_loaded")
        tb_ready, searched = sem("tb_ready"), sem.indirect("searched")
        end_ready, end_shifted = sem("end_ready"), sem("end_shifted")
        has_ready, has_prefix = sem("has_ready"), sem("has_prefix")
        lists_ready = sem("lists_ready")
        small_loaded, zeroed = sem("small_loaded"), sem("zeroed")
        zero_done = sem("zero_done")
        ps = pl.banks

        with nc.Block() as block:
            @block.sync
            def _(sp):
                def load_tiles(tile, flat):
                    n = 0
                    if whole_blocks:
                        sp.dma_start(tile[:, 0:whole_blocks, :],
                                     flat[0:whole_blocks * P * P].rearrange("(g p e) -> p g e", p=P, e=P)
                                     ).then_inc(loaded, 16)
                        n += 1
                    if rest_tiles:
                        lo = whole_blocks * P * P
                        sp.dma_start(tile[0:rest_tiles, whole_blocks, :],
                                     flat[lo:lo + rest_tiles * P].rearrange("(p e) -> p e", e=P)
                                     ).then_inc(loaded, 16)
                        n += 1
                    if rest_edges:
                        sp.dma_start(tile[rest_tiles:rest_tiles + 1, whole_blocks, 0:rest_edges],
                                     flat[whole_tiles * P:E].rearrange("(p e) -> p e", p=1)
                                     ).then_inc(loaded, 16)
                        n += 1
                    return n

                sp.wait_ge(padded, 4)
                pl.list_loads = load_tiles(dst_i, dst) + load_tiles(src_i, src) + load_tiles(weight, edge_weight)
                full = pl.N // P
                sp.dma_start(pl.x_sb[:, 0:full, :], x[0:full * P, :].rearrange("(b p) c -> p b c", p=P)
                             ).then_inc(small_loaded, 16)
                sp.dma_start(pl.x_sb[0:pl.N - full * P, full, :], x[full * P:pl.N, :]).then_inc(small_loaded, 16)
                sp.dma_start(pl.node_vec_sb[:, 0:full], node_vec[0:full * P].rearrange("(b p) -> p b", p=P),
                             allow_slow_non_contiguous=True).then_inc(small_loaded, 16)
                sp.dma_start(pl.node_vec_sb[0:pl.N - full * P, full:full + 1],
                             node_vec[full * P:pl.N].rearrange("(p b) -> p b", b=1),
                             allow_slow_non_contiguous=True).then_inc(small_loaded, 16)
                sp.wait_ge(zero_done, 1)
                sp.dma_start(pl.q_tab[pl.NP:pl.NP + P, :], zeros[:, :]).then_inc(zeroed, 16)
                sp.dma_start(pl.er_tab[pl.NP:pl.NP + P, :], zeros[:, 0:8]).then_inc(zeroed, 16)
                sp.wait_ge(dl_ready, 1)
                sp.dma_start(pl.dl_tab.rearrange("(g p) w -> p g w", p=P), dl[:, :, :]).then_inc(tables, 16)
                for H, tab in pl.neg_tab.items():
                    for h in range(H):
                        sp.dma_start(tab.rearrange("(g p h) w -> p g h w", p=P, h=H)[:, :, h, :], neg[:, :, :]
                                     ).then_inc(marks, 16)
                sp.wait_ge(rows3_copied, 1)
                sp.dma_start(pl.row_tab.rearrange("(k p) -> k p", p=P), rows3_t[:, :]).then_inc(rows, 16)
                sp.wait_ge(rows, 16)
                n = TB * P
                sp.dma_start(last_row[:, :], pl.row_tab[0:n].partition_broadcast(P)).then_inc(row_loaded, 16)
                sp.dma_start(pl.whole_row[:, :], pl.row_tab[n:2 * n].partition_broadcast(P)).then_inc(row_loaded, 16)
                sp.dma_start(window_f[:, :], pl.row_tab[2 * n:3 * n].rearrange("(a n) -> a n", a=1)
                             ).then_inc(row_loaded, 16)
                sp.wait_ge(zeroed, 32)
                sp.wait_ge(marks, 16 * sum(pl.neg_tab))
                sp.wait_ge(small_loaded, 64)

            @block.gpsimd
            def _(pool):
                pool.memset(zeros[:, :], 0.0).then_inc(zero_done, 1)
                for m in (pl.ident, shift_m, corner_m, below_m, pl.head8, pl.head4):
                    pool.memset(m[:, :], 0.0).then_inc(made, 1)
                pool.memset(ones_m[:, :], 1.0).then_inc(made, 1)
                pool.wait_ge(made, 7)
                pool.affine_select(out=pl.ident[:, :], in_=pl.ident[:, :], compare_op=ALU.not_equal, fill=1.0, base=0,
                                   pattern=[[-1, P]], channel_multiplier=1).then_inc(made, 1)
                pool.affine_select(out=shift_m[:, :], in_=shift_m[:, :], compare_op=ALU.not_equal, fill=1.0, base=1,
                                   pattern=[[-1, P]], channel_multiplier=1).then_inc(made, 1)
                pool.affine_select(out=corner_m[:, :], in_=corner_m[:, :], compare_op=ALU.not_equal, fill=1.0,
                                   base=-(P - 1), pattern=[[-P, P]], channel_multiplier=1).then_inc(made, 1)
                pool.affine_select(out=below_m[:, :], in_=below_m[:, :], compare_op=ALU.is_ge, fill=1.0, base=0,
                                   pattern=[[-1, P]], channel_multiplier=1).then_inc(made, 1)
                for m, c in ((pl.head8, 16), (pl.head4, 32)):
                    v = m[:, :].rearrange("h (a c) -> h a c", c=c)
                    pool.affine_select(out=v, in_=v, compare_op=ALU.not_equal, fill=1.0, base=0,
                                       pattern=[[-1, D // c], [0, c]], channel_multiplier=1).then_inc(made, 1)
                pool.iota(pl.iota_free_i[:, :], pattern=[[1, P]], base=0, channel_multiplier=0).then_inc(made, 1)
                pool.iota(pl.node_id_i[:, :], pattern=[[P, NB]], base=0, channel_multiplier=1).then_inc(made, 1)
                pool.wait_ge(tables, 16)
                pool.wait_ge(tb_ready, 1)
                for b in range(NB):
                    pool.indirect_dma_start(out=found[:, b, :], out_offset=None, in_=pl.dl_tab,
                                            in_offset=bass.IndirectOffsetOnAxis(ap=tb_i[:, b:b + 1], axis=0)
                                            ).then_inc(searched, 16)

            @block.vector
            def _(v):
                link = chain(v, dve)
                v.memset(dst_i[:, :, :], pl.NP).then_inc(padded, 1)
                v.memset(src_i[:, :, :], 0).then_inc(padded, 1)
                v.memset(weight[:, :, :], 0.0).then_inc(padded, 1)
                v.memset(pl.x_sb[:, :, :], 0.0)
                v.memset(pl.node_vec_sb[:, :], 0.0).then_inc(padded, 1)
                v.memset(ones_row[:, :], 1.0)
                v.memset(pl.half_pi[:, :], float(np.pi / 2))
                v.memset(pl.eps[:, :], EPS)
                v.memset(pl.one[:, :], 1.0)
                v.memset(not_first[:, :, :], 1.0)
                v.memset(dl[:, :, 2 * P:pl.DL_W], 0.0)
                link(v.memset(last_in_tile[:, :, P - 1:P], 1.0))
                link(v.memset(not_first[:, :, 0:1], 0.0))
                v.wait_ge(made, 15)
                v.tensor_copy(pl.iota_free[:, :], pl.iota_free_i[:, :])
                v.tensor_copy(pl.ident_b[:, :], pl.ident[:, :])
                link(v.tensor_copy(node_id[:, :], pl.node_id_i[:, :]))
                v.wait_ge(loaded, 16 * pl.list_loads)
                link(v.tensor_copy(dst_f[:, :, :], dst_i[:, :, :]))
                v.tensor_copy(dl[:, :, 0:P], dst_f[:, :, :])
                link(v.tensor_copy(src_f[:, :, :], src_i[:, :, :]))
                v.tensor_scalar(dst_last1[:, :], dst_f[:, :, P - 1], 1.0, None, ALU.add).then_inc(last_ready, 1)
                v.wait_ge(shifted, 1)
                link(v.tensor_scalar(prev_dst[:, :], ps[0][:, 0:TB], -1.0, None, ALU.add))
                link(v.tensor_tensor(prev_dst[:, 1:TB], prev_dst[:, 1:TB], ps[0][:, 64:64 + TB - 1], ALU.add))
                v.tensor_tensor(start[:, :, 1:P], dst_f[:, :, 1:P], dst_f[:, :, 0:P - 1], ALU.not_equal)
                link(v.tensor_tensor(start[:, :, 0], dst_f[:, :, 0], prev_dst[:, :], ALU.not_equal))
                v.tensor_copy(local_start[:, :, 1:P], start[:, :, 1:P])
                v.memset(local_start[:, :, 0:1], 1.0)
                v.tensor_reduce(n_starts[:, :], start[:, :, :], AX.X, ALU.add).then_inc(starts_ready, 1)
                link(v.tensor_copy(last_in_tile[:, :, 0:P - 1], start[:, :, 1:P]))
                link(v.tensor_tensor_scan(rank1[:, :, :].rearrange("p g e -> p (g e)"),
                                          not_first[:, :, :].rearrange("p g e -> p (g e)"),
                                          local_start[:, :, :].rearrange("p g e -> p (g e)"), 0.0, ALU.mult, ALU.add))
                v.tensor_scalar(neg[:, :, 0:P], local_start[:, :, :], FAR, None, ALU.mult)
                v.tensor_scalar(neg[:, :, P:2 * P], last_in_tile[:, :, :], FAR, None, ALU.mult)
                v.tensor_scalar(lr_last[:, :], rank1[:, :, P - 1], -1.0, None, ALU.add).then_inc(last_ready, 1)
                link(v.tensor_scalar(dl[:, :, P:2 * P], rank1[:, :, :], -1.0, None, ALU.add))
                v.wait_ge(shifted, 2)
                link(v.tensor_copy(prev_lr[:, :], ps[1][:, 0:TB]))
                link(v.tensor_tensor(prev_lr[:, 1:TB], prev_lr[:, 1:TB], ps[1][:, 64:64 + TB - 1], ALU.add))
                v.tensor_copy(dl[:, :, 2 * P], prev_lr[:, :]).then_inc(dl_ready, 1)
                v.wait_ge(prefix_done, 1)
                link(v.tensor_copy(totals[:, :], ps[2][:, 64:64 + TB]))
                link(v.tensor_tensor_scan(running[:, :], ones_row[:, 0:TB], totals[:, :], 0.0, ALU.mult, ALU.add))
                link(v.tensor_tensor(running[:, :], running[:, :], totals[:, :], ALU.subtract))
                link(v.tensor_tensor(window[:, :], running[:, :], ps[2][:, 0:TB], ALU.add))
                link(v.tensor_tensor(window[:, :], window[:, :], start[:, :, 0], ALU.add))
                v.tensor_scalar(rows3[:, 2 * TB:3 * TB], window[:, :], -1.0, None, ALU.add)
                link(v.tensor_scalar(whole[:, :], lr_last[:, :], 0.0, None, ALU.is_equal))
                link(v.tensor_scalar(prev_dst[:, :], start[:, :, 0], -1.0, 1.0, ALU.mult, ALU.add))
                v.tensor_tensor(rows3[:, TB:2 * TB], whole[:, :], prev_dst[:, :], ALU.mult)
                v.tensor_copy(rows3[:, 0:TB], dst_f[:, :, P - 1]).then_inc(rows3_ready, 1)
                link(v.tensor_scalar(tile_id[:, :], node_id[:, 0:TB], float(P), None, ALU.mult))
                link(v.tensor_tensor(tile_last[:, :], tile_id[:, :], lr_last[:, :], ALU.add))
                link(v.tensor_scalar(tile_last[:, :], tile_last[:, :], float(pl.TT * P - 1), None, ALU.min))
                v.tensor_copy(pl.tile_last_i[:, :], tile_last[:, :])
                v.wait_ge(rows3_turned, 1)
                v.tensor_copy(rows3_t[:, :], ps[3][0:3 * TB, 0:P]).then_inc(rows3_copied, 1)
                for n, out in enumerate((pl.src_col, pl.rank_col, pl.last_col, pl.weight_col)):
                    for half in range(2):
                        v.wait_ge(turned, 2 * n + half + 1)
                        lo, hi = (0, 4) if half == 0 else (4, TB)
                        v.tensor_copy(out[:, lo * P:hi * P], ps[4 + half][:, 0:(hi - lo) * P]).then_inc(turned_used, 1)
                v.wait_ge(row_loaded, 48)
                v.tensor_copy(pl.window_i[:, :], window_f[:, :])
                v.tensor_scalar(pl.whole_pen[:, :], pl.whole_row[:, :], -FAR, FAR, ALU.mult, ALU.add)
                for b in range(NB):
                    link(v.tensor_tensor(le[:, :], last_row[:, :], bc(node_id[:, b:b + 1], [P, TB * P]), ALU.is_le))
                    link(v.tensor_reduce(tb_f[:, b:b + 1], le[:, :], AX.X, ALU.add))
                v.tensor_copy(tb_i[:, :], tb_f[:, :]).then_inc(tb_ready, 1)
                v.wait_ge(searched, 16 * NB)
                link(v.tensor_tensor(hit[:, :, :], found[:, :, 0:P],
                                     bc(node_id[:, :].unsqueeze(2), [P, NB, P]), ALU.is_le))
                link(v.tensor_reduce(cnt[:, :], hit[:, :, :], AX.X, ALU.add))
                v.scalar_tensor_tensor(row_end[:, :], tb_f[:, :], float(P), cnt[:, :], ALU.mult, ALU.add
                                       ).then_inc(end_ready, 1)
                v.wait_ge(end_shifted, 1)
                link(v.tensor_copy(row_start[:, :], ps[6][:, 0:NB]))
                link(v.tensor_tensor(row_start[:, 1:NB], row_start[:, 1:NB], ps[6][:, 64:64 + NB - 1], ALU.add))
                v.tensor_tensor(pl.has_edges[:, :], row_end[:, :], row_start[:, :], ALU.is_gt).then_inc(has_ready, 1)
                v.wait_ge(has_ready, 1)
                link(v.tensor_scalar(at_edge[:, :], cnt[:, :], 0.0, None, ALU.is_equal))
                link(v.tensor_tensor(te[:, :], tb_f[:, :], at_edge[:, :], ALU.subtract))
                link(v.tensor_scalar(te[:, :], te[:, :], 0.0, None, ALU.max))
                link(v.tensor_scalar(pe_pos[:, :], cnt[:, :], -1.0, None, ALU.add))
                link(v.tensor_tensor(hit[:, :, :], bc(pl.iota_free[:, :].unsqueeze(1), [P, NB, P]),
                                     bc(pe_pos[:, :].unsqueeze(2), [P, NB, P]), ALU.is_equal))
                link(v.tensor_tensor(hit[:, :, :], hit[:, :, :], found[:, :, P:2 * P], ALU.mult))
                link(v.tensor_reduce(lr_sel[:, :], hit[:, :, :], AX.X, ALU.add))
                link(v.tensor_tensor(lr_end[:, :], at_edge[:, :], found[:, :, 2 * P], ALU.mult))
                link(v.tensor_tensor(lr_end[:, :], lr_end[:, :], lr_sel[:, :], ALU.add))
                link(v.scalar_tensor_tensor(tmp[:, :], te[:, :], float(P), lr_end[:, :], ALU.mult, ALU.add))
                v.tensor_copy(pl.part_i[:, :], tmp[:, :])
                link(v.tensor_scalar(lr_sel[:, :], te[:, :], -1.0, 0.0, ALU.add, ALU.max))
                v.tensor_copy(pl.carry_i[:, :], lr_sel[:, :])
                link(v.tensor_scalar(tmp[:, :], te[:, :], float(P), None, ALU.mult))
                link(v.tensor_tensor(tmp[:, :], row_start[:, :], tmp[:, :], ALU.is_lt))
                link(v.tensor_tensor(tmp[:, :], tmp[:, :], pl.has_edges[:, :], ALU.mult))
                v.tensor_scalar(pl.carry_pen[:, :], tmp[:, :], -FAR, FAR, ALU.mult, ALU.add)
                v.wait_ge(has_prefix, 1)
                link(v.tensor_copy(n_tot[:, :], ps[7][:, 64:64 + NB]))
                link(v.tensor_tensor_scan(n_run[:, :], ones_row[:, 0:NB], n_tot[:, :], 0.0, ALU.mult, ALU.add))
                link(v.tensor_tensor(before[:, :], n_run[:, :], n_tot[:, :], ALU.subtract))
                link(v.tensor_tensor(before[:, :], before[:, :], ps[7][:, 0:NB], ALU.add))
                link(v.tensor_tensor(compact[:, :], node_id[:, :], before[:, :], ALU.subtract))
                link(v.tensor_tensor(compact[:, :], compact[:, :], bc(n_run[:, NB - 1:NB], [P, NB]), ALU.add))
                link(v.tensor_tensor(tmp[:, :], before[:, :], compact[:, :], ALU.subtract))
                link(v.tensor_tensor(tmp[:, :], tmp[:, :], pl.has_edges[:, :], ALU.mult))
                link(v.tensor_tensor(compact[:, :], compact[:, :], tmp[:, :], ALU.add))
                link(v.tensor_copy(pl.compact_i[:, :], compact[:, :]))

            @block.tensor
            def _(pe):
                def shift(bank, vals, n, done):
                    pe.matmul(ps[bank][:, 0:n], shift_m[:, :], vals[:, 0:n], start=True, stop=True)
                    pe.matmul(ps[bank][:, 64:64 + n - 1], corner_m[:, :], vals[:, 0:n - 1], start=True, stop=True
                              ).then_inc(done, 1)

                def prefix(bank, vals, n, done):
                    pe.matmul(ps[bank][:, 0:n], below_m[:, :], vals[:, 0:n], start=True, stop=True)
                    pe.matmul(ps[bank][:, 64:64 + n], ones_m[:, :], vals[:, 0:n], start=True, stop=True
                              ).then_inc(done, 1)

                pe.wait_ge(made, 13)
                pe.wait_ge(last_ready, 1)
                shift(0, dst_last1, TB, shifted)
                pe.wait_ge(last_ready, 2)
                shift(1, lr_last, TB, shifted)
                pe.wait_ge(starts_ready, 1)
                prefix(2, n_starts, TB, prefix_done)
                pe.wait_ge(rows3_ready, 1)
                pe.transpose(ps[3][0:3 * TB, 0:P], rows3[:, :], pl.ident[:, :]).then_inc(rows3_turned, 1)
                pe.wait_ge(dl_ready, 1)
                for n, tiles in enumerate((src_f, dl[:, :, P:2 * P], last_in_tile, weight)):
                    for half in range(2):
                        wait(pe, turned_used, 2 * n + half - 1)
                        lo, hi = (0, 4) if half == 0 else (4, TB)
                        for g in range(lo, hi):
                            ins = pe.transpose(ps[4 + half][:, (g - lo) * P:(g - lo + 1) * P], tiles[:, g, :],
                                               pl.ident[:, :])
                        ins.then_inc(turned, 1)
                pe.wait_ge(end_ready, 1)
                shift(6, row_end, NB, end_shifted)
                pe.wait_ge(has_ready, 1)
                prefix(7, pl.has_edges, NB, has_prefix)
        sem.close()



def edge_sweep(nc, pl, sems, kind, H, tab, q_tab, part_tab, scale, w):
    sem = Stage(nc, sems)
    TW = tab.shape[1]
    QW = q_tab.shape[1]
    C = D // H
    R = G * H
    W = D + 2 * H
    NG = pl.NG
    QB = 1 if kind == "gat" else 2
    PAIR = 2
    NPAIR = G // PAIR
    S = SLOTS
    act_builds = kind in ("tconv", "gatv2")

    with ExitStack() as ctx:
        def sb(name, shape, dt=F32):
            return sem.tensor(ctx, name, shape, dt)

        rows = [sb(f"rows{u}", [P, G, TW]) for u in range(S)]
        qwin = [sb(f"qwin{u}", [P, G, QW]) for u in range(S)]
        neg = [sb(f"neg{u}", [R, 2 * P]) for u in range(S)]
        idx = [sb(f"idx{u}", [P, G], I32) for u in range(S)]
        hot = [sb(f"hot{u}", [P, G, P]) for u in range(S)]
        if kind != "gat":
            hot_b = [sb(f"hot_b{u}", [P, G, P], BF16) for u in range(2)]
        if act_builds:
            gap = sb("gap", [P, G, P], BF16)
        hot_t = sb("hot_t", [P, G, P])
        alpha = sb("alpha", [P, G, H])
        fwd = sb("fwd", [R, P])
        seg_max = sb("seg_max", [R, P])
        diff = sb("diff", [R, P])
        prob = sb("prob", [R, P])
        pm = sb("pm", [P, 2 * R])
        msg = sb("msg", [P, G, W])
        part = [sb(f"part{u}", [P, G, W]) for u in range(S)]
        prod = [sb(f"prod{h}", [P, HALF, D]) for h in range(2)]
        if kind == "gat":
            rel = sb("rel", [P, G])
            attr = [sb(f"attr{u}", [P, G, D]) for u in range(S)]
            ang, turns = sb("ang", [P, G, 64]), sb("turns", [P, G, 64])
            ang2 = [sb(f"ang2{u}", [P, G, 64]) for u in range(S)]
        if kind in ("gat", "tconv"):
            attr_t = [sb(f"attr_t{u}", [P, G * P]) for u in range(2 if kind == "gat" else S)]

        hot_ps = [pl.banks[0], pl.banks[2]] if kind == "gat" else [pl.banks[0][:, :].bitcast(BF16)]
        q_ps = [pl.banks[1], pl.banks[2]]
        e_ps = [pl.banks[3], pl.banks[4]]
        small = pl.banks[5]
        alpha_t = small[0:R, 0:P]
        prob_ps, max_ps = small[:, P:P + R], small[:, P + R:P + 2 * R]
        part_ps = [pl.banks[6], pl.banks[7]]

        gathered = [sem.indirect(f"gathered{u}") for u in range(S)]
        q_loaded = [sem(f"q_loaded{u}") for u in range(S)]
        neg_loaded = [sem(f"neg_loaded{u}") for u in range(S)]
        part_stored = [sem(f"part_stored{u}") for u in range(S)]
        idx_ready = sem("idx_ready")
        hot_built = sem("hot_built")
        gap_done = sem("gap_done")
        hot_turned = sem("hot_turned")
        hot_copied = sem("hot_copied")
        hot_cast = sem("hot_cast")
        q_done = sem("q_done")
        q_used = sem("q_used")
        alpha_done = sem("alpha_done")
        alpha_turned = sem("alpha_turned")
        fwd_done, max_done, diff_done = sem("fwd_done"), sem("max_done"), sem("diff_done")
        exp_done = sem("exp_done")
        prob_turned = sem("prob_turned")
        prob_copied = sem("prob_copied")
        msg_done = sem("msg_done")
        part_done = sem("part_done")
        part_copied = sem("part_copied")
        pool_passed, pe_passed = sem("pool_passed"), sem("pe_passed")
        step = sem("score_step")
        STEPS = {"gat": 7, "gatv2": 4}.get(kind, 0)
        if kind in ("gat", "tconv"):
            attr_loaded = [sem(f"attr_loaded{u}") for u in range(S)]
        if kind == "gat":
            attr_stored = [sem(f"attr_stored{u}") for u in range(2)]
            angle_done = sem("angle_done")
            cos_done = sem("cos_done")
            attr_turned = sem("attr_turned")
            attr_copied = sem("attr_copied")
            tail_zeroed = sem("tail_zeroed")
        if kind == "tconv":
            e_used = sem("e_used")
        ring = [(i, i // S, i % S) for i in range(NG + 3)]
        FIRST, LAST = 2 * S, (NG - 3) // S * S

        def bodies(eng, body):
            for i, k, u in ring[:FIRST]:
                body(i, k, u, i)
            with eng.Fori(2, LAST // S) as j:
                for u in range(S):
                    body(j * S + u, j, u, FIRST + u)
            for i, k, u in ring[LAST:]:
                body(i, k, u, i)

        def near(i, k, u, n, d):
            return i + d, k + (u + d) // S, (u + d) % S, n + d

        def has(n, d=0):
            return 0 <= n + d < NG

        with nc.Block() as block:
            @block.sync
            def _(sp):
                window = [sp.alloc_register(sem.name(f"window{t}")) for t in range(G)]

                def load(i, k, u, n):
                    if n >= S:
                        wait(sp, q_done, (i - S + 1) * QB)
                    sp.load(window, pl.window_i[0:1, bass.ds(i * G, G)])
                    for t in range(G):
                        first = sp.snap(window[t], min_val=0, max_val=pl.NP)
                        sp.dma_start(qwin[u][:, t, :], q_tab[bass.ds(first, P), :]).then_inc(q_loaded[u], 16)
                    if n >= S:
                        wait(sp, max_done, i - S + 1)
                    sp.dma_start(neg[u][:, :], pl.neg_tab[H][bass.ds(i * R, R), :]).then_inc(neg_loaded[u], 16)
                    if kind == "tconv":
                        sp.dma_start(attr_t[u][:, :], pl.attr_tab[bass.ds(i * P, P), :]).then_inc(attr_loaded[u], 16)

                def load_messages(i, k, u, n):
                    if n >= S:
                        wait(sp, attr_turned, 2 * (i - S + 1))
                    if n < NG - 1:
                        src_ap = pl.edge_attr[bass.ds(i * (G * P), G * P), :].rearrange("(t p) c -> p t c", p=P)
                        sp.dma_start(attr[u][:, :, 64:D], src_ap).then_inc(attr_loaded[u], 16)
                        return
                    sp.wait_ge(tail_zeroed, 1)
                    base = (NG - 1) * G * P
                    full = (pl.E - base) // P
                    if full:
                        sp.dma_start(attr[u][:, 0:full, 64:D],
                                     pl.edge_attr[base:base + full * P, :].rearrange("(t p) c -> p t c", p=P)
                                     ).then_inc(attr_loaded[u], 16)
                    if pl.E > base + full * P:
                        sp.dma_start(attr[u][0:pl.E - base - full * P, full, 64:D],
                                     pl.edge_attr[base + full * P:pl.E, :]).then_inc(attr_loaded[u], 16)

                def store_parts(i, k, u, n):
                    wait(sp, part_copied, (i + 1) * NPAIR)
                    out = part_tab[bass.ds(i * (G * P), G * P), :].rearrange("(t p) w -> p t w", p=P)
                    sp.dma_start(out, part[u][:, :, :]).then_inc(part_stored[u], 16)

                def store_attr(i, k, u, n):
                    wait(sp, attr_copied, 2 * (i + 1))
                    sp.dma_start(pl.attr_tab[bass.ds(i * P, P), :], attr_t[u % 2][:, :]).then_inc(attr_stored[u % 2], 16)

                def body(*g):
                    n = g[3]
                    if has(n, 2):
                        load(*near(*g, 2))
                    if kind == "gat" and has(n):
                        load_messages(*g)
                    if kind == "gat" and has(n, -3):
                        store_attr(*near(*g, -3))
                    if has(n, -2):
                        store_parts(*near(*g, -2))

                load(0, 0, 0, 0)
                load(1, 0, 1, 1)
                bodies(sp, body)
                for u in range(S):
                    count = len(range(u, NG, S))
                    sp.wait_ge(part_stored[u], 16 * count)
                if kind == "gat":
                    for u in range(2):
                        sp.wait_ge(attr_stored[u], 16 * len(range(u, NG, 2)))

            @block.gpsimd
            def _(pool):
                def gather(i, k, u, n):
                    if n >= S:
                        wait(pool, msg_done, 3 * (i - S + 1))
                    wait(pool, idx_ready, i + 1)
                    settle(pool, pool_passed)
                    for t in range(G):
                        pool.indirect_dma_start(out=rows[u][:, t, :], out_offset=None, in_=tab,
                                                in_offset=bass.IndirectOffsetOnAxis(ap=idx[u][:, t:t + 1], axis=0)
                                                ).then_inc(gathered[u], 16)

                def body(*g):
                    if has(g[3], 2):
                        gather(*near(*g, 2))

                gather(0, 0, 0, 0)
                gather(1, 0, 1, 1)
                bodies(pool, body)

            @block.scalar
            def _(act):
                def indices(i, k, u, n):
                    if n >= S:
                        wait(act, gathered[u], 16 * G * k)
                    act.activation(idx[u][:, :], pl.src_col[:, bass.ds(i * G, G)], ACT.Copy).then_inc(idx_ready, 1)

                def copy_hot(i, k, u, n):
                    wait(act, hot_turned, i + 1)
                    per = G // len(hot_ps)
                    for h, bank in enumerate(hot_ps):
                        ins = act.activation(hot_t[:, h * per:(h + 1) * per, :],
                                             bank[:, 0:per * P].rearrange("p (t e) -> p t e", t=per), ACT.Copy)
                    ins.then_inc(hot_copied, 1)

                def cast_hot(i, k, u, n):
                    wait(act, hot_built, i + 1)
                    if n >= S:
                        wait(act, part_done, NPAIR * (i - S + 1))
                    act.activation(hot[u][:, :, :], hot_b[u % 2][:, :, :], ACT.Copy).then_inc(hot_cast, 1)

                def measure(i, k, u, n, half):
                    if n >= 1:
                        wait(act, hot_built, i)
                    for t in range(half * HALF, (half + 1) * HALF):
                        ins = act.activation(gap[:, t, :], pl.iota_free[:, :], ACT.Abs, scale=-1.0,
                                             bias=pl.rank_col[:, bass.ds(i * G + t, 1)])
                    if half:
                        ins.then_inc(gap_done, 1)

                def build_hot(i, k, u, n):
                    wait(act, gap_done, i + 1)
                    if n >= 2:
                        wait(act, hot_turned, i - 1)
                        wait(act, hot_cast, i - 1)
                    act.activation(hot_b[u % 2][:, :, :], gap[:, :, :], ACT.Relu, scale=-1.0, bias=pl.one[:, 0:1]
                                   ).then_inc(hot_built, 1)

                def exps(i, k, u, n):
                    wait(act, diff_done, i + 1)
                    if n >= 1:
                        wait(act, prob_turned, i)
                    act.activation(prob[:, :], diff[:, :], ACT.Exp, scale=scale).then_inc(exp_done, 1)

                def copy_probs(i, k, u, n):
                    wait(act, prob_turned, i + 1)
                    if n >= 1:
                        wait(act, msg_done, 3 * i)
                    act.activation(pm[:, :], small[:, P:P + 2 * R], ACT.Copy).then_inc(prob_copied, 1)

                def copy_parts(i, k, u, n, c):
                    if n >= S and c == 0:
                        wait(act, part_stored[u], 16 * k)
                    wait(act, part_done, NPAIR * i + c + 1)
                    act.activation(part[u][:, PAIR * c:PAIR * (c + 1), :],
                                   part_ps[c % 2][:, 0:PAIR * W].rearrange("p (t w) -> p t w", t=PAIR), ACT.Copy
                                   ).then_inc(part_copied, 1)

                def cosines(i, k, u, n):
                    wait(act, angle_done, i + 1)
                    if n >= S:
                        wait(act, attr_turned, 2 * (i - S + 1))
                    act.activation(attr[u][:, :, 0:64], ang2[u][:, :, :], ACT.Sin, bias=pl.half_pi[:, 0:1]
                                   ).then_inc(cos_done, 1)

                def copy_attr(i, k, u, n):
                    if n >= 2:
                        wait(act, attr_stored[u % 2], 16 * (2 * k + u // 2))
                    for h in range(2):
                        wait(act, attr_turned, 2 * i + h + 1)
                        act.activation(attr_t[u % 2][:, h * HALF * P:(h + 1) * HALF * P], e_ps[h][:, :], ACT.Copy
                                       ).then_inc(attr_copied, 1)

                def body(*g):
                    u, n = g[2:]
                    if has(n, -1):
                        exps(*near(*g, -1))
                    if act_builds and has(n, 2):
                        measure(*near(*g, 2), 0)
                    if has(n, 1):
                        copy_hot(*near(*g, 1))
                    if has(n, -2):
                        copy_parts(*near(*g, -2), 0)
                        copy_parts(*near(*g, -2), 1)
                    if has(n, -1):
                        copy_probs(*near(*g, -1))
                    if has(n, -2):
                        for c in range(2, NPAIR):
                            copy_parts(*near(*g, -2), c)
                    if kind == "gat" and has(n, -3):
                        copy_attr(*near(*g, -3))
                    if kind != "gat" and has(n, 1):
                        cast_hot(*near(*g, 1))
                    if act_builds and has(n, 2):
                        measure(*near(*g, 2), 1)
                        build_hot(*near(*g, 2))
                    if has(n, 3):
                        indices(*near(*g, 3))
                    if kind == "gat" and u % 2 == 0:
                        for d in (-2, -1):
                            if has(n, d):
                                cosines(*near(*g, d))

                indices(0, 0, 0, 0)
                indices(1, 0, 1, 1)
                indices(2, 0, 2, 2)
                if act_builds:
                    for i in range(2):
                        for half in range(2):
                            measure(i, 0, i, i, half)
                        build_hot(i, 0, i, i)
                copy_hot(0, 0, 0, 0)
                if kind != "gat":
                    cast_hot(0, 0, 0, 0)
                bodies(act, body)

            @block.tensor
            def _(pe):
                def turn_hot(i, k, u, n):
                    wait(pe, hot_built, i + 1)
                    if n >= 1:
                        wait(pe, hot_copied, i)
                    per = G // len(hot_ps)
                    one_hot, ident = (hot[u], pl.ident) if kind == "gat" else (hot_b[u % 2], pl.ident_b)
                    for t in range(G):
                        ins = pe.transpose(hot_ps[t // per][:, t % per * P:(t % per + 1) * P], one_hot[:, t, :], ident[:, :])
                    ins.then_inc(hot_turned, 1)

                def spread(i, k, u, n):
                    wait(pe, hot_copied, i + 1)
                    wait(pe, q_loaded[u], 16 * G * (k + 1))
                    if kind == "tconv":
                        wait(pe, attr_loaded[u], 16 * (k + 1))
                    per = G // QB
                    for h in range(QB):
                        if n >= 1:
                            wait(pe, q_used, QB * (i - 1) + h + 1)
                        if kind == "tconv":
                            if n >= 1:
                                wait(pe, e_used, 2 * (i - 1) + h + 1)
                            for t in range(h * per, (h + 1) * per):
                                pe.matmul(e_ps[h][:, (t - h * per) * D:(t - h * per + 1) * D],
                                          attr_t[u][:, t * P:(t + 1) * P], w["We"][:, :], start=True, stop=True)
                        for t in range(h * per, (h + 1) * per):
                            ins = pe.matmul(q_ps[h][:, (t - h * per) * QW:(t - h * per + 1) * QW], hot_t[:, t, :],
                                            qwin[u][:, t, :], start=True, stop=True)
                        ins.then_inc(q_done, 1)

                def turn_probs(i, k, u, n):
                    wait(pe, exp_done, i + 1)
                    settle(pe, pe_passed)
                    pe.transpose(max_ps, seg_max[:, :], pl.ident[0:R, 0:R])
                    pe.transpose(prob_ps, prob[:, :], pl.ident[0:R, 0:R]).then_inc(prob_turned, 1)

                def turn_alpha(i, k, u, n):
                    wait(pe, alpha_done, QB * (i + 1))
                    if n >= 1:
                        wait(pe, prob_copied, i)
                    settle(pe, pe_passed)
                    pe.transpose(alpha_t, alpha[:, :, :].rearrange("p t h -> p (t h)"), pl.ident[:, :]
                                 ).then_inc(alpha_turned, 1)

                def sum_parts(i, k, u, n, c):
                    if c == 0:
                        if kind != "gat":
                            wait(pe, hot_cast, i + 1)
                        wait(pe, msg_done, 3 * (i + 1))
                    if n >= 1 or c >= 2:
                        wait(pe, part_copied, NPAIR * i + c - 1)
                    for t in range(PAIR):
                        ins = pe.matmul(part_ps[c % 2][:, t * W:(t + 1) * W], hot[u][:, PAIR * c + t, :],
                                        msg[:, PAIR * c + t, :], start=True, stop=True)
                    ins.then_inc(part_done, 1)

                def turn_attr(i, k, u, n):
                    wait(pe, cos_done, i + 1)
                    if n < NG - 1:
                        wait(pe, attr_loaded[u], 16 * (k + 1))
                    else:
                        rest = pl.E - (NG - 1) * G * P
                        wait(pe, attr_loaded[u], 16 * (k + (rest >= P) + (rest % P > 0)))
                    for h in range(2):
                        if n >= 1:
                            wait(pe, attr_copied, 2 * (i - 1) + h + 1)
                        for t in range(HALF):
                            ins = pe.transpose(e_ps[h][:, t * P:(t + 1) * P], attr[u][:, h * HALF + t, :],
                                               pl.ident[:, :])
                        ins.then_inc(attr_turned, 1)

                def body(*g):
                    n = g[3]
                    if has(n, 1):
                        turn_hot(*near(*g, 1))
                    if has(n, -2):
                        sum_parts(*near(*g, -2), 0)
                        sum_parts(*near(*g, -2), 1)
                    if kind == "gat" and has(n, -3):
                        turn_attr(*near(*g, -3))
                    if has(n, -1):
                        turn_probs(*near(*g, -1))
                    if has(n, -2):
                        for c in range(2, NPAIR):
                            sum_parts(*near(*g, -2), c)
                    if has(n):
                        turn_alpha(*g)
                    if has(n, 1):
                        spread(*near(*g, 1))

                turn_hot(0, 0, 0, 0)
                spread(0, 0, 0, 0)
                bodies(pe, body)

            @block.vector
            def _(v):
                def build_hot(i, k, u, n):
                    if kind == "gat":
                        if n >= S:
                            wait(v, part_done, NPAIR * (i - S + 1))
                    elif n >= 2:
                        wait(v, hot_turned, i - 1)
                        wait(v, hot_cast, i - 1)
                    out = hot[u] if kind == "gat" else hot_b[u % 2]
                    v.tensor_tensor(out[:, :, :], bc(pl.iota_free[:, :].unsqueeze(1), [P, G, P]),
                                    bc(pl.rank_col[:, bass.ds(i * G, G)].unsqueeze(2), [P, G, P]),
                                    ALU.is_equal).then_inc(hot_built, 1)

                def maxima(i, k, u, n):
                    wait(v, alpha_turned, i + 1)
                    wait(v, neg_loaded[u], 16 * (k + 1))
                    v.tensor_tensor_scan(fwd[:, :], neg[u][:, 0:P], alpha_t, 0.0, ALU.add, ALU.max).then_inc(fwd_done, 1)
                    wait(v, fwd_done, i + 1)
                    if n >= 1:
                        wait(v, prob_turned, i)
                    v.tensor_tensor_scan(seg_max[:, ::-1], neg[u][:, 2 * P - 1:P - 1:-1], fwd[:, ::-1], 0.0,
                                         ALU.add, ALU.max).then_inc(max_done, 1)
                    wait(v, max_done, i + 1)
                    if n >= 1:
                        wait(v, exp_done, i)
                    v.tensor_tensor(diff[:, :], alpha_t, seg_max[:, :], ALU.subtract).then_inc(diff_done, 1)

                def stepper(i):
                    at = [0]

                    def then(ins):
                        at[0] += 1
                        ins.then_inc(step, 1)
                        wait(v, step, i * STEPS + at[0])

                    return then

                def scores(i, k, u, n):
                    wait(v, gathered[u], 16 * G * (k + 1))
                    if n >= 1:
                        wait(v, alpha_turned, i)
                    if kind == "gat":
                        wait(v, q_done, i + 1)
                        s = prod[0][:, 0, 0:G * H].rearrange("p (t h) -> p t h", h=H)
                        v.tensor_tensor(s, q_ps[0][:, 0:G * H].rearrange("p (t h) -> p t h", h=H),
                                        rows[u][:, :, D:D + H], ALU.add).then_inc(q_used, 1)
                        wait(v, q_used, i + 1)
                        v.scalar_tensor_tensor(alpha[:, :, :], s, 0.01, s, ALU.mult, ALU.max).then_inc(alpha_done, 1)
                        return
                    then = stepper(i)
                    for h in range(2):
                        wait(v, q_done, 2 * i + h + 1)
                        t0, t1 = h * HALF, (h + 1) * HALF
                        q = q_ps[h][:, :].rearrange("p (t d) -> p t d", t=HALF)
                        if kind == "tconv":
                            e = e_ps[h][:, :].rearrange("p (t d) -> p t d", t=HALF)
                            kv = rows[u][:, t0:t1, :].rearrange("p t (a d) -> p t a d", a=2)
                            v.tensor_tensor(kv, kv, bc(e.unsqueeze(2), [P, HALF, 2, D]), ALU.add).then_inc(e_used, 1)
                            wait(v, e_used, 2 * i + h + 1)
                        if kind == "gatv2":
                            v.tensor_tensor(prod[h][:, :, :], q, rows[u][:, t0:t1, :], ALU.add).then_inc(q_used, 1)
                            wait(v, q_used, 2 * i + h + 1)
                            flat = prod[h][:, :, :].rearrange("p t d -> p (t d)")
                            then(v.scalar_tensor_tensor(flat, flat, 0.2, flat, ALU.mult, ALU.max))
                            then(v.tensor_tensor(prod[h][:, :, :], prod[h][:, :, :],
                                                 bc(w["att"][:, :].unsqueeze(1), [P, HALF, D]), ALU.mult))
                        else:
                            v.tensor_tensor(prod[h][:, :, :], q, rows[u][:, t0:t1, 0:D], ALU.mult).then_inc(q_used, 1)
                            wait(v, q_used, 2 * i + h + 1)
                        v.tensor_reduce(alpha[:, t0:t1, :], prod[h][:, :, :].rearrange("p t (h c) -> p t h c", c=C),
                                        AX.X, ALU.add).then_inc(alpha_done, 1)

                def angles(i, k, u, n):
                    then = stepper(i)
                    fl = "p t c -> p (t c)"
                    a, tn = ang[:, :, :].rearrange(fl), turns[:, :, :].rearrange(fl)
                    then(v.tensor_tensor(rel[:, :], rows[u][:, :, D + H], pl.weight_col[:, bass.ds(i * G, G)], ALU.subtract))
                    then(v.tensor_tensor(ang[:, :, :], bc(rel[:, :].unsqueeze(2), [P, G, 64]),
                                         bc(w["Wt"][:, :].unsqueeze(1), [P, G, 64]), ALU.mult))
                    then(v.tensor_tensor(ang[:, :, :], ang[:, :, :], bc(w["bt"][:, :].unsqueeze(1), [P, G, 64]), ALU.add))
                    then(v.tensor_scalar(tn, a, float(1 / (2 * np.pi)), MAGIC, ALU.mult, ALU.add))
                    then(v.tensor_scalar(tn, tn, MAGIC, None, ALU.subtract))
                    then(v.scalar_tensor_tensor(a, tn, -TWO_PI_HIGH, a, ALU.mult, ALU.add))
                    then(v.scalar_tensor_tensor(a, tn, -TWO_PI_LOW, a, ALU.mult, ALU.add))
                    if n >= S:
                        wait(v, cos_done, i - S + 1)
                    v.scalar_tensor_tensor(ang2[u][:, :, :].rearrange(fl), a, -1.0, a, ALU.mult, ALU.min
                                           ).then_inc(angle_done, 1)

                def messages(i, k, u, n):
                    wait(v, prob_copied, i + 1)
                    if n >= 1:
                        wait(v, part_done, NPAIR * i)
                    vals = rows[u][:, :, TW - D:TW] if kind in ("tconv", "mha") else rows[u][:, :, 0:D]
                    p = pm[:, 0:R].rearrange("p (t h) -> p t h", h=H)
                    v.tensor_copy(msg[:, :, D:D + H], p).then_inc(msg_done, 1)
                    v.tensor_tensor(msg[:, :, 0:D].rearrange("p t (h c) -> p t h c", c=C),
                                    vals.rearrange("p t (h c) -> p t h c", c=C),
                                    bc(p.unsqueeze(3), [P, G, H, C]), ALU.mult).then_inc(msg_done, 1)
                    v.tensor_tensor(msg[:, :, D + H:W], pm[:, R:2 * R].rearrange("p (t h) -> p t h", h=H),
                                    bc(pl.last_col[:, bass.ds(i * G, G)].unsqueeze(2), [P, G, H]), ALU.mult
                                    ).then_inc(msg_done, 1)

                def body(*g):
                    n = g[3]
                    if has(n, -1):
                        maxima(*near(*g, -1))
                    if has(n):
                        scores(*g)
                    if kind == "gat":
                        if has(n):
                            angles(*g)
                        if n == NG - 1:
                            v.wait_ge(attr_turned, 2 * (NG - S))
                            v.memset(attr[(NG - 1) % S][:, :, 64:D], 0.0).then_inc(tail_zeroed, 1)
                    if has(n, -1):
                        messages(*near(*g, -1))
                    if not act_builds and has(n, 2):
                        build_hot(*near(*g, 2))

                if not act_builds:
                    build_hot(0, 0, 0, 0)
                    build_hot(1, 0, 1, 1)
                bodies(v, body)
        sem.close()



def merge_parts(nc, pl, sems, H, scale, att):
    sem = Stage(nc, sems)
    TB, NB = pl.TB, pl.NB
    W = D + 2 * H
    C = D // H
    NT = TB * P
    HALVES = ((0, 4), (4, TB))
    head = pl.head8 if H == 8 else pl.head4
    part_tab, carry_tab = pl.part_tab[H], pl.carry_tab[H]
    with ExitStack() as ctx:
        def sb(name, shape, dt=F32):
            return sem.tensor(ctx, name, shape, dt)

        last_rows = sb("last_rows", [P, TB, W])
        num, num_run = sb("num", [P, NT]), sb("num_run", [P, NT])
        den, den_run = sb("den", [H, NT]), sb("den_run", [H, NT])
        top = sb("top", [H, NT])
        top_run = sb("top_run", [H, 1 + NT])
        keep, take = sb("keep", [H, NT]), sb("take", [H, NT])
        keep_e, take_e = sb("keep_e", [H, NT]), sb("take_e", [H, NT])
        carry = sb("carry", [P, TB, W])
        own = sb("own", [P, NB, W])
        run = sb("run", [P, NB, W])
        m_run, m_all = sb("m_run", [P, NB, H]), sb("m_all", [P, NB, H])
        d_own, d_run = sb("d_own", [P, NB, H]), sb("d_run", [P, NB, H])
        f_own, f_run = sb("f_own", [P, NB, H]), sb("f_run", [P, NB, H])
        s_own, s_run = sb("s_own", [P, NB, H]), sb("s_run", [P, NB, H])
        last_got, own_got, run_got = sem.indirect("last_gathered"), sem.indirect("own_gathered"), sem.indirect("run_gathered")
        turned, copied = sem("turned"), sem("copied")
        args_ready, exps_ready, spread = sem("args_ready"), sem("exps_ready"), sem("spread")
        carried, back, back_copied, stored = sem("carried"), sem("back"), sem("back_copied"), sem("carry_stored")
        node_args, node_exps = sem("node_args"), sem("node_exps")
        dve = sem("dve")
        ps = pl.banks

        with nc.Block() as block:
            @block.gpsimd
            def _(pool):
                for g in range(TB):
                    pool.indirect_dma_start(out=last_rows[:, g, :], out_offset=None, in_=part_tab,
                                            in_offset=bass.IndirectOffsetOnAxis(ap=pl.tile_last_i[:, g:g + 1], axis=0)
                                            ).then_inc(last_got, 16)
                for b in range(NB):
                    pool.indirect_dma_start(out=own[:, b, :], out_offset=None, in_=part_tab,
                                            in_offset=bass.IndirectOffsetOnAxis(ap=pl.part_i[:, b:b + 1], axis=0)
                                            ).then_inc(own_got, 16)
                pool.wait_ge(stored, 16)
                for b in range(NB):
                    pool.indirect_dma_start(out=run[:, b, :], out_offset=None, in_=carry_tab,
                                            in_offset=bass.IndirectOffsetOnAxis(ap=pl.carry_i[:, b:b + 1], axis=0)
                                            ).then_inc(run_got, 16)

            @block.sync
            def _(sp):
                sp.wait_ge(back_copied, 2 + 2 * TB)
                sp.dma_start(carry_tab.rearrange("(g p) w -> p g w", p=P), carry[:, :, :]).then_inc(stored, 16)
                sp.wait_ge(stored, 16)

            @block.tensor
            def _(pe):
                pe.wait_ge(last_got, 16 * TB)
                for lo, hi, rows, bank in ((0, D, P, 0), (D, D + H, H, 2), (D + H, W, H, 4)):
                    for half, (a, b) in enumerate(HALVES):
                        for g in range(a, b):
                            ins = pe.transpose(ps[bank + half][0:rows, (g - a) * P:(g - a + 1) * P],
                                               last_rows[:, g, lo:hi], pl.ident[:, :])
                        ins.then_inc(turned, 1)
                pe.wait_ge(exps_ready, 2)
                pe.wait_ge(copied, 6)
                for f, bank in ((keep_e, 0), (take_e, 2)):
                    for half, (a, b) in enumerate(HALVES):
                        pe.matmul(ps[bank + half][:, 0:(b - a) * P], head[0:H, :], f[:, a * P:b * P], start=True, stop=True
                                  ).then_inc(spread, 1)
                pe.wait_ge(carried, 2)
                for half, (a, b) in enumerate(HALVES):
                    for g in range(a, b):
                        ins = pe.transpose(ps[4 + half][:, (g - a) * P:(g - a + 1) * P], num_run[:, g * P:(g + 1) * P],
                                           pl.ident[:, :])
                    ins.then_inc(back, 1)
                for g in range(TB):
                    pe.transpose(ps[6][:, 2 * g * H:(2 * g + 1) * H], den_run[:, g * P:(g + 1) * P], pl.ident[0:H, 0:H])
                    ins = pe.transpose(ps[6][:, (2 * g + 1) * H:(2 * g + 2) * H], top_run[:, 1 + g * P:1 + (g + 1) * P],
                                       pl.ident[0:H, 0:H])
                ins.then_inc(back, 1)

            @block.scalar
            def _(act):
                n = 0
                for out, rows, bank in ((num, P, 0), (den, H, 2), (top, H, 4)):
                    for half, (a, b) in enumerate(HALVES):
                        n += 1
                        act.wait_ge(turned, n)
                        act.activation(out[:, a * P:b * P], ps[bank + half][0:rows, 0:(b - a) * P], ACT.Copy
                                       ).then_inc(copied, 1)
                act.wait_ge(args_ready, 1)
                act.activation(keep_e[:, :], keep[:, :], ACT.Exp, scale=scale).then_inc(exps_ready, 1)
                act.activation(take_e[:, :], take[:, :], ACT.Exp, scale=scale).then_inc(exps_ready, 1)
                for half, (a, b) in enumerate(HALVES):
                    act.wait_ge(back, half + 1)
                    act.activation(carry[:, a:b, 0:D], ps[4 + half][:, 0:(b - a) * P].rearrange("p (g d) -> p g d", d=D),
                                   ACT.Copy).then_inc(back_copied, 1)
                act.wait_ge(back, 3)
                for g in range(TB):
                    for k in range(2):
                        act.activation(carry[:, g, D + k * H:D + (k + 1) * H], ps[6][:, (2 * g + k) * H:(2 * g + k + 1) * H],
                                       ACT.Copy).then_inc(back_copied, 1)
                act.wait_ge(node_args, 1)
                act.activation(f_own[:, :, :], d_own[:, :, :], ACT.Exp, scale=scale).then_inc(node_exps, 1)
                act.activation(f_run[:, :, :], d_run[:, :, :], ACT.Exp, scale=scale).then_inc(node_exps, 1)

            @block.vector
            def _(v):
                link = chain(v, dve)
                link(v.memset(top_run[:, 0:1], 0.0))
                v.wait_ge(copied, 6)
                link(v.tensor_tensor_scan(top_run[:, 1:1 + NT], pl.whole_pen[0:H, :], top[:, :], 0.0, ALU.add, ALU.max))
                link(v.tensor_tensor(keep[:, :], top_run[:, 0:NT], pl.whole_pen[0:H, :], ALU.add))
                link(v.tensor_tensor(keep[:, :], keep[:, :], top_run[:, 1:1 + NT], ALU.subtract))
                v.tensor_tensor(take[:, :], top[:, :], top_run[:, 1:1 + NT], ALU.subtract).then_inc(args_ready, 1)
                v.wait_ge(exps_ready, 2)
                link(v.tensor_tensor(den[:, :], den[:, :], take_e[:, :], ALU.mult))
                v.tensor_tensor_scan(den_run[:, :], keep_e[:, :], den[:, :], 0.0, ALU.mult, ALU.add).then_inc(carried, 1)
                v.wait_ge(spread, 4)
                for half, (a, b) in enumerate(HALVES):
                    link(v.tensor_tensor(num[:, a * P:b * P], num[:, a * P:b * P], ps[2 + half][:, 0:(b - a) * P], ALU.mult))
                a = HALVES[0][1] * P
                link(v.tensor_tensor_scan(num_run[:, 0:a], ps[0][:, 0:a], num[:, 0:a], 0.0, ALU.mult, ALU.add))
                v.tensor_tensor_scan(num_run[:, a:NT], ps[1][:, 0:NT - a], num[:, a:NT], num_run[:, a - 1:a],
                                     ALU.mult, ALU.add).then_inc(carried, 1)
                v.wait_ge(own_got, 16 * NB)
                v.wait_ge(run_got, 16 * NB)
                link(v.tensor_tensor(m_run[:, :, :], run[:, :, D + H:W],
                                     bc(pl.carry_pen[:, :].unsqueeze(2), [P, NB, H]), ALU.add))
                link(v.tensor_tensor(m_all[:, :, :], own[:, :, D + H:W], m_run[:, :, :], ALU.max))
                v.tensor_tensor(d_own[:, :, :], own[:, :, D + H:W], m_all[:, :, :], ALU.subtract)
                v.tensor_tensor(d_run[:, :, :], m_run[:, :, :], m_all[:, :, :], ALU.subtract).then_inc(node_args, 1)
                v.wait_ge(node_exps, 2)
                v.tensor_tensor(s_own[:, :, :], own[:, :, D:D + H], f_own[:, :, :], ALU.mult)
                link(v.tensor_tensor(s_run[:, :, :], run[:, :, D:D + H], f_run[:, :, :], ALU.mult))
                link(v.tensor_tensor(s_own[:, :, :], s_own[:, :, :], s_run[:, :, :], ALU.add))
                link(v.tensor_scalar(s_own[:, :, :], s_own[:, :, :], TINY, None, ALU.max))
                link(v.reciprocal(s_run[:, :, :], s_own[:, :, :]))
                link(v.tensor_tensor(s_run[:, :, :], s_run[:, :, :],
                                     bc(pl.has_edges[:, :].unsqueeze(2), [P, NB, H]), ALU.mult))
                v.tensor_tensor(f_own[:, :, :], f_own[:, :, :], s_run[:, :, :], ALU.mult)
                link(v.tensor_tensor(f_run[:, :, :], f_run[:, :, :], s_run[:, :, :], ALU.mult))
                for b in range(NB):
                    o = att[:, b, :].rearrange("p (h c) -> p h c", c=C)
                    r = run[:, b, 0:D].rearrange("p (h c) -> p h c", c=C)
                    v.tensor_tensor(o, own[:, b, 0:D].rearrange("p (h c) -> p h c", c=C),
                                    bc(f_own[:, b, :].unsqueeze(2), [P, H, C]), ALU.mult)
                    ins = v.tensor_tensor(r, r, bc(f_run[:, b, :].unsqueeze(2), [P, H, C]), ALU.mult)
                link(ins)
                link(v.tensor_tensor(att[:, :, :], att[:, :, :], run[:, :, 0:D], ALU.add))
        sem.close()



class Norm:

    def __init__(self, nc, ctx, pl, sem):
        def sb(name, shape):
            return sem.tensor(ctx, "ln_" + name, shape, F32)

        self.pl = pl
        self.square = sb("square", [P, pl.NB, D])
        self.mean, self.var, self.std = sb("mean", [P, pl.NB]), sb("var", [P, pl.NB]), sb("std", [P, pl.NB])
        self.var_ready, self.std_ready = sem("var_ready"), sem("std_ready")
        self.count = 0

    def roots(self, act, n):
        for k in range(n):
            act.wait_ge(self.var_ready, k + 1)
            act.activation(self.std[:, :], self.var[:, :], ACT.Sqrt, bias=self.pl.eps[:, 0:1], scale=1.0 / D
                           ).then_inc(self.std_ready, 1)

    def apply(self, v, link, out, x):
        shape = [P, self.pl.NB, D]
        link(v.tensor_reduce(self.mean[:, :], x, AX.X, ALU.add))
        link(v.tensor_scalar(self.mean[:, :], self.mean[:, :], 1.0 / D, None, ALU.mult))
        link(v.tensor_tensor(out, x, bc(self.mean[:, :].unsqueeze(2), shape), ALU.subtract))
        link(v.tensor_tensor(self.square[:, :, :], out, out, ALU.mult))
        v.tensor_reduce(self.var[:, :], self.square[:, :, :], AX.X, ALU.add).then_inc(self.var_ready, 1)
        self.count += 1
        v.wait_ge(self.std_ready, self.count)
        link(v.reciprocal(self.std[:, :], self.std[:, :]))
        link(v.tensor_tensor(out, out, bc(self.std[:, :].unsqueeze(2), shape), ALU.mult))


def norm_input(nc, pl, sems):
    sem = Stage(nc, sems)
    with ExitStack() as ctx:
        norm = Norm(nc, ctx, pl, sem)
        dve = sem("dve")
        with nc.Block() as block:
            @block.scalar
            def _(act):
                norm.roots(act, 1)

            @block.vector
            def _(v):
                link = chain(v, dve)
                norm.apply(v, link, pl.hn[:, :, :], pl.x_sb[:, :, :])
                link(v.tensor_scalar(pl.hn[:, :, :], pl.hn[:, :, :], 0.0, None, ALU.max))
        sem.close()


def project(nc, pl, sems, weights, biases, dest, gat=None):
    sem = Stage(nc, sems)
    NB = pl.NB
    n_out = len(weights)
    cols = [d for d in dest if d in ("k", "v", "xl", "z")]
    TW = D + 16 if gat else D * len(cols)
    table = pl.gat_tab if gat else (pl.kv_tab if len(cols) == 2 else pl.xl_tab)
    with ExitStack() as ctx:
        def sb(name, shape, dt=F32):
            return sem.tensor(ctx, name, shape, dt)

        wcat = sb("wcat", [P, n_out * D])
        flag = sb("flag", [P, 1])
        bias = sb("bias", [P, n_out * D])
        hb = [sb(f"hb{u}", [P, P]) for u in range(2)]
        ht = [sb(f"ht{u}", [P, P]) for u in range(2)]
        q_rows = sb("q_rows", [P, NB, 8 if gat else D])
        t_rows = sb("t_rows", [P, NB, TW])
        if gat:
            a_l, a_r, prod = sb("a_l", [P, D]), sb("a_r", [P, D]), sb("prod", [P, NB, D])
        loaded, stored, scattered = sem("loaded"), sem("stored"), sem.indirect("scattered")
        block_ready = [sem(f"block_ready{u}") for u in range(2)]
        turned = [sem(f"turned{u}") for u in range(2)]
        turned_copied = [sem(f"turned_copied{u}") for u in range(2)]
        multiplied = [sem(f"multiplied{u}") for u in range(2)]
        written = [sem(f"written{u}") for u in range(2)]
        dve, tables_ready = sem("dve"), sem("tables_ready")
        n_loads = n_out + sum(b is not None for b in biases) + (2 if gat else 0)
        place = {"q": (q_rows, 0), "res": (pl.res, 0), "k": (t_rows, 0), "xl": (t_rows, 0), "z": (t_rows, 0), "v": (t_rows, D)}

        def target(d, b):
            t, lo = place[d]
            return t[:, bass.ds(b, 1), lo:lo + D].rearrange("p a d -> p (a d)")

        with nc.Block() as block:
            @block.sync
            def _(sp):
                for n, wt in enumerate(weights):
                    out = wcat[:, n * D:(n + 1) * D]
                    if len(wt.shape) == 3:
                        out = out.rearrange("d (h k) -> d h k", h=wt.shape[0])
                        wt = wt.rearrange("h d k -> d h k")
                    sp.dma_start(out, wt).then_inc(loaded, 16)
                for n, b in enumerate(biases):
                    if b is not None:
                        sp.dma_start(bias[:, n * D:(n + 1) * D], b.partition_broadcast(P)).then_inc(loaded, 16)
                if gat:
                    for t, a in ((a_l, gat[0]), (a_r, gat[1])):
                        sp.dma_start(t[:, :], a.rearrange("h k -> (h k)").partition_broadcast(P)).then_inc(loaded, 16)
                sp.wait_ge(tables_ready, 1)
                sp.dma_start(table.rearrange("(b p) w -> p b w", p=P), t_rows[:, :, :]).then_inc(stored, 16)
                sp.wait_ge(stored, 16)

            @block.gpsimd
            def _(pool):
                pool.wait_ge(tables_ready, 1)
                q_tab = pl.er_tab if gat else pl.q_tab
                for b in range(NB):
                    pool.indirect_dma_start(out=q_tab, out_offset=bass.IndirectOffsetOnAxis(
                        ap=pl.compact_i[:, b:b + 1], axis=0), in_=q_rows[:, b, :], in_offset=None).then_inc(scattered, 16)
                pool.wait_ge(scattered, 16 * NB)

            @block.scalar
            def _(act):
                def pair(j):
                    for u in range(2):
                        wait(act, turned[u], j)
                        act.activation(hb[u][:, :], pl.hn[:, bass.ds(j * 2 + u, 1), :].rearrange("p a d -> p (a d)"),
                                       ACT.Copy).then_inc(block_ready[u], 1)
                    for u in range(2):
                        wait(act, turned[u], j + 1)
                        wait(act, multiplied[u], j)
                        act.activation(ht[u][:, :], pl.banks[u][:, 0:P], ACT.Copy).then_inc(turned_copied[u], 1)

                pairs(act, pair, NB // 2)

            @block.tensor
            def _(pe):
                pe.wait_ge(loaded, 16 * n_loads)
                def pair(j):
                    for u in range(2):
                        wait(pe, block_ready[u], j + 1)
                        wait(pe, turned_copied[u], j)
                        pe.transpose(pl.banks[u][:, 0:P], hb[u][:, :], pl.ident[:, :]).then_inc(turned[u], 1)
                    for u in range(2):
                        wait(pe, turned_copied[u], j + 1)
                        wait(pe, written[u], j * n_out)
                        pe.matmul(pl.banks[2 + u][:, 0:n_out * D], ht[u][:, :], wcat[:, :], start=True, stop=True
                                  ).then_inc(multiplied[u], 1)

                pairs(pe, pair, NB // 2)

            @block.vector
            def _(v):
                link = chain(v, dve)
                if gat:
                    v.memset(t_rows[:, :, D + 9:TW], 0.0)
                v.wait_ge(loaded, 16 * n_loads)
                def pair(j):
                    for u in range(2):
                        wait(v, multiplied[u], j + 1)
                        for n, (d, b) in enumerate(zip(dest, biases)):
                            got = pl.banks[2 + u][:, n * D:(n + 1) * D]
                            if b is None:
                                ins = v.tensor_copy(target(d, j * 2 + u), got)
                            else:
                                ins = v.tensor_tensor(target(d, j * 2 + u), got, bias[:, n * D:(n + 1) * D], ALU.add)
                            ins.then_inc(written[u], 1)

                pairs(v, pair, NB // 2)
                for u in range(2):
                    v.wait_ge(written[u], NB // 2 * n_out)
                if gat:
                    H, K = gat[0].shape
                    for t, a, out in ((t_rows, a_l, t_rows[:, :, D:D + H]), (t_rows, a_r, q_rows[:, :, :])):
                        link(v.tensor_tensor(prod[:, :, :], t[:, :, 0:D], bc(a[:, :].unsqueeze(1), [P, NB, D]), ALU.mult))
                        link(v.tensor_reduce(out, prod[:, :, :].rearrange("p b (h k) -> p b h k", k=K), AX.X, ALU.add))
                    link(v.tensor_copy(t_rows[:, :, D + H], pl.node_vec_sb[:, :]))
                    link(v.tensor_copy(pl.res[:, :, :], pl.hn[:, :, :]))
                v.memset(flag[:, :], 1.0).then_inc(tables_ready, 1)
        sem.close()


def feed_forward(nc, pl, sems, att, gamma, beta, W1, b1, W2, b2):
    sem = Stage(nc, sems)
    NB = pl.NB
    CH = W1.shape[1] // P
    with ExitStack() as ctx:
        def sb(name, shape, dt=F32):
            return sem.tensor(ctx, name, shape, dt)

        norm = Norm(nc, ctx, pl, sem)
        g_row, be_row, b2_row = sb("g_row", [P, D]), sb("be_row", [P, D]), sb("b2_row", [P, D])
        w1 = sb("w1", [P, CH * P])
        w2 = sb("w2", [P, CH, D])
        b1_col = sb("b1_col", [P, CH])
        below = sb("below", [P, NB, D])
        e = sb("e", [P, NB, D])
        hb = [sb(f"hb{u}", [P, P]) for u in range(2)]
        ht = [sb(f"ht{u}", [P, P]) for u in range(2)]
        inter = [sb(f"inter{u}", [P, CH, P]) for u in range(2)]
        loaded, min_ready, exp_ready, normed, dve = sem("loaded"), sem("min_ready"), sem("exp_ready"), sem("normed"), sem("dve")
        block_ready = [sem(f"block_ready{u}") for u in range(2)]
        turned = [sem(f"turned{u}") for u in range(2)]
        turned_copied = [sem(f"turned_copied{u}") for u in range(2)]
        hidden = [sem(f"hidden{u}") for u in range(2)]
        hidden_used = [sem(f"hidden_used{u}") for u in range(2)]
        multiplied = [sem(f"multiplied{u}") for u in range(2)]
        written = [sem(f"written{u}") for u in range(2)]
        shape = [P, NB, D]
        with nc.Block() as block:
            @block.sync
            def _(sp):
                for t, a in ((g_row, gamma), (be_row, beta), (b2_row, b2)):
                    sp.dma_start(t[:, :], a.partition_broadcast(P)).then_inc(loaded, 16)
                sp.dma_start(w1[:, :], W1).then_inc(loaded, 16)
                sp.dma_start(w2[:, :, :], W2.rearrange("(c p) n -> p c n", p=P)).then_inc(loaded, 16)
                sp.dma_start(b1_col[:, :], b1.rearrange("(c p) -> p c", p=P), allow_slow_non_contiguous=True).then_inc(loaded, 16)
                sp.wait_ge(loaded, 96)

            @block.scalar
            def _(act):
                act.wait_ge(min_ready, 1)
                act.activation(e[:, :, :], below[:, :, :], ACT.Exp).then_inc(exp_ready, 1)
                norm.roots(act, 1)
                act.wait_ge(loaded, 96)
                act.wait_ge(normed, 1)
                def pair(j):
                    for u in range(2):
                        wait(act, turned[u], j)
                        act.activation(hb[u][:, :], pl.hn[:, bass.ds(j * 2 + u, 1), :].rearrange("p a d -> p (a d)"),
                                       ACT.Copy).then_inc(block_ready[u], 1)
                    for u in range(2):
                        wait(act, turned[u], j + 1)
                        wait(act, hidden[u], j)
                        act.activation(ht[u][:, :], pl.banks[u][:, 0:P], ACT.Copy).then_inc(turned_copied[u], 1)
                    for u in range(2):
                        wait(act, hidden[u], j + 1)
                        wait(act, multiplied[u], j)
                        for c in range(CH):
                            act.activation(inter[u][:, c, :], pl.banks[2 + u][:, c * P:(c + 1) * P], ACT.Relu,
                                           bias=b1_col[:, c:c + 1]).then_inc(hidden_used[u], 1)

                pairs(act, pair, NB // 2)

            @block.tensor
            def _(pe):
                pe.wait_ge(loaded, 96)
                def pair(j):
                    for u in range(2):
                        wait(pe, block_ready[u], j + 1)
                        wait(pe, turned_copied[u], j)
                        pe.transpose(pl.banks[u][:, 0:P], hb[u][:, :], pl.ident[:, :]).then_inc(turned[u], 1)
                    for u in range(2):
                        wait(pe, turned_copied[u], j + 1)
                        wait(pe, hidden_used[u], j * CH)
                        for c in range(CH):
                            ins = pe.matmul(pl.banks[2 + u][:, c * P:(c + 1) * P], w1[:, c * P:(c + 1) * P], ht[u][:, :],
                                            start=True, stop=True)
                        ins.then_inc(hidden[u], 1)
                    for u in range(2):
                        wait(pe, hidden_used[u], j * CH + CH)
                        wait(pe, written[u], j)
                        for c in range(CH):
                            ins = pe.matmul(pl.banks[4 + u][:, 0:D], inter[u][:, c, :], w2[:, c, :],
                                            start=(c == 0), stop=(c == CH - 1))
                        ins.then_inc(multiplied[u], 1)

                pairs(pe, pair, NB // 2)

            @block.vector
            def _(v):
                link = chain(v, dve)
                v.tensor_scalar(below[:, :, :], att[:, :, :], 0.0, None, ALU.min).then_inc(min_ready, 1)
                link(v.tensor_scalar(att[:, :, :], att[:, :, :], 0.0, None, ALU.max))
                link(v.tensor_tensor(att[:, :, :], att[:, :, :], pl.res[:, :, :], ALU.add))
                v.wait_ge(exp_ready, 1)
                f = "p b d -> p (b d)"
                link(v.scalar_tensor_tensor(att[:, :, :].rearrange(f), e[:, :, :].rearrange(f), -1.0,
                                            att[:, :, :].rearrange(f), ALU.add, ALU.add))
                norm.apply(v, link, pl.hn[:, :, :], att[:, :, :])
                v.wait_ge(loaded, 96)
                link(v.tensor_tensor(pl.hn[:, :, :], pl.hn[:, :, :], bc(g_row[:, :].unsqueeze(1), shape), ALU.mult))
                v.tensor_tensor(pl.hn[:, :, :], pl.hn[:, :, :], bc(be_row[:, :].unsqueeze(1), shape), ALU.add
                                ).then_inc(normed, 1)
                link(v.tensor_tensor(att[:, :, :], att[:, :, :], bc(b2_row[:, :].unsqueeze(1), shape), ALU.add))
                link(v.tensor_tensor(pl.x_sb[:, :, :], pl.x_sb[:, :, :], att[:, :, :], ALU.add))
                def pair(j):
                    for u in range(2):
                        wait(v, multiplied[u], j + 1)
                        o = pl.x_sb[:, bass.ds(j * 2 + u, 1), :].rearrange("p a d -> p (a d)")
                        v.tensor_tensor(o, o, pl.banks[4 + u][:, 0:D], ALU.add).then_inc(written[u], 1)

                pairs(v, pair, NB // 2)
                for u in range(2):
                    v.wait_ge(written[u], NB // 2)
        sem.close()


def add_residual(nc, pl, sems, att, to_stream, bias=None, norm_by=None):
    sem = Stage(nc, sems)
    NB = pl.NB
    shape = [P, NB, D]
    with ExitStack() as ctx:
        def sb(name, shape):
            return sem.tensor(ctx, name, shape, F32)

        dve, loaded = sem("dve"), sem("loaded")
        norm = Norm(nc, ctx, pl, sem) if norm_by else None
        rows = [sb(f"row{n}", [P, D]) for n in range(3)] if norm_by else []
        with nc.Block() as block:
            if norm_by:
                @block.sync
                def _(sp):
                    for t, a in zip(rows, (bias,) + norm_by):
                        sp.dma_start(t[:, :], a.partition_broadcast(P)).then_inc(loaded, 16)
                    sp.wait_ge(loaded, 48)

                @block.scalar
                def _(act):
                    norm.roots(act, 1)

            @block.vector
            def _(v):
                link = chain(v, dve)
                if norm_by:
                    v.wait_ge(loaded, 48)
                    r = [bc(t[:, :].unsqueeze(1), shape) for t in rows]
                    link(v.tensor_tensor(att[:, :, :], att[:, :, :], r[0], ALU.add))
                    link(v.tensor_scalar(att[:, :, :], att[:, :, :], 0.0, None, ALU.max))
                    norm.apply(v, link, pl.hn[:, :, :], att[:, :, :])
                    link(v.tensor_tensor(pl.hn[:, :, :], pl.hn[:, :, :], r[1], ALU.mult))
                    link(v.tensor_tensor(pl.hn[:, :, :], pl.hn[:, :, :], r[2], ALU.add))
                    if to_stream:
                        link(v.tensor_tensor(pl.x_sb[:, :, :], pl.x_sb[:, :, :], pl.hn[:, :, :], ALU.add))
                elif to_stream:
                    link(v.tensor_tensor(att[:, :, :], att[:, :, :], pl.res[:, :, :], ALU.add))
                    link(v.tensor_tensor(pl.x_sb[:, :, :], pl.x_sb[:, :, :], att[:, :, :], ALU.add))
                else:
                    link(v.tensor_tensor(pl.hn[:, :, :], att[:, :, :], pl.res[:, :, :], ALU.add))
        sem.close()


def load_sweep_weights(nc, sems, ctx, pieces):
    sem = Stage(nc, sems)
    loaded = sem("loaded")
    out = {}
    for name, ap in pieces.items():
        shape = list(ap.shape) if len(ap.shape) == 2 else [P, ap.shape[0]]
        out[name] = ctx.enter_context(nc.sbuf_tensor(f"s{sem.number}_{name}", shape, F32))
    with nc.Block() as block:
        @block.sync
        def _(sp):
            for name, ap in pieces.items():
                sp.dma_start(out[name][:, :], ap if len(ap.shape) == 2 else ap.partition_broadcast(P)
                             ).then_inc(loaded, 16)
            sp.wait_ge(loaded, 16 * len(pieces))
    sem.close()
    return out


def store_output(nc, pl, sems, out):
    sem = Stage(nc, sems)
    stored = sem("stored")
    full = pl.N // P
    with nc.Block() as block:
        @block.sync
        def _(sp):
            sp.dma_start(out[0:full * P, :].rearrange("(b p) c -> p b c", p=P), pl.x_sb[:, 0:full, :]).then_inc(stored, 16)
            sp.dma_start(out[full * P:pl.N, :], pl.x_sb[0:pl.N - full * P, full, :]).then_inc(stored, 16)
            sp.wait_ge(stored, 32)


def gnn_kernel(nc, a, out):
    sems = {"semaphores": [], "stages": 0}
    with ExitStack() as ctx:
        pl = Plan(nc, ctx, a["x"], a["src"], a["edge_attr_64"])
        att_shape = [P, pl.NB, D]

        def attend(name, kind, H, tab, q_tab, scale, pieces, after):
            with ExitStack() as c:
                w = load_sweep_weights(nc, sems, c, pieces) if pieces else {}
                edge_sweep(nc, pl, sems, kind, H, tab, q_tab, pl.part_tab[H], scale, w)
            with ExitStack() as c:
                att = c.enter_context(nc.sbuf_tensor("att_" + name, att_shape, F32))
                merge_parts(nc, pl, sems, H, scale, att)
                after(att)

        setup_graph(nc, pl, sems, a["x"], a["src"], a["dst"], a["edge_weight"], a["node_vec"])

        norm_input(nc, pl, sems)
        project(nc, pl, sems, [a["L0_gnn_W_fc"]], [None], ["z"], gat=(a["L0_gnn_a_l"], a["L0_gnn_a_r"]))
        attend("gat", "gat", 8, pl.gat_tab, pl.er_tab, 1.0,
               {"Wt": a["L1_gnn_Wt"].rearrange("a c -> (a c)"), "bt": a["L1_gnn_bt"]},
               lambda att: feed_forward(nc, pl, sems, att, a["L0_gnn_ln_gamma"], a["L0_gnn_ln_beta"], a["L0_gnn_W1"],
                                        a["L0_gnn_b1"], a["L0_gnn_W2"], a["L0_gnn_b2"]))

        norm_input(nc, pl, sems)
        for n in "12":
            w = {k: a[f"L1_gnn_{k}{n}"] for k in ("Wq", "bq", "Wk", "bk", "Wv", "bv", "We", "Wskip", "bskip")}
            project(nc, pl, sems, [w["Wq"], w["Wk"], w["Wv"], w["Wskip"]], [w["bq"], w["bk"], w["bv"], w["bskip"]],
                    ["q", "k", "v", "res"])
            attend("conv" + n, "tconv", 4, pl.kv_tab, pl.q_tab, 32 ** -0.5, {"We": w["We"]},
                   lambda att: add_residual(nc, pl, sems, att, n == "2"))

        norm_input(nc, pl, sems)
        w = {k: a[f"L2_gnn_{k}"] for k in ("Wq", "bq", "Wk", "bk", "Wv", "bv", "Wr", "br")}
        project(nc, pl, sems, [w["Wq"], w["Wk"], w["Wv"], w["Wr"]], [w["bq"], w["bk"], w["bv"], w["br"]],
                ["q", "k", "v", "res"])
        attend("mha", "mha", 4, pl.kv_tab, pl.q_tab, 32 ** -0.5, {},
               lambda att: add_residual(nc, pl, sems, att, True))

        norm_input(nc, pl, sems)
        for n in "12":
            project(nc, pl, sems, [a["L3_gnn_Wl" + n], a["L3_gnn_Wr" + n]], [None, None], ["xl", "q"])
            attend("gatv2" + n, "gatv2", 8, pl.xl_tab, pl.q_tab, 1.0,
                   {"att": a["L3_gnn_att" + n].rearrange("h k -> (h k)")},
                   lambda att: add_residual(nc, pl, sems, att, n == "2", a["L3_gnn_b" + n],
                                            (a["L3_gnn_g" + n], a["L3_gnn_be" + n])))
        store_output(nc, pl, sems, out)


def kernel(**inputs):
    import numpy as _np
    import concourse.bacc as _bacc
    from concourse import mybir as _mybir
    from concourse.bass_utils import run_bass_kernel_spmd as _run

    nc = _bacc.Bacc("TRN2", target_bir_lowering=False, num_devices=1)
    arrays, args = {}, {}
    for name, value in inputs.items():
        a = _np.ascontiguousarray(value)
        arrays["in_" + name] = a
        args[name] = nc.dram_tensor("in_" + name, a.shape, _mybir.dt.from_np(a.dtype), kind="ExternalInput").ap()
    out = nc.dram_tensor("out", arrays["in_x"].shape, F32, kind="ExternalOutput").ap()
    gnn_kernel(nc, args, out)
    return _run(nc, [arrays], core_ids=[0]).results[0]["out"]
```

```python
from contextlib import ExitStack

import numpy as np

import concourse.bass as bass
from concourse import mybir

F32 = mybir.dt.float32
I32 = mybir.dt.int32
BF16 = mybir.dt.bfloat16
ALU = mybir.AluOpType
ACT = mybir.ActivationFunctionType
AX = mybir.AxisListType

P = 128
D = 128
G = 8
HALF = G // 2
SLOTS = 4
CHUNKS = 4
FIRST_CHUNK = 4
FAR = -1.0e38
TINY = 1.0e-9
EPS = 1.0e-5
MAGIC = 12582912.0
TWO_PI_HIGH = 6.28125
TWO_PI_LOW = float(2 * np.pi - 6.28125)


def bc(ap, shape):
    return ap.to_broadcast(shape)


class Plan:

    def __init__(self, nc, ctx, x, src, edge_attr):
        self.N, self.E = x.shape[0], src.shape[0]
        tiles = -(-self.E // P)
        self.NG = -(-tiles // G)
        self.TT = self.NG * G
        self.TB = -(-self.TT // P)
        self.NB = 2 * -(-self.N // (2 * P))
        self.NP = self.NB * P
        self.DL_W = 2 * P + 4
        self.edge_attr = edge_attr
        assert self.NG >= 16 and x.shape[1] == D

        def sb(name, shape, dt=F32):
            return ctx.enter_context(nc.sbuf_tensor(name, shape, dt))

        def dram(name, shape):
            return nc.dram_tensor(name, shape, F32, kind="Internal").ap()

        NB, TB, NP, TT = self.NB, self.TB, self.NP, self.TT
        self.banks = [ctx.enter_context(nc.psum_tensor(f"bank{b}", [P, 512], F32)) for b in range(8)]
        self.ident = sb("ident", [P, P])
        self.ident_b = sb("ident_b", [P, P], BF16)
        self.head8, self.head4 = sb("head8", [P, D]), sb("head4", [P, D])
        self.iota_free, self.iota_free_i = sb("iota_free", [P, P]), sb("iota_free_i", [P, P], I32)
        self.node_id_i = sb("node_id_i", [P, NB], I32)
        self.half_pi = sb("half_pi", [P, 1])
        self.eps = sb("eps", [P, 1])
        self.one = sb("one", [P, 1])
        self.x_sb = sb("x_sb", [P, NB, D])
        self.hn = sb("hn", [P, NB, D])
        self.res = sb("res", [P, NB, D])
        self.node_vec_sb = sb("node_vec_sb", [P, NB])
        self.src_col = sb("src_col", [P, TB * P])
        self.rank_col = sb("rank_col", [P, TB * P])
        self.last_col = sb("last_col", [P, TB * P])
        self.weight_col = sb("weight_col", [P, TB * P])
        self.whole_row = sb("whole_row", [P, TB * P])
        self.whole_pen = sb("whole_pen", [P, TB * P])
        self.window_i = sb("window_i", [1, TB * P], I32)
        self.tile_last_i = sb("tile_last_i", [P, TB], I32)
        self.part_i = sb("part_i", [P, NB], I32)
        self.goes_on_pen = sb("goes_on_pen", [P, TB])
        self.has_edges = sb("has_edges", [P, NB])
        self.compact_i = sb("compact_i", [P, NB], I32)
        self.dl_tab = dram("dl_tab", [TB * P, self.DL_W])
        self.neg_tab = dram("neg_tab", [TB * P, 2 * P])
        self.row_tab = dram("row_tab", [2 * TB * P])
        self.gat_tab = dram("gat_tab", [NP, D + 16])
        self.kv_tab = dram("kv_tab", [NP, 2 * D])
        self.xl_tab = dram("xl_tab", [NP, D])
        self.q_tab = dram("q_tab", [NP + P, D])
        self.er_tab = dram("er_tab", [NP + P, 8])
        self.attr_tab = dram("attr_tab", [self.NG * P, G * P])
        self.part_tab = {H: dram(f"part_tab{H}", [TT * P, D + 2 * H]) for H in (8, 4)}


def wait(eng, sem, value):
    if isinstance(value, int) and value <= 0:
        return
    eng.wait_ge(sem, value)


def settle(eng, passed):
    eng.sem_inc(passed, 1)


class Stage:

    def __init__(self, nc, shared):
        self.nc, self.shared, self.used = nc, shared, {}
        shared["stages"] += 1
        self.number = shared["stages"]
        self.free = shared["sets"][self.number % 2]
        self.left = shared["left"]

    def __call__(self, name):
        if name not in self.used:
            if len(self.used) == len(self.free):
                self.free.append(self.nc.alloc_semaphore(f"stage_semaphore_{self.number % 2}_{len(self.free)}"))
            self.used[name] = self.free[len(self.used)]
        return self.used[name]

    def clear_last(self, pe):
        for s in self.left:
            pe.sem_clear(s)

    def indirect(self, name):
        return self.nc.alloc_semaphore(self.name(name))

    def lasting(self, name):
        known = self.shared["lasting"]
        if name not in known:
            known[name] = [self.nc.alloc_semaphore(name), 0]
        known[name][1] += 1
        return known[name][0], known[name][1] - 1

    def name(self, name):
        return f"s{self.number}_{name}"

    def tensor(self, ctx, name, shape, dt=F32):
        return ctx.enter_context(self.nc.sbuf_tensor(self.name(name), shape, dt))

    def close(self):
        self.shared["left"] = list(self.used.values())


def chain(eng, sem):
    count = [0]

    def link(ins):
        count[0] += 1
        ins.then_inc(sem, 1)
        eng.wait_ge(sem, count[0])

    return link



def setup_graph(nc, pl, sems, x, src, dst, edge_weight, node_vec):
    sem = Stage(nc, sems)
    TB, NB = pl.TB, pl.NB
    E = pl.E
    whole_tiles = E // P
    whole_blocks = whole_tiles // P
    rest_tiles = whole_tiles - whole_blocks * P
    rest_edges = E - whole_tiles * P

    with ExitStack() as ctx:
        def sb(name, shape, dt=F32):
            return sem.tensor(ctx, name, shape, dt)

        src_i = sb("src_i", [P, TB, P], I32)
        dst_i = sb("dst_i", [P, TB, P], I32)
        weight = sb("weight", [P, TB, P])
        dst_f = sb("dst_f", [P, TB, P])
        src_f = sb("src_f", [P, TB, P])
        start = sb("start", [P, TB, P])
        local_start = sb("local_start", [P, TB, P])
        not_first = sb("not_first", [P, TB, P])
        rank1 = sb("rank1", [P, TB, P])
        last_in_tile = sb("last_in_tile", [P, TB, P])
        dl = sb("dl", [P, TB, pl.DL_W])
        neg = sb("neg", [P, TB, 2 * P])
        dst_last1 = sb("dst_last1", [P, TB])
        prev_dst = sb("prev_dst", [P, TB])
        lr_last = sb("lr_last", [P, TB])
        prev_lr = sb("prev_lr", [P, TB])
        n_starts = sb("n_starts", [P, TB])
        totals = sb("totals", [P, TB])
        running = sb("running", [P, TB])
        ones_row = sb("ones_row", [P, max(TB, NB)])
        window = sb("window", [P, TB])
        whole = sb("whole", [P, TB])
        tile_id = sb("tile_id", [P, TB])
        tile_last = sb("tile_last", [P, TB])
        tile_rows = sb("tile_rows", [P, 2 * TB])
        tile_rows_t = sb("tile_rows_t", [2 * TB, P])
        window_f = sb("window_f", [1, TB * P])
        shift_m = sb("shift_m", [P, P])
        corner_m = sb("corner_m", [P, P])
        below_m = sb("below_m", [P, P])
        ones_m = sb("ones_m", [P, P])
        zeros = sb("zeros", [P, P])
        node_row_i = pl.hn[:, :, :].rearrange("p b d -> p (b d)").bitcast(I32)
        node_row = pl.res[:, :, :].rearrange("p b d -> p (b d)")
        hit = pl.hn
        ended = sb("ended", [P, TB, pl.NP], BF16)
        ones_b = sb("ones_b", [P, 1], BF16)
        tb_f = sb("tb_f", [P, NB])
        tb_i = sb("tb_i", [P, NB], I32)
        found = sb("found", [P, NB, pl.DL_W])
        cnt = sb("cnt", [P, NB])
        row_end = sb("row_end", [P, NB])
        row_start = sb("row_start", [P, NB])
        lr_end = sb("lr_end", [P, NB])
        lr_sel = sb("lr_sel", [P, NB])
        at_edge = sb("at_edge", [P, NB])
        pe_pos = sb("pe_pos", [P, NB])
        te = sb("te", [P, NB])
        tmp = sb("tmp", [P, NB])
        node_id = sb("node_id", [P, NB])
        before = sb("before", [P, NB])
        n_tot = sb("n_tot", [P, NB])
        n_run = sb("n_run", [P, NB])
        compact = sb("compact", [P, NB])

        padded, loaded = sem("padded"), sem("loaded")
        made = sem("pool_made")
        shifted = sem("shifted")
        tables, marks, rows = sem("tables_stored"), sem("marks_stored"), sem("rows_stored")
        turned, turned_used = sem("turned"), sem("turned_used")
        dve = sem("dve")
        dl_ready, last_ready = sem("dl_ready"), sem("last_ready")
        starts_ready, prefix_done = sem("starts_ready"), sem("prefix_done")
        rows_ready, rows_turned, rows_copied = sem("rows_ready"), sem("rows_turned"), sem("rows_copied")
        node_row_ready, ended_ready, ended_summed = sem("node_row_ready"), sem("ended_ready"), sem("ended_summed")
        row_loaded = sem("row_loaded")
        tb_ready, searched = sem("tb_ready"), [sem.indirect(f"searched{h}") for h in range(2)]
        halves = ((0, NB // 2), (NB // 2, NB))
        end_ready, end_shifted = sem("end_ready"), sem("end_shifted")
        has_ready, has_prefix = sem("has_ready"), sem("has_prefix")
        small_loaded, zeroed = sem("small_loaded"), sem("zeroed")
        zero_done = sem("zero_done")
        ps = pl.banks

        with nc.Block() as block:
            @block.sync
            def _(sp):
                def load_tiles(tile, flat):
                    n = 0
                    if whole_blocks:
                        sp.dma_start(tile[:, 0:whole_blocks, :],
                                     flat[0:whole_blocks * P * P].rearrange("(g p e) -> p g e", p=P, e=P)
                                     ).then_inc(loaded, 16)
                        n += 1
                    if rest_tiles:
                        lo = whole_blocks * P * P
                        sp.dma_start(tile[0:rest_tiles, whole_blocks, :],
                                     flat[lo:lo + rest_tiles * P].rearrange("(p e) -> p e", e=P)
                                     ).then_inc(loaded, 16)
                        n += 1
                    if rest_edges:
                        sp.dma_start(tile[rest_tiles:rest_tiles + 1, whole_blocks, 0:rest_edges],
                                     flat[whole_tiles * P:E].rearrange("(p e) -> p e", p=1)
                                     ).then_inc(loaded, 16)
                        n += 1
                    return n

                sp.wait_ge(padded, 4)
                pl.list_loads = load_tiles(dst_i, dst) + load_tiles(src_i, src) + load_tiles(weight, edge_weight)
                full = pl.N // P
                sp.dma_start(pl.x_sb[:, 0:full, :], x[0:full * P, :].rearrange("(b p) c -> p b c", p=P)
                             ).then_inc(small_loaded, 16)
                sp.dma_start(pl.x_sb[0:pl.N - full * P, full, :], x[full * P:pl.N, :]).then_inc(small_loaded, 16)
                sp.dma_start(pl.node_vec_sb[:, 0:full], node_vec[0:full * P].rearrange("(b p) -> p b", p=P),
                             allow_slow_non_contiguous=True).then_inc(small_loaded, 16)
                sp.dma_start(pl.node_vec_sb[0:pl.N - full * P, full:full + 1],
                             node_vec[full * P:pl.N].rearrange("(p b) -> p b", b=1),
                             allow_slow_non_contiguous=True).then_inc(small_loaded, 16)
                sp.wait_ge(zero_done, 1)
                sp.dma_start(pl.q_tab[pl.NP:pl.NP + P, :], zeros[:, :]).then_inc(zeroed, 16)
                sp.dma_start(pl.er_tab[pl.NP:pl.NP + P, :], zeros[:, 0:8]).then_inc(zeroed, 16)
                sp.wait_ge(dl_ready, 1)
                sp.dma_start(pl.dl_tab.rearrange("(g p) w -> p g w", p=P), dl[:, :, :]).then_inc(tables, 16)
                sp.dma_start(pl.neg_tab.rearrange("(g p) w -> p g w", p=P), neg[:, :, :]).then_inc(marks, 16)
                sp.wait_ge(rows_copied, 1)
                sp.dma_start(pl.row_tab.rearrange("(k p) -> k p", p=P), tile_rows_t[:, :]).then_inc(rows, 16)
                sp.wait_ge(rows, 16)
                n = TB * P
                sp.dma_start(pl.whole_row[:, :], pl.row_tab[0:n].partition_broadcast(P)).then_inc(row_loaded, 16)
                sp.dma_start(window_f[:, :], pl.row_tab[n:2 * n].rearrange("(a n) -> a n", a=1)).then_inc(row_loaded, 16)
                sp.wait_ge(zeroed, 32)
                sp.wait_ge(marks, 16)
                sp.wait_ge(small_loaded, 64)

            @block.gpsimd
            def _(pool):
                pool.memset(zeros[:, :], 0.0).then_inc(zero_done, 1)
                for m in (pl.ident, shift_m, corner_m, below_m, pl.head8, pl.head4):
                    pool.memset(m[:, :], 0.0).then_inc(made, 1)
                pool.memset(ones_m[:, :], 1.0).then_inc(made, 1)
                pool.wait_ge(made, 7)
                pool.affine_select(out=pl.ident[:, :], in_=pl.ident[:, :], compare_op=ALU.not_equal, fill=1.0, base=0,
                                   pattern=[[-1, P]], channel_multiplier=1).then_inc(made, 1)
                pool.affine_select(out=shift_m[:, :], in_=shift_m[:, :], compare_op=ALU.not_equal, fill=1.0, base=1,
                                   pattern=[[-1, P]], channel_multiplier=1).then_inc(made, 1)
                pool.affine_select(out=corner_m[:, :], in_=corner_m[:, :], compare_op=ALU.not_equal, fill=1.0,
                                   base=-(P - 1), pattern=[[-P, P]], channel_multiplier=1).then_inc(made, 1)
                pool.affine_select(out=below_m[:, :], in_=below_m[:, :], compare_op=ALU.is_ge, fill=1.0, base=0,
                                   pattern=[[-1, P]], channel_multiplier=1).then_inc(made, 1)
                for m, c in ((pl.head8, 16), (pl.head4, 32)):
                    v = m[:, :].rearrange("h (a c) -> h a c", c=c)
                    pool.affine_select(out=v, in_=v, compare_op=ALU.not_equal, fill=1.0, base=0,
                                       pattern=[[-1, D // c], [0, c]], channel_multiplier=1).then_inc(made, 1)
                pool.iota(pl.iota_free_i[:, :], pattern=[[1, P]], base=0, channel_multiplier=0).then_inc(made, 1)
                pool.iota(pl.node_id_i[:, :], pattern=[[P, NB]], base=0, channel_multiplier=1).then_inc(made, 1)
                pool.iota(node_row_i, pattern=[[1, pl.NP]], base=0, channel_multiplier=0).then_inc(made, 1)
                pool.wait_ge(tables, 16)
                pool.wait_ge(tb_ready, 1)
                for half, (lo, hi) in enumerate(halves):
                    for b in range(lo, hi):
                        pool.indirect_dma_start(out=found[:, b, :], out_offset=None, in_=pl.dl_tab,
                                                in_offset=bass.IndirectOffsetOnAxis(ap=tb_i[:, b:b + 1], axis=0)
                                                ).then_inc(searched[half], 16)

            @block.scalar
            def _(act):
                act.wait_ge(made, 16)
                act.activation(node_row, node_row_i, ACT.Copy).then_inc(node_row_ready, 1)

            @block.vector
            def _(v):
                link = chain(v, dve)
                v.memset(dst_i[:, :, :], pl.NP).then_inc(padded, 1)
                v.memset(src_i[:, :, :], 0).then_inc(padded, 1)
                v.memset(weight[:, :, :], 0.0).then_inc(padded, 1)
                v.memset(pl.x_sb[:, pl.N // P:NB, :], 0.0)
                v.memset(pl.node_vec_sb[:, :], 0.0).then_inc(padded, 1)
                v.memset(ones_row[:, :], 1.0)
                v.memset(ones_b[:, :], 1.0)
                v.memset(pl.half_pi[:, :], float(np.pi / 2))
                v.memset(pl.eps[:, :], EPS)
                v.memset(pl.one[:, :], 1.0)
                v.memset(not_first[:, :, :], 1.0)
                v.memset(dl[:, :, 2 * P:pl.DL_W], 0.0)
                link(v.memset(last_in_tile[:, :, P - 1:P], 1.0))
                link(v.memset(not_first[:, :, 0:1], 0.0))
                v.wait_ge(made, 15)
                v.tensor_copy(pl.iota_free[:, :], pl.iota_free_i[:, :])
                v.tensor_copy(pl.ident_b[:, :], pl.ident[:, :])
                link(v.tensor_copy(node_id[:, :], pl.node_id_i[:, :]))
                v.wait_ge(loaded, 16 * pl.list_loads)
                link(v.tensor_copy(dst_f[:, :, :], dst_i[:, :, :]))
                v.tensor_copy(dl[:, :, 0:P], dst_f[:, :, :])
                link(v.tensor_copy(src_f[:, :, :], src_i[:, :, :]))
                v.tensor_scalar(dst_last1[:, :], dst_f[:, :, P - 1], 1.0, None, ALU.add).then_inc(last_ready, 1)
                v.wait_ge(shifted, 1)
                link(v.tensor_scalar(prev_dst[:, :], ps[0][:, 0:TB], -1.0, None, ALU.add))
                link(v.tensor_tensor(prev_dst[:, 1:TB], prev_dst[:, 1:TB], ps[0][:, 64:64 + TB - 1], ALU.add))
                v.tensor_tensor(start[:, :, 1:P], dst_f[:, :, 1:P], dst_f[:, :, 0:P - 1], ALU.not_equal)
                link(v.tensor_tensor(start[:, :, 0], dst_f[:, :, 0], prev_dst[:, :], ALU.not_equal))
                v.tensor_copy(local_start[:, :, 1:P], start[:, :, 1:P])
                v.memset(local_start[:, :, 0:1], 1.0)
                v.tensor_reduce(n_starts[:, :], start[:, :, :], AX.X, ALU.add).then_inc(starts_ready, 1)
                link(v.tensor_copy(last_in_tile[:, :, 0:P - 1], start[:, :, 1:P]))
                link(v.tensor_tensor_scan(rank1[:, :, :].rearrange("p g e -> p (g e)"),
                                          not_first[:, :, :].rearrange("p g e -> p (g e)"),
                                          local_start[:, :, :].rearrange("p g e -> p (g e)"), 0.0, ALU.mult, ALU.add))
                v.tensor_scalar(neg[:, :, 0:P], local_start[:, :, :], FAR, None, ALU.mult)
                v.tensor_scalar(neg[:, :, P:2 * P], last_in_tile[:, :, :], FAR, None, ALU.mult)
                v.tensor_scalar(lr_last[:, :], rank1[:, :, P - 1], -1.0, None, ALU.add).then_inc(last_ready, 1)
                link(v.tensor_scalar(dl[:, :, P:2 * P], rank1[:, :, :], -1.0, None, ALU.add))
                v.wait_ge(shifted, 2)
                link(v.tensor_copy(prev_lr[:, :], ps[1][:, 0:TB]))
                link(v.tensor_tensor(prev_lr[:, 1:TB], prev_lr[:, 1:TB], ps[1][:, 64:64 + TB - 1], ALU.add))
                v.tensor_copy(dl[:, :, 2 * P], prev_lr[:, :]).then_inc(dl_ready, 1)
                v.wait_ge(node_row_ready, 1)
                for g in range(TB):
                    v.tensor_scalar(ended[:, g, :], node_row, dst_f[:, g, P - 1:P], None, ALU.is_ge).then_inc(ended_ready, 1)
                v.wait_ge(prefix_done, 1)
                link(v.tensor_copy(totals[:, :], ps[2][:, 64:64 + TB]))
                link(v.tensor_tensor_scan(running[:, :], ones_row[:, 0:TB], totals[:, :], 0.0, ALU.mult, ALU.add))
                link(v.tensor_tensor(running[:, :], running[:, :], totals[:, :], ALU.subtract))
                link(v.tensor_tensor(window[:, :], running[:, :], ps[2][:, 0:TB], ALU.add))
                link(v.tensor_tensor(window[:, :], window[:, :], start[:, :, 0], ALU.add))
                v.tensor_scalar(tile_rows[:, TB:2 * TB], window[:, :], -1.0, None, ALU.add)
                link(v.tensor_scalar(whole[:, :], lr_last[:, :], 0.0, None, ALU.is_equal))
                link(v.tensor_scalar(prev_dst[:, :], start[:, :, 0], -1.0, 1.0, ALU.mult, ALU.add))
                v.tensor_scalar(pl.goes_on_pen[:, :], prev_dst[:, :], -FAR, FAR, ALU.mult, ALU.add)
                v.tensor_tensor(tile_rows[:, 0:TB], whole[:, :], prev_dst[:, :], ALU.mult).then_inc(rows_ready, 1)
                v.wait_ge(ended_summed, 1)
                v.tensor_copy(tb_i[:, :], ps[6][:, 256:256 + NB]).then_inc(tb_ready, 1)
                v.tensor_copy(tb_f[:, :], ps[6][:, 256:256 + NB])
                link(v.tensor_scalar(tile_id[:, :], node_id[:, 0:TB], float(P), None, ALU.mult))
                link(v.tensor_tensor(tile_last[:, :], tile_id[:, :], lr_last[:, :], ALU.add))
                link(v.tensor_scalar(tile_last[:, :], tile_last[:, :], float(pl.TT * P - 1), None, ALU.min))
                v.tensor_copy(pl.tile_last_i[:, :], tile_last[:, :])
                v.wait_ge(rows_turned, 1)
                v.tensor_copy(tile_rows_t[:, :], ps[3][0:2 * TB, 0:P]).then_inc(rows_copied, 1)
                for n, out in enumerate((pl.src_col, pl.rank_col, pl.last_col, pl.weight_col)):
                    for half in range(2):
                        v.wait_ge(turned, 2 * n + half + 1)
                        lo, hi = (0, 4) if half == 0 else (4, TB)
                        v.tensor_copy(out[:, lo * P:hi * P], ps[4 + half][:, 0:(hi - lo) * P]).then_inc(turned_used, 1)
                v.wait_ge(row_loaded, 32)
                v.tensor_copy(pl.window_i[:, :], window_f[:, :])
                v.tensor_scalar(pl.whole_pen[:, :], pl.whole_row[:, :], -FAR, FAR, ALU.mult, ALU.add)
                for half, (lo, hi) in enumerate(halves):
                    n, h = hi - lo, slice(lo, hi)
                    v.wait_ge(searched[half], 16 * n)
                    link(v.tensor_tensor(hit[:, h, :], found[:, h, 0:P], bc(node_id[:, h].unsqueeze(2), [P, n, P]), ALU.is_le))
                    link(v.tensor_reduce(cnt[:, h], hit[:, h, :], AX.X, ALU.add))
                    link(v.tensor_scalar(pe_pos[:, h], cnt[:, h], -1.0, None, ALU.add))
                    link(v.tensor_tensor(hit[:, h, :], bc(pl.iota_free[:, :].unsqueeze(1), [P, n, P]),
                                         bc(pe_pos[:, h].unsqueeze(2), [P, n, P]), ALU.is_equal))
                    link(v.tensor_tensor(hit[:, h, :], hit[:, h, :], found[:, h, P:2 * P], ALU.mult))
                    link(v.tensor_reduce(lr_sel[:, h], hit[:, h, :], AX.X, ALU.add))
                v.scalar_tensor_tensor(row_end[:, :], tb_f[:, :], float(P), cnt[:, :], ALU.mult, ALU.add
                                       ).then_inc(end_ready, 1)
                v.wait_ge(end_shifted, 1)
                link(v.tensor_copy(row_start[:, :], ps[6][:, 0:NB]))
                link(v.tensor_tensor(row_start[:, 1:NB], row_start[:, 1:NB], ps[6][:, 64:64 + NB - 1], ALU.add))
                v.tensor_tensor(pl.has_edges[:, :], row_end[:, :], row_start[:, :], ALU.is_gt).then_inc(has_ready, 1)
                v.wait_ge(has_ready, 1)
                link(v.tensor_scalar(at_edge[:, :], cnt[:, :], 0.0, None, ALU.is_equal))
                link(v.tensor_tensor(te[:, :], tb_f[:, :], at_edge[:, :], ALU.subtract))
                link(v.tensor_scalar(te[:, :], te[:, :], 0.0, None, ALU.max))
                link(v.tensor_tensor(lr_end[:, :], at_edge[:, :], found[:, :, 2 * P], ALU.mult))
                link(v.tensor_tensor(lr_end[:, :], lr_end[:, :], lr_sel[:, :], ALU.add))
                link(v.scalar_tensor_tensor(tmp[:, :], te[:, :], float(P), lr_end[:, :], ALU.mult, ALU.add))
                v.tensor_copy(pl.part_i[:, :], tmp[:, :])
                v.wait_ge(has_prefix, 1)
                link(v.tensor_copy(n_tot[:, :], ps[7][:, 64:64 + NB]))
                link(v.tensor_tensor_scan(n_run[:, :], ones_row[:, 0:NB], n_tot[:, :], 0.0, ALU.mult, ALU.add))
                link(v.tensor_tensor(before[:, :], n_run[:, :], n_tot[:, :], ALU.subtract))
                link(v.tensor_tensor(before[:, :], before[:, :], ps[7][:, 0:NB], ALU.add))
                link(v.tensor_tensor(compact[:, :], node_id[:, :], before[:, :], ALU.subtract))
                link(v.tensor_tensor(compact[:, :], compact[:, :], bc(n_run[:, NB - 1:NB], [P, NB]), ALU.add))
                link(v.tensor_tensor(tmp[:, :], before[:, :], compact[:, :], ALU.subtract))
                link(v.tensor_tensor(tmp[:, :], tmp[:, :], pl.has_edges[:, :], ALU.mult))
                link(v.tensor_tensor(compact[:, :], compact[:, :], tmp[:, :], ALU.add))
                link(v.tensor_copy(pl.compact_i[:, :], compact[:, :]))

            @block.tensor
            def _(pe):
                sem.clear_last(pe)
                def shift(bank, vals, n, done):
                    pe.matmul(ps[bank][:, 0:n], shift_m[:, :], vals[:, 0:n], start=True, stop=True)
                    pe.matmul(ps[bank][:, 64:64 + n - 1], corner_m[:, :], vals[:, 0:n - 1], start=True, stop=True
                              ).then_inc(done, 1)

                def prefix(bank, vals, n, done):
                    pe.matmul(ps[bank][:, 0:n], below_m[:, :], vals[:, 0:n], start=True, stop=True)
                    pe.matmul(ps[bank][:, 64:64 + n], ones_m[:, :], vals[:, 0:n], start=True, stop=True
                              ).then_inc(done, 1)

                pe.wait_ge(made, 13)
                pe.wait_ge(last_ready, 1)
                shift(0, dst_last1, TB, shifted)
                pe.wait_ge(last_ready, 2)
                shift(1, lr_last, TB, shifted)
                pe.wait_ge(starts_ready, 1)
                prefix(2, n_starts, TB, prefix_done)
                for b in range(NB):
                    for g in range(TB):
                        if b == 0:
                            pe.wait_ge(ended_ready, g + 1)
                        ins = pe.matmul(ps[6][:, 256 + b:257 + b], ended[:, g, b * P:(b + 1) * P], ones_b[:, :],
                                        start=(g == 0), stop=(g == TB - 1))
                ins.then_inc(ended_summed, 1)
                pe.wait_ge(rows_ready, 1)
                pe.transpose(ps[3][0:2 * TB, 0:P], tile_rows[:, :], pl.ident[:, :]).then_inc(rows_turned, 1)
                pe.wait_ge(dl_ready, 1)
                for n, tiles in enumerate((src_f, dl[:, :, P:2 * P], last_in_tile, weight)):
                    for half in range(2):
                        wait(pe, turned_used, 2 * n + half - 1)
                        lo, hi = (0, 4) if half == 0 else (4, TB)
                        for g in range(lo, hi):
                            ins = pe.transpose(ps[4 + half][:, (g - lo) * P:(g - lo + 1) * P], tiles[:, g, :],
                                               pl.ident[:, :])
                        ins.then_inc(turned, 1)
                pe.wait_ge(end_ready, 1)
                shift(6, row_end, NB, end_shifted)
                pe.wait_ge(has_ready, 1)
                prefix(7, pl.has_edges, NB, has_prefix)
        sem.close()



def edge_sweep(nc, pl, sems, kind, H, tab, q_tab, part_tab, last_rows, scale, w):
    sem = Stage(nc, sems)
    TW = tab.shape[1]
    QW = q_tab.shape[1]
    C = D // H
    R = G * H
    W = D + 2 * H
    NG = pl.NG
    QB = 1 if kind == "gat" else 2
    PAIR = 2
    NPAIR = G // PAIR
    S = SLOTS
    act_builds = kind in ("tconv", "gatv2")

    with ExitStack() as ctx:
        def sb(name, shape, dt=F32):
            return sem.tensor(ctx, name, shape, dt)

        rows = [sb(f"rows{u}", [P, G, TW]) for u in range(S)]
        qwin = [sb(f"qwin{u}", [P, G, QW]) for u in range(S)]
        neg = [sb(f"neg{u}", [R, 2 * P]) for u in range(S)]
        idx = [sb(f"idx{u}", [P, G], I32) for u in range(S)]
        hot = [sb(f"hot{u}", [P, G, P]) for u in range(S)]
        if kind != "gat":
            hot_b = [sb(f"hot_b{u}", [P, G, P], BF16) for u in range(2)]
        if act_builds:
            gap = sb("gap", [P, G, P], BF16)
        hot_t = sb("hot_t", [P, G, P])
        alpha = sb("alpha", [P, G, H])
        fwd = sb("fwd", [R, P])
        seg_max = sb("seg_max", [R, P])
        diff = sb("diff", [R, P])
        prob = sb("prob", [R, P])
        pm = sb("pm", [P, 2 * R])
        msg = sb("msg", [P, G, W])
        part = [sb(f"part{u}", [P, G, W]) for u in range(S)]
        prod = [sb(f"prod{h}", [P, HALF, D]) for h in range(2)]
        if kind == "gat":
            rel = sb("rel", [P, G])
            attr = [sb(f"attr{u}", [P, G, D]) for u in range(S)]
            ang, turns = sb("ang", [P, G, 64]), sb("turns", [P, G, 64])
            ang2 = [sb(f"ang2{u}", [P, G, 64]) for u in range(S)]
        if kind in ("gat", "tconv"):
            attr_t = [sb(f"attr_t{u}", [P, G * P]) for u in range(2 if kind == "gat" else S)]

        hot_ps = [pl.banks[0], pl.banks[2]] if kind == "gat" else [pl.banks[0][:, :].bitcast(BF16)]
        q_ps = [pl.banks[1], pl.banks[2]]
        e_ps = [pl.banks[3], pl.banks[4]]
        small = pl.banks[5]
        alpha_t = small[0:R, 0:P]
        prob_ps, max_ps = small[:, P:P + R], small[:, P + R:P + 2 * R]
        part_ps = [pl.banks[6], pl.banks[7]]

        gathered = [sem.indirect(f"gathered{u}") for u in range(S)]
        last_got, passes = sem.lasting("last_gathered")
        done_blocks = (NG - 1) // (P // G)
        q_loaded = [sem(f"q_loaded{u}") for u in range(S)]
        neg_loaded = [sem(f"neg_loaded{u}") for u in range(S)]
        part_stored = [sem(f"part_stored{u}") for u in range(S)]
        idx_ready = sem("idx_ready")
        hot_built = sem("hot_built")
        gap_done = sem("gap_done")
        hot_turned = sem("hot_turned")
        hot_copied = sem("hot_copied")
        hot_cast = sem("hot_cast")
        q_done = sem("q_done")
        q_used = sem("q_used")
        alpha_done = sem("alpha_done")
        alpha_turned = sem("alpha_turned")
        fwd_done, max_done, diff_done = sem("fwd_done"), sem("max_done"), sem("diff_done")
        exp_done = sem("exp_done")
        prob_turned = sem("prob_turned")
        prob_copied = sem("prob_copied")
        msg_done = sem("msg_done")
        part_done = sem("part_done")
        part_copied = sem("part_copied")
        pool_passed, pe_passed = sem("pool_passed"), sem("pe_passed")
        step = sem("score_step")
        STEPS = {"gat": 7, "gatv2": 4}.get(kind, 0)
        if kind in ("gat", "tconv"):
            attr_loaded = [sem(f"attr_loaded{u}") for u in range(S)]
        if kind == "gat":
            attr_stored = [sem(f"attr_stored{u}") for u in range(2)]
            angle_done = sem("angle_done")
            cos_done = sem("cos_done")
            attr_turned = sem("attr_turned")
            attr_copied = sem("attr_copied")
            tail_zeroed = sem("tail_zeroed")
        if kind == "tconv":
            e_used = sem("e_used")
        ring = [(i, i // S, i % S) for i in range(NG + 3)]
        FIRST, LAST = 2 * S, (NG - 3) // S * S

        def bodies(eng, body):
            for i, k, u in ring[:FIRST]:
                body(i, k, u, i)
            with eng.Fori(2, LAST // S) as j:
                for u in range(S):
                    body(j * S + u, j, u, FIRST + u)
            for i, k, u in ring[LAST:]:
                body(i, k, u, i)

        def near(i, k, u, n, d):
            return i + d, k + (u + d) // S, (u + d) % S, n + d

        def has(n, d=0):
            return 0 <= n + d < NG

        with nc.Block() as block:
            @block.sync
            def _(sp):
                window = [sp.alloc_register(sem.name(f"window{t}")) for t in range(G)]

                def load(i, k, u, n):
                    if n >= S:
                        wait(sp, q_done, (i - S + 1) * QB)
                    sp.load(window, pl.window_i[0:1, bass.ds(i * G, G)])
                    for t in range(G):
                        first = sp.snap(window[t], min_val=0, max_val=pl.NP)
                        sp.dma_start(qwin[u][:, t, :], q_tab[bass.ds(first, P), :]).then_inc(q_loaded[u], 16)
                    if n >= S:
                        wait(sp, max_done, i - S + 1)
                    marks = pl.neg_tab[bass.ds(i * G, G), :].unsqueeze(1)
                    sp.dma_start(neg[u][:, :], bc(marks, [G, H, 2 * P])).then_inc(neg_loaded[u], 16)
                    if kind == "tconv":
                        sp.dma_start(attr_t[u][:, :], pl.attr_tab[bass.ds(i * P, P), :]).then_inc(attr_loaded[u], 16)

                def load_messages(i, k, u, n):
                    if n >= S:
                        wait(sp, attr_turned, 2 * (i - S + 1))
                    if n < NG - 1:
                        src_ap = pl.edge_attr[bass.ds(i * (G * P), G * P), :].rearrange("(t p) c -> p t c", p=P)
                        sp.dma_start(attr[u][:, :, 64:D], src_ap).then_inc(attr_loaded[u], 16)
                        return
                    sp.wait_ge(tail_zeroed, 1)
                    base = (NG - 1) * G * P
                    full = (pl.E - base) // P
                    if full:
                        sp.dma_start(attr[u][:, 0:full, 64:D],
                                     pl.edge_attr[base:base + full * P, :].rearrange("(t p) c -> p t c", p=P)
                                     ).then_inc(attr_loaded[u], 16)
                    if pl.E > base + full * P:
                        sp.dma_start(attr[u][0:pl.E - base - full * P, full, 64:D],
                                     pl.edge_attr[base + full * P:pl.E, :]).then_inc(attr_loaded[u], 16)

                def store_parts(i, k, u, n):
                    wait(sp, part_copied, (i + 1) * NPAIR)
                    out = part_tab[bass.ds(i * (G * P), G * P), :].rearrange("(t p) w -> p t w", p=P)
                    sp.dma_start(out, part[u][:, :, :]).then_inc(part_stored[u], 16)

                def store_attr(i, k, u, n):
                    wait(sp, attr_copied, 2 * (i + 1))
                    sp.dma_start(pl.attr_tab[bass.ds(i * P, P), :], attr_t[u % 2][:, :]).then_inc(attr_stored[u % 2], 16)

                def body(*g):
                    n = g[3]
                    if has(n, 2):
                        load(*near(*g, 2))
                    if kind == "gat" and has(n):
                        load_messages(*g)
                    if kind == "gat" and has(n, -3):
                        store_attr(*near(*g, -3))
                    if has(n, -2):
                        store_parts(*near(*g, -2))

                load(0, 0, 0, 0)
                load(1, 0, 1, 1)
                bodies(sp, body)
                for u in range(S):
                    count = len(range(u, NG, S))
                    sp.wait_ge(part_stored[u], 16 * count)
                if kind == "gat":
                    for u in range(2):
                        sp.wait_ge(attr_stored[u], 16 * len(range(u, NG, 2)))

            @block.gpsimd
            def _(pool):
                def gather(i, k, u, n):
                    if n >= S:
                        wait(pool, msg_done, 3 * (i - S + 1))
                    wait(pool, idx_ready, i + 1)
                    settle(pool, pool_passed)
                    for t in range(G):
                        pool.indirect_dma_start(out=rows[u][:, t, :], out_offset=None, in_=tab,
                                                in_offset=bass.IndirectOffsetOnAxis(ap=idx[u][:, t:t + 1], axis=0)
                                                ).then_inc(gathered[u], 16)

                def body(*g):
                    if has(g[3], 2):
                        gather(*near(*g, 2))

                gather(0, 0, 0, 0)
                gather(1, 0, 1, 1)
                bodies(pool, body)
                for u in range(S):
                    pool.wait_ge(part_stored[u], 16 * len(range(u, done_blocks * (P // G), S)))
                gather_last(pool, pl, part_tab, last_rows, last_got, 0, done_blocks)

            @block.scalar
            def _(act):
                def indices(i, k, u, n):
                    if n >= S:
                        wait(act, gathered[u], 16 * G * k)
                    act.activation(idx[u][:, :], pl.src_col[:, bass.ds(i * G, G)], ACT.Copy).then_inc(idx_ready, 1)

                def copy_hot(i, k, u, n):
                    wait(act, hot_turned, i + 1)
                    per = G // len(hot_ps)
                    for h, bank in enumerate(hot_ps):
                        ins = act.activation(hot_t[:, h * per:(h + 1) * per, :],
                                             bank[:, 0:per * P].rearrange("p (t e) -> p t e", t=per), ACT.Copy)
                    ins.then_inc(hot_copied, 1)

                def cast_hot(i, k, u, n):
                    wait(act, hot_built, i + 1)
                    if n >= S:
                        wait(act, part_done, NPAIR * (i - S + 1))
                    act.activation(hot[u][:, :, :], hot_b[u % 2][:, :, :], ACT.Copy).then_inc(hot_cast, 1)

                def measure(i, k, u, n, half):
                    if n >= 1:
                        wait(act, hot_built, i)
                    for t in range(half * HALF, (half + 1) * HALF):
                        ins = act.activation(gap[:, t, :], pl.iota_free[:, :], ACT.Abs, scale=-1.0,
                                             bias=pl.rank_col[:, bass.ds(i * G + t, 1)])
                    if half:
                        ins.then_inc(gap_done, 1)

                def build_hot(i, k, u, n):
                    wait(act, gap_done, i + 1)
                    if n >= 2:
                        wait(act, hot_turned, i - 1)
                        wait(act, hot_cast, i - 1)
                    act.activation(hot_b[u % 2][:, :, :], gap[:, :, :], ACT.Relu, scale=-1.0, bias=pl.one[:, 0:1]
                                   ).then_inc(hot_built, 1)

                def exps(i, k, u, n):
                    wait(act, diff_done, i + 1)
                    if n >= 1:
                        wait(act, prob_turned, i)
                    act.activation(prob[:, :], diff[:, :], ACT.Exp, scale=scale).then_inc(exp_done, 1)

                def copy_probs(i, k, u, n):
                    wait(act, prob_turned, i + 1)
                    if n >= 1:
                        wait(act, msg_done, 3 * i)
                    act.activation(pm[:, :], small[:, P:P + 2 * R], ACT.Copy).then_inc(prob_copied, 1)

                def copy_parts(i, k, u, n, c):
                    if n >= S and c == 0:
                        wait(act, part_stored[u], 16 * k)
                    wait(act, part_done, NPAIR * i + c + 1)
                    act.activation(part[u][:, PAIR * c:PAIR * (c + 1), :],
                                   part_ps[c % 2][:, 0:PAIR * W].rearrange("p (t w) -> p t w", t=PAIR), ACT.Copy
                                   ).then_inc(part_copied, 1)

                def cosines(i, k, u, n):
                    wait(act, angle_done, i + 1)
                    if n >= S:
                        wait(act, attr_turned, 2 * (i - S + 1))
                    act.activation(attr[u][:, :, 0:64], ang2[u][:, :, :], ACT.Sin, bias=pl.half_pi[:, 0:1]
                                   ).then_inc(cos_done, 1)

                def copy_attr(i, k, u, n):
                    if n >= 2:
                        wait(act, attr_stored[u % 2], 16 * (2 * k + u // 2))
                    for h in range(2):
                        wait(act, attr_turned, 2 * i + h + 1)
                        act.activation(attr_t[u % 2][:, h * HALF * P:(h + 1) * HALF * P], e_ps[h][:, :], ACT.Copy
                                       ).then_inc(attr_copied, 1)

                def body(*g):
                    u, n = g[2:]
                    if has(n, -1):
                        exps(*near(*g, -1))
                    if act_builds and has(n, 2):
                        measure(*near(*g, 2), 0)
                    if has(n, 1):
                        copy_hot(*near(*g, 1))
                    if has(n, -2):
                        copy_parts(*near(*g, -2), 0)
                        copy_parts(*near(*g, -2), 1)
                    if has(n, -1):
                        copy_probs(*near(*g, -1))
                    if has(n, -2):
                        for c in range(2, NPAIR):
                            copy_parts(*near(*g, -2), c)
                    if kind == "gat" and has(n, -3):
                        copy_attr(*near(*g, -3))
                    if kind != "gat" and has(n, 1):
                        cast_hot(*near(*g, 1))
                    if act_builds and has(n, 2):
                        measure(*near(*g, 2), 1)
                        build_hot(*near(*g, 2))
                    if has(n, 3):
                        indices(*near(*g, 3))
                    if kind == "gat" and u % 2 == 0:
                        for d in (-2, -1):
                            if has(n, d):
                                cosines(*near(*g, d))

                indices(0, 0, 0, 0)
                indices(1, 0, 1, 1)
                indices(2, 0, 2, 2)
                if act_builds:
                    for i in range(2):
                        for half in range(2):
                            measure(i, 0, i, i, half)
                        build_hot(i, 0, i, i)
                copy_hot(0, 0, 0, 0)
                if kind != "gat":
                    cast_hot(0, 0, 0, 0)
                bodies(act, body)

            @block.tensor
            def _(pe):
                sem.clear_last(pe)
                def turn_hot(i, k, u, n):
                    wait(pe, hot_built, i + 1)
                    if n >= 1:
                        wait(pe, hot_copied, i)
                    per = G // len(hot_ps)
                    one_hot, ident = (hot[u], pl.ident) if kind == "gat" else (hot_b[u % 2], pl.ident_b)
                    for t in range(G):
                        ins = pe.transpose(hot_ps[t // per][:, t % per * P:(t % per + 1) * P], one_hot[:, t, :], ident[:, :])
                    ins.then_inc(hot_turned, 1)

                def spread(i, k, u, n):
                    wait(pe, hot_copied, i + 1)
                    wait(pe, q_loaded[u], 16 * G * (k + 1))
                    if kind == "tconv":
                        wait(pe, attr_loaded[u], 16 * (k + 1))
                    per = G // QB
                    for h in range(QB):
                        if n >= 1:
                            wait(pe, q_used, QB * (i - 1) + h + 1)
                        if kind == "tconv":
                            if n >= 1:
                                wait(pe, e_used, 2 * (i - 1) + h + 1)
                            for t in range(h * per, (h + 1) * per):
                                pe.matmul(e_ps[h][:, (t - h * per) * D:(t - h * per + 1) * D],
                                          attr_t[u][:, t * P:(t + 1) * P], w["We"][:, :], start=True, stop=True)
                        for t in range(h * per, (h + 1) * per):
                            ins = pe.matmul(q_ps[h][:, (t - h * per) * QW:(t - h * per + 1) * QW], hot_t[:, t, :],
                                            qwin[u][:, t, :], start=True, stop=True)
                        ins.then_inc(q_done, 1)

                def turn_probs(i, k, u, n):
                    wait(pe, exp_done, i + 1)
                    settle(pe, pe_passed)
                    pe.transpose(max_ps, seg_max[:, :], pl.ident[0:R, 0:R])
                    pe.transpose(prob_ps, prob[:, :], pl.ident[0:R, 0:R]).then_inc(prob_turned, 1)

                def turn_alpha(i, k, u, n):
                    wait(pe, alpha_done, QB * (i + 1))
                    if n >= 1:
                        wait(pe, prob_copied, i)
                    settle(pe, pe_passed)
                    pe.transpose(alpha_t, alpha[:, :, :].rearrange("p t h -> p (t h)"), pl.ident[:, :]
                                 ).then_inc(alpha_turned, 1)

                def sum_parts(i, k, u, n, c):
                    if c == 0:
                        if kind != "gat":
                            wait(pe, hot_cast, i + 1)
                        wait(pe, msg_done, 3 * (i + 1))
                    if n >= 1 or c >= 2:
                        wait(pe, part_copied, NPAIR * i + c - 1)
                    for t in range(PAIR):
                        ins = pe.matmul(part_ps[c % 2][:, t * W:(t + 1) * W], hot[u][:, PAIR * c + t, :],
                                        msg[:, PAIR * c + t, :], start=True, stop=True)
                    ins.then_inc(part_done, 1)

                def turn_attr(i, k, u, n):
                    wait(pe, cos_done, i + 1)
                    if n < NG - 1:
                        wait(pe, attr_loaded[u], 16 * (k + 1))
                    else:
                        rest = pl.E - (NG - 1) * G * P
                        wait(pe, attr_loaded[u], 16 * (k + (rest >= P) + (rest % P > 0)))
                    for h in range(2):
                        if n >= 1:
                            wait(pe, attr_copied, 2 * (i - 1) + h + 1)
                        for t in range(HALF):
                            ins = pe.transpose(e_ps[h][:, t * P:(t + 1) * P], attr[u][:, h * HALF + t, :],
                                               pl.ident[:, :])
                        ins.then_inc(attr_turned, 1)

                def body(*g):
                    n = g[3]
                    if has(n, 1):
                        turn_hot(*near(*g, 1))
                    if has(n, -2):
                        sum_parts(*near(*g, -2), 0)
                        sum_parts(*near(*g, -2), 1)
                    if kind == "gat" and has(n, -3):
                        turn_attr(*near(*g, -3))
                    if has(n, -1):
                        turn_probs(*near(*g, -1))
                    if has(n, -2):
                        for c in range(2, NPAIR):
                            sum_parts(*near(*g, -2), c)
                    if has(n):
                        turn_alpha(*g)
                    if has(n, 1):
                        spread(*near(*g, 1))

                turn_hot(0, 0, 0, 0)
                spread(0, 0, 0, 0)
                bodies(pe, body)

            @block.vector
            def _(v):
                def build_hot(i, k, u, n):
                    if kind == "gat":
                        if n >= S:
                            wait(v, part_done, NPAIR * (i - S + 1))
                    elif n >= 2:
                        wait(v, hot_turned, i - 1)
                        wait(v, hot_cast, i - 1)
                    out = hot[u] if kind == "gat" else hot_b[u % 2]
                    v.tensor_tensor(out[:, :, :], bc(pl.iota_free[:, :].unsqueeze(1), [P, G, P]),
                                    bc(pl.rank_col[:, bass.ds(i * G, G)].unsqueeze(2), [P, G, P]),
                                    ALU.is_equal).then_inc(hot_built, 1)

                def maxima(i, k, u, n):
                    wait(v, alpha_turned, i + 1)
                    wait(v, neg_loaded[u], 16 * (k + 1))
                    v.tensor_tensor_scan(fwd[:, :], neg[u][:, 0:P], alpha_t, 0.0, ALU.add, ALU.max).then_inc(fwd_done, 1)
                    wait(v, fwd_done, i + 1)
                    if n >= 1:
                        wait(v, prob_turned, i)
                    v.tensor_tensor_scan(seg_max[:, ::-1], neg[u][:, 2 * P - 1:P - 1:-1], fwd[:, ::-1], 0.0,
                                         ALU.add, ALU.max).then_inc(max_done, 1)
                    wait(v, max_done, i + 1)
                    if n >= 1:
                        wait(v, exp_done, i)
                    v.tensor_tensor(diff[:, :], alpha_t, seg_max[:, :], ALU.subtract).then_inc(diff_done, 1)

                def stepper(i):
                    at = [0]

                    def then(ins):
                        at[0] += 1
                        ins.then_inc(step, 1)
                        wait(v, step, i * STEPS + at[0])

                    return then

                def scores(i, k, u, n):
                    wait(v, gathered[u], 16 * G * (k + 1))
                    if n >= 1:
                        wait(v, alpha_turned, i)
                    if kind == "gat":
                        wait(v, q_done, i + 1)
                        s = prod[0][:, 0, 0:G * H].rearrange("p (t h) -> p t h", h=H)
                        v.tensor_tensor(s, q_ps[0][:, 0:G * H].rearrange("p (t h) -> p t h", h=H),
                                        rows[u][:, :, D:D + H], ALU.add).then_inc(q_used, 1)
                        wait(v, q_used, i + 1)
                        v.scalar_tensor_tensor(alpha[:, :, :], s, 0.01, s, ALU.mult, ALU.max).then_inc(alpha_done, 1)
                        return
                    then = stepper(i)
                    for h in range(2):
                        wait(v, q_done, 2 * i + h + 1)
                        t0, t1 = h * HALF, (h + 1) * HALF
                        q = q_ps[h][:, :].rearrange("p (t d) -> p t d", t=HALF)
                        if kind == "tconv":
                            e = e_ps[h][:, :].rearrange("p (t d) -> p t d", t=HALF)
                            kv = rows[u][:, t0:t1, :].rearrange("p t (a d) -> p t a d", a=2)
                            v.tensor_tensor(kv, kv, bc(e.unsqueeze(2), [P, HALF, 2, D]), ALU.add).then_inc(e_used, 1)
                            wait(v, e_used, 2 * i + h + 1)
                        if kind == "gatv2":
                            v.tensor_tensor(prod[h][:, :, :], q, rows[u][:, t0:t1, :], ALU.add).then_inc(q_used, 1)
                            wait(v, q_used, 2 * i + h + 1)
                            flat = prod[h][:, :, :].rearrange("p t d -> p (t d)")
                            then(v.scalar_tensor_tensor(flat, flat, 0.2, flat, ALU.mult, ALU.max))
                            then(v.tensor_tensor(prod[h][:, :, :], prod[h][:, :, :],
                                                 bc(w["att"][:, :].unsqueeze(1), [P, HALF, D]), ALU.mult))
                        else:
                            v.tensor_tensor(prod[h][:, :, :], q, rows[u][:, t0:t1, 0:D], ALU.mult).then_inc(q_used, 1)
                            wait(v, q_used, 2 * i + h + 1)
                        v.tensor_reduce(alpha[:, t0:t1, :], prod[h][:, :, :].rearrange("p t (h c) -> p t h c", c=C),
                                        AX.X, ALU.add).then_inc(alpha_done, 1)

                def angles(i, k, u, n):
                    then = stepper(i)
                    fl = "p t c -> p (t c)"
                    a, tn = ang[:, :, :].rearrange(fl), turns[:, :, :].rearrange(fl)
                    then(v.tensor_tensor(rel[:, :], rows[u][:, :, D + H], pl.weight_col[:, bass.ds(i * G, G)], ALU.subtract))
                    then(v.tensor_tensor(ang[:, :, :], bc(rel[:, :].unsqueeze(2), [P, G, 64]),
                                         bc(w["Wt"][:, :].unsqueeze(1), [P, G, 64]), ALU.mult))
                    then(v.tensor_tensor(ang[:, :, :], ang[:, :, :], bc(w["bt"][:, :].unsqueeze(1), [P, G, 64]), ALU.add))
                    then(v.tensor_scalar(tn, a, float(1 / (2 * np.pi)), MAGIC, ALU.mult, ALU.add))
                    then(v.tensor_scalar(tn, tn, MAGIC, None, ALU.subtract))
                    then(v.scalar_tensor_tensor(a, tn, -TWO_PI_HIGH, a, ALU.mult, ALU.add))
                    then(v.scalar_tensor_tensor(a, tn, -TWO_PI_LOW, a, ALU.mult, ALU.add))
                    if n >= S:
                        wait(v, cos_done, i - S + 1)
                    v.scalar_tensor_tensor(ang2[u][:, :, :].rearrange(fl), a, -1.0, a, ALU.mult, ALU.min
                                           ).then_inc(angle_done, 1)

                def messages(i, k, u, n):
                    wait(v, prob_copied, i + 1)
                    if n >= 1:
                        wait(v, part_done, NPAIR * i)
                    vals = rows[u][:, :, TW - D:TW] if kind in ("tconv", "mha") else rows[u][:, :, 0:D]
                    p = pm[:, 0:R].rearrange("p (t h) -> p t h", h=H)
                    v.tensor_copy(msg[:, :, D:D + H], p).then_inc(msg_done, 1)
                    v.tensor_tensor(msg[:, :, 0:D].rearrange("p t (h c) -> p t h c", c=C),
                                    vals.rearrange("p t (h c) -> p t h c", c=C),
                                    bc(p.unsqueeze(3), [P, G, H, C]), ALU.mult).then_inc(msg_done, 1)
                    v.tensor_tensor(msg[:, :, D + H:W], pm[:, R:2 * R].rearrange("p (t h) -> p t h", h=H),
                                    bc(pl.last_col[:, bass.ds(i * G, G)].unsqueeze(2), [P, G, H]), ALU.mult
                                    ).then_inc(msg_done, 1)

                def body(*g):
                    n = g[3]
                    if has(n, -1):
                        maxima(*near(*g, -1))
                    if has(n):
                        scores(*g)
                    if kind == "gat":
                        if has(n):
                            angles(*g)
                        if n == NG - 1:
                            v.wait_ge(attr_turned, 2 * (NG - S))
                            v.memset(attr[(NG - 1) % S][:, :, 64:D], 0.0).then_inc(tail_zeroed, 1)
                    if has(n, -1):
                        messages(*near(*g, -1))
                    if not act_builds and has(n, 2):
                        build_hot(*near(*g, 2))

                if not act_builds:
                    build_hot(0, 0, 0, 0)
                    build_hot(1, 0, 1, 1)
                bodies(v, body)
        sem.close()
    return last_got, passes, done_blocks


def gather_last(pool, pl, part_tab, last_rows, got, first, end):
    for g in range(first, end):
        pool.indirect_dma_start(out=last_rows[:, g, :], out_offset=None, in_=part_tab[0:min(end * P, pl.TT) * P, :],
                                in_offset=bass.IndirectOffsetOnAxis(ap=pl.tile_last_i[:, g:g + 1], axis=0)
                                ).then_inc(got, 16)



def node_stage(nc, pl, sems, merge=None, after=None, vectors=(), norm_input=False, proj=None, pieces=(), out=None,
               ffn=None):
    sem = Stage(nc, sems)
    TB, NB = pl.TB, pl.NB
    NT = TB * P
    edges = [0] + [FIRST_CHUNK + -(-(NB - FIRST_CHUNK) * c // (CHUNKS - 1)) for c in range(CHUNKS)]
    chunks = list(zip(edges, edges[1:]))
    most = max(hi - lo for lo, hi in chunks)
    ps = pl.banks
    HALVES = ((0, 4), (4, TB))
    if merge:
        H, scale, last_rows, (last_got, merges, done_blocks) = merge
        W = D + 2 * H
        C = D // H
        head = pl.head8 if H == 8 else pl.head4
        part_tab = pl.part_tab[H]
    if proj:
        weights, biases, dest, gat = proj
        n_out = len(weights)
        n_cols = sum(d in ("k", "v", "xl", "z") for d in dest)
        TW = D + 16 if gat else D * n_cols
        table = pl.gat_tab if gat else (pl.kv_tab if n_cols == 2 else pl.xl_tab)
        q_tab = pl.er_tab if gat else pl.q_tab

    with ExitStack() as ctx:
        def sb(name, shape, dt=F32):
            return sem.tensor(ctx, name, shape, dt)

        if merge:
            num, den, top = sb("num", [P, NT]), sb("den", [H, NT]), sb("top", [H, NT])
            num_run, den_run, top_run = sb("num_run", [P, 1 + NT]), sb("den_run", [H, 1 + NT]), sb("top_run", [H, 1 + NT])
            keep, take = sb("keep", [H, NT]), sb("take", [H, NT])
            keep_e, take_e = sb("keep_e", [H, NT]), sb("take_e", [H, NT])
            first = sb("first", [P, TB, W])
            carry = sb("carry", [P, TB, D])
            m_run, m_all = sb("m_run", [P, TB, H]), sb("m_all", [P, TB, H])
            d_own, d_run = sb("d_own", [P, TB, H]), sb("d_run", [P, TB, H])
            f_own, f_run = sb("f_own", [P, TB, H]), sb("f_run", [P, TB, H])
            s_own, s_run = sb("s_own", [P, TB, H]), sb("s_run", [P, TB, H])
            own = sb("own", [P, NB, W])
            share, weight = sb("share", [P, NB, H]), sb("weight", [P, NB, H])
            att = pl.hn if after == "ffn" else own[:, :, 0:D]
            first_rows = part_tab.rearrange("(t r) w -> t (r w)", r=P)
            full_tiles = pl.TT // P * P
            own_got = [sem.lasting(f"own_gathered{c}")[0] for c in range(len(chunks))]
            turned_tiles, copied = sem("turned_tiles"), sem("copied")
            args_ready, exps_ready, spread = sem("args_ready"), sem("exps_ready"), sem("spread")
            carried, back = sem("carried"), sem("back")
            firsts_zeroed, firsts_loaded, firsts_joined = sem("firsts_zeroed"), sem("firsts_loaded"), sem("firsts_joined")
            firsts_stored, join_args, join_exps = sem("firsts_stored"), sem("join_args"), sem("join_exps")
            first_dmas = (full_tiles > 0) + (pl.TT > full_tiles)
        stats, moments = sb("stats", [P, NB, 6]), sb("moments", [P, NB, 2])
        std, rstd, shift = sb("std", [P, NB]), sb("rstd", [P, NB]), sb("shift", [P, NB])
        if after == "ffn":
            W1, b1, W2 = ffn
            PARTS = W1.shape[1] // P
            h = pl.res
            below = sb("below", [P, most, D])
            w1, w2, b1_col = sb("w1", [P, PARTS * P]), sb("w2", [P, PARTS, D]), sb("b1_col", [P, PARTS])
            ffn_t = [sb(f"ffn_t{u}", [P, P]) for u in range(2)]
            hidden = [sb(f"hidden{u}", [P, PARTS, P]) for u in range(2)]
            hidden_ps, ffn_ps = ps[4:6], ps[6:8]
            ffn_loaded = sem("ffn_loaded")
            elu_args, elu_exps, ffn_ready = sem("elu_args"), sem("elu_exps"), sem("ffn_ready")
            ffn_turned, ffn_copied = sem("ffn_turned"), sem("ffn_copied")
            hidden_done, hidden_used, ffn_done, ffn_added = sem("hidden_done"), sem("hidden_used"), sem("ffn_done"), sem("ffn_added")
        normed = norm_input or after in ("norm", "norm_stream")
        moments_ready, std_ready = sem("moments_ready"), sem("std_ready")
        rows = [sb(f"row{n}", [P, D]) for n in range(len(vectors))]
        vectors_loaded, pieces_loaded = sem("vectors_loaded"), sem("pieces_loaded")
        dve = sem("dve")
        stream_ready, stream_stored = sem("stream_ready"), sem("stream_stored")
        if proj:
            wcat = sb("wcat", [P, n_out * D])
            bias = sb("bias", [P, n_out * D])
            ht = [sb(f"ht{u}", [P, P]) for u in range(2)]
            q_rows = sb("q_rows", [P, NB, 8 if gat else D])
            t_rows = sb("t_rows", [P, NB, TW])
            if gat:
                a_l, a_r, prod = sb("a_l", [P, D]), sb("a_r", [P, D]), sb("prod", [P, most, D])
            loaded, stored = sem("loaded"), sem("stored")
            scattered, projections = sem.lasting("scattered")
            input_ready = sem("input_ready")
            terms_ready = sem("terms_ready")
            block_ready = sem("block_ready")
            turned, turned_copied, multiplied = sem("turned"), sem("turned_copied"), sem("multiplied")
            written = sem("written")
            in_ps, out_ps = ps[0:2], ps[2:4] if after == "ffn" else ps[2:8]
            x_in = pl.res if gat else pl.hn
            n_loads = n_out + sum(b is not None for b in biases) + (2 if gat else 0)
            if after == "norm":
                gamma_col, beta_col = sb("gamma_col", [P, 1]), sb("beta_col", [P, 1])
                beta_wide = sb("beta_wide", [P, P])
                cols_loaded, beta_ready, beta_done = sem("cols_loaded"), sem("beta_ready"), sem("beta_done")
                weights_ready = sem("weights_ready")
            place = {"q": (q_rows, 0), "res": (pl.res, 0), "k": (t_rows, 0), "xl": (t_rows, 0), "z": (t_rows, 0), "v": (t_rows, D)}
            groups = []
            for n, (d, b) in enumerate(zip(dest, biases)):
                t, lo = place[d]
                if groups and groups[-1][2] is t and groups[-1][3] + (groups[-1][1] - groups[-1][0]) == lo:
                    groups[-1][1] += D
                else:
                    groups.append([n * D, (n + 1) * D, t, lo, b is not None or after == "norm"])

        def rows_ready(eng, c):
            if gat:
                eng.wait_ge(terms_ready, c + 1)
            else:
                eng.wait_ge(written, chunks[c][1] * len(groups))

        with nc.Block() as block:
            @block.sync
            def _(sp):
                for t, a in zip(rows, vectors):
                    sp.dma_start(t[:, :], a.partition_broadcast(P)).then_inc(vectors_loaded, 16)
                if proj:
                    for n, wt in enumerate(weights):
                        to = wcat[:, n * D:(n + 1) * D]
                        if len(wt.shape) == 3:
                            to = to.rearrange("d (h k) -> d h k", h=wt.shape[0])
                            wt = wt.rearrange("h d k -> d h k")
                        sp.dma_start(to, wt).then_inc(loaded, 16)
                    for n, b in enumerate(biases):
                        if b is not None:
                            sp.dma_start(bias[:, n * D:(n + 1) * D], b.partition_broadcast(P)).then_inc(loaded, 16)
                    if gat:
                        for t, a in ((a_l, gat[0]), (a_r, gat[1])):
                            sp.dma_start(t[:, :], a.rearrange("h k -> (h k)").partition_broadcast(P)).then_inc(loaded, 16)
                if after == "norm":
                    for t, a in ((gamma_col, vectors[1]), (beta_col, vectors[2])):
                        sp.dma_start(t[:, :], a.rearrange("(p a) -> p a", a=1), allow_slow_non_contiguous=True
                                     ).then_inc(cols_loaded, 16)
                if after == "ffn":
                    sp.dma_start(w1[:, :], W1).then_inc(ffn_loaded, 16)
                    sp.dma_start(w2[:, :, :], W2.rearrange("(c p) n -> p c n", p=P)).then_inc(ffn_loaded, 16)
                    sp.dma_start(b1_col[:, :], b1.rearrange("(c p) -> p c", p=P), allow_slow_non_contiguous=True
                                 ).then_inc(ffn_loaded, 16)
                for t, a in pieces:
                    sp.dma_start(t[:, :], a if len(a.shape) == 2 else a.partition_broadcast(P)).then_inc(pieces_loaded, 16)
                if merge:
                    def move_firsts(cols, done, load):
                        def move(tile, rows):
                            dst, src = (tile, rows) if load else (rows, tile)
                            sp.dma_start(dst, src).then_inc(done, 16)

                        n = full_tiles // P
                        if n:
                            move(first[:, 0:n, 0:cols], first_rows[0:full_tiles, 0:cols].rearrange("(g p) w -> p g w", p=P))
                        if pl.TT > full_tiles:
                            move(first[0:pl.TT - full_tiles, n, 0:cols], first_rows[full_tiles:pl.TT, 0:cols])

                    sp.wait_ge(firsts_zeroed, 1)
                    move_firsts(W, firsts_loaded, True)
                    sp.wait_ge(firsts_joined, 1)
                    move_firsts(D + H, firsts_stored, False)
                    sp.wait_ge(firsts_stored, 16 * first_dmas)
                n_stored = 0
                for c, (lo, hi) in enumerate(chunks):
                    if proj:
                        rows_ready(sp, c)
                        sp.dma_start(table[lo * P:hi * P, :].rearrange("(b p) w -> p b w", p=P), t_rows[:, lo:hi, :]
                                     ).then_inc(stored, 16)
                    if out is not None:
                        sp.wait_ge(stream_ready, c + 1)
                        full = min(hi, pl.N // P)
                        if full > lo:
                            sp.dma_start(out[lo * P:full * P, :].rearrange("(b p) c -> p b c", p=P), pl.x_sb[:, lo:full, :]
                                         ).then_inc(stream_stored, 16)
                            n_stored += 1
                        if lo <= full < hi and pl.N > full * P:
                            sp.dma_start(out[full * P:pl.N, :], pl.x_sb[0:pl.N - full * P, full, :]).then_inc(stream_stored, 16)
                            n_stored += 1
                if proj:
                    sp.wait_ge(stored, 16 * len(chunks))
                if out is not None:
                    sp.wait_ge(stream_stored, 16 * n_stored)
                if pieces:
                    sp.wait_ge(pieces_loaded, 16 * len(pieces))

            @block.gpsimd
            def _(pool):
                if merge:
                    gather_last(pool, pl, part_tab, last_rows, last_got, done_blocks, TB)
                    pool.wait_ge(firsts_stored, 16 * first_dmas)
                    for c, (lo, hi) in enumerate(chunks):
                        for b in range(lo, hi):
                            pool.indirect_dma_start(out=own[:, b, :], out_offset=None, in_=part_tab,
                                                    in_offset=bass.IndirectOffsetOnAxis(ap=pl.part_i[:, b:b + 1], axis=0)
                                                    ).then_inc(own_got[c], 16)
                if proj:
                    for c, (lo, hi) in enumerate(chunks):
                        if gat:
                            rows_ready(pool, c)
                        for b in range(lo, hi):
                            if not gat:
                                pool.wait_ge(written, (b + 1) * len(groups))
                            pool.indirect_dma_start(out=q_tab, out_offset=bass.IndirectOffsetOnAxis(
                                ap=pl.compact_i[:, b:b + 1], axis=0), in_=q_rows[:, b, :], in_offset=None
                                ).then_inc(scattered, 16)
                    pool.wait_ge(scattered, 16 * NB * (projections + 1))

            @block.tensor
            def _(pe):
                sem.clear_last(pe)
                if after == "norm":
                    pe.wait_ge(loaded, 16 * n_loads)
                    pe.wait_ge(beta_ready, 1)
                    pe.matmul(ps[7][:, 0:n_out * D], beta_wide[:, :], wcat[:, :], start=True, stop=True).then_inc(beta_done, 1)
                if merge:
                    pe.wait_ge(last_got, 16 * TB * (merges + 1))
                    for lo, hi, n_rows, bank in ((0, D, P, 0), (D, D + H, H, 2), (D + H, W, H, 4)):
                        for half, (a, b) in enumerate(HALVES):
                            for g in range(a, b):
                                ins = pe.transpose(ps[bank + half][0:n_rows, (g - a) * P:(g - a + 1) * P],
                                                   last_rows[:, g, lo:hi], pl.ident[:, :])
                            ins.then_inc(turned_tiles, 1)
                    pe.wait_ge(exps_ready, 2)
                    pe.wait_ge(copied, 6)
                    for f, bank in ((keep_e, 0), (take_e, 2)):
                        for half, (a, b) in enumerate(HALVES):
                            pe.matmul(ps[bank + half][:, 0:(b - a) * P], head[0:H, :], f[:, a * P:b * P], start=True,
                                      stop=True).then_inc(spread, 1)
                    pe.wait_ge(carried, 2)
                    for half, (a, b) in enumerate(HALVES):
                        for g in range(a, b):
                            ins = pe.transpose(ps[4 + half][:, (g - a) * P:(g - a + 1) * P], num_run[:, g * P:(g + 1) * P],
                                               pl.ident[:, :])
                        ins.then_inc(back, 1)
                    for g in range(TB):
                        pe.transpose(ps[6][:, 2 * g * H:(2 * g + 1) * H], den_run[:, g * P:(g + 1) * P], pl.ident[0:H, 0:H])
                        ins = pe.transpose(ps[6][:, (2 * g + 1) * H:(2 * g + 2) * H], top_run[:, g * P:(g + 1) * P],
                                           pl.ident[0:H, 0:H])
                    ins.then_inc(back, 1)
                if proj:
                    pe.wait_ge(loaded, 16 * n_loads)
                    if after == "norm":
                        pe.wait_ge(weights_ready, 1)

                    def turn(b):
                        pe.wait_ge(block_ready, b + 1)
                        wait(pe, turned_copied, b - 1)
                        pe.transpose(in_ps[b % 2][:, 0:P], x_in[:, b, :], pl.ident[:, :]).then_inc(turned, 1)

                    def multiply(c):
                        lo, hi = chunks[c]
                        turn(lo)
                        for b in range(lo, hi):
                            if b + 1 < hi:
                                turn(b + 1)
                            pe.wait_ge(turned_copied, b + 1)
                            wait(pe, written, (b - len(out_ps) + 1) * len(groups))
                            pe.matmul(out_ps[b % len(out_ps)][:, 0:n_out * D], ht[b % 2][:, :], wcat[:, :], start=True,
                                      stop=True).then_inc(multiplied, 1)

                def ffn_turn(b):
                    wait(pe, ffn_copied, b - 1)
                    pe.transpose(ps[b % 2][:, 0:P], pl.hn[:, b, :], pl.ident[:, :]).then_inc(ffn_turned, 1)

                def ffn_hidden(b):
                    pe.wait_ge(ffn_copied, b + 1)
                    wait(pe, hidden_used, b - 1)
                    for k in range(PARTS):
                        ins = pe.matmul(hidden_ps[b % 2][:, k * P:(k + 1) * P], w1[:, k * P:(k + 1) * P], ffn_t[b % 2][:, :],
                                        start=True, stop=True)
                    ins.then_inc(hidden_done, 1)

                def ffn_out(b):
                    pe.wait_ge(hidden_used, b + 1)
                    wait(pe, ffn_added, b - 1)
                    for k in range(PARTS):
                        ins = pe.matmul(ffn_ps[b % 2][:, 0:D], hidden[b % 2][:, k, :], w2[:, k, :], start=(k == 0),
                                        stop=(k == PARTS - 1))
                    ins.then_inc(ffn_done, 1)

                def feed_forward(c):
                    if c == 0:
                        pe.wait_ge(ffn_loaded, 48)
                    lo, hi = chunks[c]
                    pe.wait_ge(ffn_ready, c + 1)
                    ffn_turn(lo)
                    for b in range(lo, hi):
                        if b + 1 < hi:
                            ffn_turn(b + 1)
                        ffn_hidden(b)
                        if b > lo:
                            ffn_out(b - 1)
                    ffn_out(hi - 1)

                for step in range(len(chunks) + 2):
                    c = step - 1
                    if after == "ffn" and 0 <= c < len(chunks):
                        feed_forward(c)
                    c = step - 2
                    if proj and 0 <= c:
                        multiply(c)

            @block.scalar
            def _(act):
                def tiles():
                    n = 0
                    for to, n_rows, bank in ((num, P, 0), (den, H, 2), (top, H, 4)):
                        for half, (a, b) in enumerate(HALVES):
                            n += 1
                            act.wait_ge(turned_tiles, n)
                            act.activation(to[:, a * P:b * P], ps[bank + half][0:n_rows, 0:(b - a) * P], ACT.Copy
                                           ).then_inc(copied, 1)
                    act.wait_ge(args_ready, 1)
                    act.activation(keep_e[:, :], keep[:, :], ACT.Exp, scale=scale).then_inc(exps_ready, 1)
                    act.activation(take_e[:, :], take[:, :], ACT.Exp, scale=scale).then_inc(exps_ready, 1)
                    act.wait_ge(join_args, 1)
                    act.activation(f_own[:, :, :], d_own[:, :, :], ACT.Exp, scale=scale).then_inc(join_exps, 1)
                    act.activation(f_run[:, :, :], d_run[:, :, :], ACT.Exp, scale=scale).then_inc(join_exps, 1)

                norms = [0]

                def roots(c):
                    lo, hi = chunks[c]
                    norms[0] += 1
                    act.wait_ge(moments_ready, norms[0])
                    act.activation(std[:, lo:hi], moments[:, lo:hi, 1], ACT.Sqrt, bias=pl.eps[:, 0:1]).then_inc(std_ready, 1)

                def elus(c):
                    lo, hi = chunks[c]
                    act.wait_ge(elu_args, c + 1)
                    act.activation(below[:, 0:hi - lo, :], below[:, 0:hi - lo, :], ACT.Exp).then_inc(elu_exps, 1)

                def ffn_copy(b):
                    act.wait_ge(ffn_turned, b + 1)
                    wait(act, hidden_done, b - 1)
                    act.activation(ffn_t[b % 2][:, :], ps[b % 2][:, 0:P], ACT.Copy).then_inc(ffn_copied, 1)

                def ffn_relu(b):
                    act.wait_ge(hidden_done, b + 1)
                    wait(act, ffn_done, b - 1)
                    for k in range(PARTS):
                        ins = act.activation(hidden[b % 2][:, k, :], hidden_ps[b % 2][:, k * P:(k + 1) * P], ACT.Relu,
                                             bias=b1_col[:, k:k + 1])
                    ins.then_inc(hidden_used, 1)

                def feed_forward(c):
                    if c == 0:
                        act.wait_ge(ffn_loaded, 48)
                    lo, hi = chunks[c]
                    ffn_copy(lo)
                    for b in range(lo, hi):
                        if b + 1 < hi:
                            ffn_copy(b + 1)
                        ffn_relu(b)

                def inputs(c):
                    act.wait_ge(input_ready, c + 1)

                    def put(b):
                        if norm_input:
                            act.activation(x_in[:, b, :], pl.x_sb[:, b, :], ACT.Relu, scale=rstd[:, b:b + 1],
                                           bias=shift[:, b:b + 1]).then_inc(block_ready, 1)
                        elif after == "norm":
                            act.activation(x_in[:, b, :], att[:, b, :], ACT.Identity, scale=rstd[:, b:b + 1],
                                           bias=shift[:, b:b + 1]).then_inc(block_ready, 1)
                        else:
                            act.sem_inc(block_ready, 1)

                    lo, hi = chunks[c]
                    put(lo)
                    for b in range(lo, hi):
                        if b + 1 < hi:
                            put(b + 1)
                        act.wait_ge(turned, b + 1)
                        wait(act, multiplied, b - 1)
                        act.activation(ht[b % 2][:, :], in_ps[b % 2][:, 0:P], ACT.Copy).then_inc(turned_copied, 1)

                if merge:
                    tiles()
                if after == "ffn":
                    for step in range(len(chunks) + 2):
                        if step < len(chunks):
                            elus(step)
                            roots(step)
                        if 1 <= step <= len(chunks):
                            feed_forward(step - 1)
                            roots(step - 1)
                        if step >= 2:
                            inputs(step - 2)
                else:
                    for c in range(len(chunks) + 1):
                        if proj and c >= 1:
                            inputs(c - 1)
                        if normed and c < len(chunks):
                            roots(c)

            @block.vector
            def _(v):
                link = chain(v, dve)

                def tiles():
                    v.memset(first[:, :, :], 0.0).then_inc(firsts_zeroed, 1)
                    for t in (num_run, den_run, top_run):
                        ins = v.memset(t[:, 0:1], 0.0)
                    link(ins)
                    v.wait_ge(copied, 6)
                    link(v.tensor_tensor_scan(top_run[:, 1:1 + NT], pl.whole_pen[0:H, :], top[:, :], 0.0, ALU.add, ALU.max))
                    link(v.tensor_tensor(keep[:, :], top_run[:, 0:NT], pl.whole_pen[0:H, :], ALU.add))
                    link(v.tensor_tensor(keep[:, :], keep[:, :], top_run[:, 1:1 + NT], ALU.subtract))
                    v.tensor_tensor(take[:, :], top[:, :], top_run[:, 1:1 + NT], ALU.subtract).then_inc(args_ready, 1)
                    v.wait_ge(exps_ready, 2)
                    link(v.tensor_tensor(den[:, :], den[:, :], take_e[:, :], ALU.mult))
                    v.tensor_tensor_scan(den_run[:, 1:1 + NT], keep_e[:, :], den[:, :], 0.0, ALU.mult, ALU.add).then_inc(carried, 1)
                    v.wait_ge(spread, 4)
                    for half, (a, b) in enumerate(HALVES):
                        link(v.tensor_tensor(num[:, a * P:b * P], num[:, a * P:b * P], ps[2 + half][:, 0:(b - a) * P], ALU.mult))
                    a = HALVES[0][1] * P
                    link(v.tensor_tensor_scan(num_run[:, 1:1 + a], ps[0][:, 0:a], num[:, 0:a], 0.0, ALU.mult, ALU.add))
                    v.tensor_tensor_scan(num_run[:, 1 + a:1 + NT], ps[1][:, 0:NT - a], num[:, a:NT], num_run[:, a:a + 1],
                                         ALU.mult, ALU.add).then_inc(carried, 1)

                    v.wait_ge(back, 3)
                    v.wait_ge(firsts_loaded, 16 * first_dmas)
                    into = ps[6][:, 0:2 * TB * H].rearrange("p (g k h) -> p g k h", k=2, h=H)
                    link(v.tensor_tensor(m_run[:, :, :], into[:, :, 1, :], bc(pl.goes_on_pen[:, :].unsqueeze(2), [P, TB, H]), ALU.add))
                    link(v.tensor_tensor(m_all[:, :, :], first[:, :, D + H:W], m_run[:, :, :], ALU.max))
                    v.tensor_tensor(d_own[:, :, :], first[:, :, D + H:W], m_all[:, :, :], ALU.subtract)
                    v.tensor_tensor(d_run[:, :, :], m_run[:, :, :], m_all[:, :, :], ALU.subtract).then_inc(join_args, 1)
                    v.wait_ge(join_exps, 2)
                    v.tensor_tensor(s_own[:, :, :], first[:, :, D:D + H], f_own[:, :, :], ALU.mult)
                    v.tensor_tensor(s_run[:, :, :], into[:, :, 0, :], f_run[:, :, :], ALU.mult)
                    x = first[:, :, 0:D].rearrange("p g (h c) -> p g h c", c=C)
                    v.tensor_tensor(x, x, bc(f_own[:, :, :].unsqueeze(3), [P, TB, H, C]), ALU.mult)
                    for half, (a, b) in enumerate(HALVES):
                        link(v.tensor_tensor(carry[:, a:b, :].rearrange("p g (h c) -> p g h c", c=C),
                                             ps[4 + half][:, 0:(b - a) * D].rearrange("p (g h c) -> p g h c", h=H, c=C),
                                             bc(f_run[:, a:b, :].unsqueeze(3), [P, b - a, H, C]), ALU.mult))
                    link(v.tensor_tensor(first[:, :, D:D + H], s_own[:, :, :], s_run[:, :, :], ALU.add))
                    v.tensor_tensor(first[:, :, 0:D], first[:, :, 0:D], carry[:, :, :], ALU.add).then_inc(firsts_joined, 1)

                def join(c):
                    lo, hi = chunks[c]
                    n, s = hi - lo, slice(lo, hi)
                    v.wait_ge(own_got[c], 16 * n * (merges + 1))
                    link(v.tensor_scalar(share[:, s, :], own[:, s, D:D + H], TINY, None, ALU.max))
                    link(v.reciprocal(weight[:, s, :], share[:, s, :]))
                    link(v.tensor_tensor(weight[:, s, :], weight[:, s, :], bc(pl.has_edges[:, s].unsqueeze(2), [P, n, H]), ALU.mult))
                    link(v.tensor_tensor(att[:, s, :].rearrange("p b (h c) -> p b h c", c=C),
                                         own[:, s, 0:D].rearrange("p b (h c) -> p b h c", c=C),
                                         bc(weight[:, s, :].unsqueeze(3), [P, n, H, C]), ALU.mult))

                norms = [0]

                def mean_and_spread(c, x):
                    norms[0] += 1
                    lo, hi = chunks[c]
                    s = slice(lo, hi)
                    for b in range(lo, hi):
                        ins = v.bn_stats(stats[:, b, :], x[:, b, :])
                    link(ins)
                    for b in range(lo, hi):
                        ins = v.bn_aggr(moments[:, b, :], stats[:, b, :])
                    ins.then_inc(moments_ready, 1)
                    if proj and c >= 1 and after != "ffn":
                        products(c - 1)
                    v.wait_ge(std_ready, norms[0])
                    link(v.reciprocal(rstd[:, s], std[:, s]))
                    return v.scalar_tensor_tensor(shift[:, s], moments[:, s, 0], -1.0, rstd[:, s], ALU.mult, ALU.mult)

                def use(c):
                    lo, hi = chunks[c]
                    n, s = hi - lo, slice(lo, hi)
                    if after == "stream":
                        return v.tensor_tensor(pl.x_sb[:, s, :], pl.x_sb[:, s, :], att[:, s, :], ALU.add)
                    if after == "hidden":
                        return v.tensor_tensor(pl.hn[:, s, :], att[:, s, :], pl.res[:, s, :], ALU.add)
                    if after in ("norm", "norm_stream"):
                        if c == 0:
                            v.wait_ge(vectors_loaded, 16 * len(vectors))
                        r = [bc(t[:, :].unsqueeze(1), [P, n, D]) for t in rows]
                        hn = pl.hn[:, s, :]
                        link(v.tensor_tensor(att[:, s, :], att[:, s, :], r[0], ALU.add))
                        link(v.tensor_scalar(att[:, s, :], att[:, s, :], 0.0, None, ALU.max))
                        if after == "norm":
                            return mean_and_spread(c, att)
                        link(mean_and_spread(c, att))
                        for b in range(lo, hi):
                            ins = v.tensor_scalar(pl.hn[:, b, :], att[:, b, :], rstd[:, b:b + 1], shift[:, b:b + 1],
                                                  ALU.mult, ALU.add)
                        link(ins)
                        link(v.tensor_tensor(hn, hn, r[1], ALU.mult))
                        return v.tensor_tensor(pl.x_sb[:, s, :], pl.x_sb[:, s, :], hn, ALU.add)
                    flat = "p b d -> p (b d)"
                    af, hf, ef = pl.hn[:, s, :].rearrange(flat), h[:, s, :].rearrange(flat), below[:, 0:n, :].rearrange(flat)
                    v.tensor_scalar(ef, af, 0.0, None, ALU.min).then_inc(elu_args, 1)
                    link(v.scalar_tensor_tensor(hf, af, 0.0, hf, ALU.max, ALU.add))
                    v.wait_ge(elu_exps, c + 1)
                    link(v.scalar_tensor_tensor(hf, ef, -1.0, hf, ALU.add, ALU.add))
                    link(mean_and_spread(c, h))
                    for b in range(lo, hi):
                        ins = v.tensor_scalar(pl.hn[:, b, :], h[:, b, :], rstd[:, b:b + 1], shift[:, b:b + 1], ALU.mult, ALU.add)
                    link(ins)
                    link(v.tensor_tensor(pl.hn[:, s, :], pl.hn[:, s, :], bc(rows[0][:, :].unsqueeze(1), [P, n, D]), ALU.mult))
                    return v.tensor_tensor(pl.hn[:, s, :], pl.hn[:, s, :], bc(rows[1][:, :].unsqueeze(1), [P, n, D]), ALU.add)

                def feed_forward(c):
                    lo, hi = chunks[c]
                    link(v.tensor_tensor(pl.x_sb[:, lo:hi, :], pl.x_sb[:, lo:hi, :], h[:, lo:hi, :], ALU.add))
                    for b in range(lo, hi):
                        v.wait_ge(ffn_done, b + 1)
                        v.tensor_tensor(pl.x_sb[:, b, :], pl.x_sb[:, b, :], ffn_ps[b % 2][:, 0:D], ALU.add).then_inc(ffn_added, 1)
                    v.wait_ge(ffn_added, hi)

                def products(c):
                    if c == 0:
                        v.wait_ge(loaded, 16 * n_loads)
                    for b in range(*chunks[c]):
                        v.wait_ge(multiplied, b + 1)
                        for first, last, t, lo, with_bias in groups:
                            got, to = out_ps[b % len(out_ps)][:, first:last], t[:, b, lo:lo + last - first]
                            if with_bias:
                                ins = v.tensor_tensor(to, got, bias[:, first:last], ALU.add)
                            else:
                                ins = v.tensor_copy(to, got)
                            ins.then_inc(written, 1)
                    if gat:
                        lo, hi = chunks[c]
                        n, s = hi - lo, slice(lo, hi)
                        K = gat[0].shape[1]
                        v.wait_ge(written, hi * len(groups))
                        for a, to in ((a_l, t_rows[:, s, D:D + D // K]), (a_r, q_rows[:, s, :])):
                            link(v.tensor_tensor(prod[:, 0:n, :], t_rows[:, s, 0:D], bc(a[:, :].unsqueeze(1), [P, n, D]), ALU.mult))
                            link(v.tensor_reduce(to, prod[:, 0:n, :].rearrange("p b (h k) -> p b h k", k=K), AX.X, ALU.add))
                        v.memset(t_rows[:, s, D + 9:TW], 0.0)
                        v.tensor_copy(t_rows[:, s, D + 8], pl.node_vec_sb[:, s]).then_inc(terms_ready, 1)

                if after == "norm":
                    v.wait_ge(cols_loaded, 32)
                    v.tensor_copy(beta_wide[:, :], bc(beta_col[:, :], [P, P])).then_inc(beta_ready, 1)
                    v.wait_ge(beta_done, 1)
                    v.tensor_copy(bias[:, :], ps[7][:, 0:n_out * D])
                    v.tensor_scalar(wcat[:, :], wcat[:, :], gamma_col[:, 0:1], None, ALU.mult).then_inc(weights_ready, 1)
                    v.wait_ge(weights_ready, 1)
                if after == "norm_stream":
                    v.wait_ge(vectors_loaded, 16 * len(vectors))
                    link(v.tensor_tensor(pl.x_sb[:, :, :], pl.x_sb[:, :, :], bc(rows[2][:, :].unsqueeze(1), [P, NB, D]), ALU.add))
                if after == "stream":
                    link(v.tensor_tensor(pl.x_sb[:, :, :], pl.x_sb[:, :, :], pl.res[:, :, :], ALU.add))
                if merge:
                    tiles()
                if after == "ffn":
                    v.wait_ge(vectors_loaded, 16 * len(vectors))
                    link(v.tensor_tensor(pl.x_sb[:, :, :], pl.x_sb[:, :, :], bc(rows[2][:, :].unsqueeze(1), [P, NB, D]), ALU.add))
                    for step in range(len(chunks) + 2):
                        if step < len(chunks):
                            join(step)
                            use(step).then_inc(ffn_ready, 1)
                        if 1 <= step <= len(chunks):
                            feed_forward(step - 1)
                            mean_and_spread(step - 1, pl.x_sb).then_inc(input_ready, 1)
                        if step >= 2:
                            products(step - 2)
                else:
                    for c in range(len(chunks)):
                        ins = None
                        if merge:
                            join(c)
                            ins = use(c)
                        if norm_input:
                            if ins is not None:
                                link(ins)
                            ins = mean_and_spread(c, pl.x_sb)
                        ins.then_inc(input_ready if proj else stream_ready, 1)
                        if proj and c >= 1 and not normed:
                            products(c - 1)
                    if proj:
                        products(len(chunks) - 1)
        sem.close()


def gnn_kernel(nc, a, out):
    sems = {"sets": ([], []), "left": [], "lasting": {}, "stages": 0}
    with ExitStack() as ctx:
        pl = Plan(nc, ctx, a["x"], a["src"], a["edge_attr_64"])
        def tile(c, name, shape):
            return c.enter_context(nc.sbuf_tensor(name, shape, F32))

        last_flat = tile(ctx, "last_rows", [P, pl.TB * (D + 16)])
        last_rows = {H: last_flat[:, 0:pl.TB * (D + 2 * H)].rearrange("p (g w) -> p g w", w=D + 2 * H) for H in (8, 4)}

        def sweep(kind, H, tab, q_tab, scale, w):
            return H, scale, last_rows[H], edge_sweep(nc, pl, sems, kind, H, tab, q_tab, pl.part_tab[H], last_rows[H], scale, w)

        setup_graph(nc, pl, sems, a["x"], a["src"], a["dst"], a["edge_weight"], a["node_vec"])

        with ExitStack() as c:
            w = {k: tile(c, "gat_" + k, [P, 64]) for k in ("Wt", "bt")}
            node_stage(nc, pl, sems, norm_input=True,
                       proj=([a["L0_gnn_W_fc"]], [None], ["z"], (a["L0_gnn_a_l"], a["L0_gnn_a_r"])),
                       pieces=[(w["Wt"], a["L1_gnn_Wt"].rearrange("a c -> (a c)")), (w["bt"], a["L1_gnn_bt"])])
            parts = sweep("gat", 8, pl.gat_tab, pl.er_tab, 1.0, w)

        def conv(n):
            w = {k: a[f"L1_gnn_{k}{n}"] for k in ("Wq", "bq", "Wk", "bk", "Wv", "bv", "Wskip", "bskip")}
            return [w["Wq"], w["Wk"], w["Wv"], w["Wskip"]], [w["bq"], w["bk"], w["bv"], w["bskip"]], ["q", "k", "v", "res"], None

        for n in "12":
            with ExitStack() as c:
                We = tile(c, "We" + n, [P, D])
                stage = dict(proj=conv(n), pieces=[(We, a["L1_gnn_We" + n])])
                if n == "1":
                    node_stage(nc, pl, sems, merge=parts, after="ffn", norm_input=True,
                               vectors=[a["L0_gnn_ln_gamma"], a["L0_gnn_ln_beta"], a["L0_gnn_b2"]],
                               ffn=(a["L0_gnn_W1"], a["L0_gnn_b1"], a["L0_gnn_W2"]), **stage)
                else:
                    node_stage(nc, pl, sems, merge=parts, after="hidden", **stage)
                parts = sweep("tconv", 4, pl.kv_tab, pl.q_tab, 32 ** -0.5, {"We": We})

        w = {k: a[f"L2_gnn_{k}"] for k in ("Wq", "bq", "Wk", "bk", "Wv", "bv", "Wr", "br")}
        node_stage(nc, pl, sems, merge=parts, after="stream", norm_input=True,
                   proj=([w["Wq"], w["Wk"], w["Wv"], w["Wr"]], [w["bq"], w["bk"], w["bv"], w["br"]],
                         ["q", "k", "v", "res"], None))
        parts = sweep("mha", 4, pl.kv_tab, pl.q_tab, 32 ** -0.5, {})

        def post(n):
            return [a["L3_gnn_b" + n], a["L3_gnn_g" + n], a["L3_gnn_be" + n]]

        for n in "12":
            with ExitStack() as c:
                v = tile(c, "att" + n, [P, D])
                stage = dict(proj=([a["L3_gnn_Wl" + n], a["L3_gnn_Wr" + n]], [None, None], ["xl", "q"], None),
                             pieces=[(v, a["L3_gnn_att" + n].rearrange("h k -> (h k)"))])
                if n == "1":
                    node_stage(nc, pl, sems, merge=parts, after="stream", norm_input=True, **stage)
                else:
                    node_stage(nc, pl, sems, merge=parts, after="norm", vectors=post("1"), **stage)
                parts = sweep("gatv2", 8, pl.xl_tab, pl.q_tab, 1.0, {"att": v})
        node_stage(nc, pl, sems, merge=parts, after="norm_stream", vectors=post("2"), out=out)


def kernel(**inputs):
    import numpy as _np
    import concourse.bacc as _bacc
    from concourse import mybir as _mybir
    from concourse.bass_utils import run_bass_kernel_spmd as _run

    nc = _bacc.Bacc("TRN2", target_bir_lowering=False, num_devices=1)
    arrays, args = {}, {}
    for name, value in inputs.items():
        a = _np.ascontiguousarray(value)
        arrays["in_" + name] = a
        args[name] = nc.dram_tensor("in_" + name, a.shape, _mybir.dt.from_np(a.dtype), kind="ExternalInput").ap()
    out = nc.dram_tensor("out", arrays["in_x"].shape, F32, kind="ExternalOutput").ap()
    gnn_kernel(nc, args, out)
    return _run(nc, [arrays], core_ids=[0]).results[0]["out"]
```
